# Optimizing a Trainium2 kernel written in Bass

```python
import numpy as np
import jax
import jax.numpy as jnp

def _softmax(x, axis=-1):
    return jax.nn.softmax(x, axis=axis)

def _gelu(x):
    return jax.nn.gelu(x, approximate=True)

def _silu(x):
    return jax.nn.silu(x)

def _sigmoid(x):
    return jax.nn.sigmoid(x)

def _layernorm(x, axis=-1, eps=1e-05):
    m = jnp.mean(x, axis=axis, keepdims=True)
    v = jnp.var(x, axis=axis, keepdims=True)
    return (x - m) / jnp.sqrt(v + eps)

def _scatter_add(tgt, idx, src, axis=0):
    return tgt.at[idx].add(src)

def _segment_sum(src, seg, n):
    return jax.ops.segment_sum(src, seg, n)
kernel_name = 'mk_gnn_preln_d4_gnn_r8_acdee5'

def setup_inputs(seed: int=0):
    np.random.seed(seed)
    _w = jnp.asarray

    def _rec_inputs():
        import jax
        import jax.numpy as jnp
        _gk = jax.random.key(seed)
        x = -1.686e-05 + 1 * jax.random.normal(jax.random.fold_in(_gk, 1), (6250, 160), jnp.float32)
        src = jax.random.randint(jax.random.fold_in(_gk, 2), (100000,), 0, 6250, jnp.int32)
        dst = jax.random.randint(jax.random.fold_in(_gk, 3), (100000,), 0, 6250, jnp.int32)
        _o = jnp.argsort(dst, stable=True)
        src = src[_o]
        dst = dst[_o]
        edge_attr_10 = jax.random.uniform(jax.random.fold_in(_gk, 12), (100000, 10), jnp.float32, 0.0, 1)
        edge_attr_12 = jax.random.uniform(jax.random.fold_in(_gk, 13), (100000, 12), jnp.float32, 0.0, 1)
        edge_attr_3 = 0.00047201 + 1.00023 * jax.random.normal(jax.random.fold_in(_gk, 14), (100000, 3), jnp.float32)
        edge_attr_4 = 0.000486536 + 0.999406 * jax.random.normal(jax.random.fold_in(_gk, 15), (100000, 4), jnp.float32)
        edge_attr_64 = 0.000279952 + 1.00013 * jax.random.normal(jax.random.fold_in(_gk, 16), (100000, 64), jnp.float32)
        edge_attr_8 = 0.000398945 + 1.00003 * jax.random.normal(jax.random.fold_in(_gk, 17), (100000, 8), jnp.float32)
        node_vec1 = jax.random.uniform(jax.random.fold_in(_gk, 19), (6250, 1), jnp.float32, 0.0, 0.999994)
        node_vec1_n2 = jax.random.uniform(jax.random.fold_in(_gk, 20), (6250, 1), jnp.float32, 0.0, 0.999994)
        node_vec1_n3 = jax.random.uniform(jax.random.fold_in(_gk, 21), (6250, 1), jnp.float32, 0.0, 0.999994)
        return (x, src, dst, edge_attr_10, edge_attr_12, edge_attr_3, edge_attr_4, edge_attr_64, edge_attr_8, node_vec1, node_vec1_n2, node_vec1_n3)
    x, src, dst, edge_attr_10, edge_attr_12, edge_attr_3, edge_attr_4, edge_attr_64, edge_attr_8, node_vec1, node_vec1_n2, node_vec1_n3 = _rec_inputs()

    def _L0_gnn_setup():
        import jax, jax.numpy as jnp
        import numpy as np
        N = 6250
        E = 50000
        MUL0 = 64
        MUL1 = 32
        NEF = 12
        RN = 100
        NUM_NEIGHBORS = 8.0
        WNUM = MUL0 + MUL0 + MUL1 + MUL1

        def _split(x):
            return (x[:, :MUL0], x[:, MUL0:].reshape(-1, MUL1, 3))

        def _fctp_scalar_attr(x0, x1, z, Ws, Wv):
            s = x0 @ Ws * z / np.sqrt(Ws.shape[0])
            v = jnp.einsum('nuc,uw->nwc', x1, Wv) * z[:, :, None] / np.sqrt(Wv.shape[0])
            return (s, v)
        key = jax.random.key(seed)
        ks = jax.random.split(key, 16)
        return {'node_input': jax.random.normal(ks[0], (N, MUL0 + 3 * MUL1), jnp.float32), 'node_attr': jax.random.uniform(ks[1], (N, 1), dtype=jnp.float32), 'edge_src': jax.random.randint(ks[2], (E,), 0, N), 'edge_dst': jax.random.randint(ks[3], (E,), 0, N), 'edge_attr': jax.random.normal(ks[4], (E, 4), jnp.float32), 'edge_features': jax.random.uniform(ks[5], (E, NEF), dtype=jnp.float32), 'W_sc0': jax.random.normal(ks[6], (MUL0, MUL0), jnp.float32), 'W_sc1': jax.random.normal(ks[7], (MUL1, MUL1), jnp.float32), 'W_l1_0': jax.random.normal(ks[8], (MUL0, MUL0), jnp.float32), 'W_l1_1': jax.random.normal(ks[9], (MUL1, MUL1), jnp.float32), 'W_fc1': jax.random.normal(ks[10], (NEF, RN), jnp.float32), 'W_fc2': jax.random.normal(ks[11], (RN, WNUM), jnp.float32), 'W_l2_0': jax.random.normal(ks[12], (MUL0 + MUL1, MUL0), jnp.float32), 'W_l2_1': jax.random.normal(ks[13], (MUL0 + MUL1, MUL1), jnp.float32)}
    _L0_gnn_all = _L0_gnn_setup()
    _L0_gnn_in = {k: v for k, v in _L0_gnn_all.items() if k in ('W_sc0', 'W_sc1', 'W_l1_0', 'W_l1_1', 'W_fc1', 'W_fc2', 'W_l2_0', 'W_l2_1')}
    del _L0_gnn_all

    def _L1_gnn_setup():
        import jax, jax.numpy as jnp
        import numpy as np
        N = 3125
        E = 50000
        S = 64
        V = 32
        NB = 10
        H = 100
        WN = 192
        MID = 96
        NUM_NEIGHBORS = 16.0
        C_S = float(np.sin(np.pi / 8.0))
        C_X = float(np.cos(np.pi / 8.0))
        SQRT3 = float(np.sqrt(3.0))

        def fctp_scalar_attr(xs, xv, attr, Ws, Wv):
            s = xs * attr @ Ws
            v = jnp.einsum('nuc,uo->noc', xv * attr[:, :, None], Wv)
            return (s, v)
        key = jax.random.key(seed)
        k = jax.random.split(key, 24)

        def w(i, shape):
            return jax.random.normal(k[i], shape, jnp.float32) / np.sqrt(float(shape[0]))
        return {'node_input': jax.random.normal(k[0], (N, S + 3 * V), jnp.float32), 'node_attr': jax.random.normal(k[1], (N, 1), jnp.float32), 'node_crystal_attr': jax.random.normal(k[2], (N, 1), jnp.float32), 'sym_mask': jax.random.normal(k[3], (N, 1), jnp.float32), 'edge_attr': jax.random.normal(k[4], (E, 4), jnp.float32), 'edge_length_embedded': jax.random.uniform(k[5], (E, NB), dtype=jnp.float32), 'edge_src': jax.random.randint(k[6], (E,), 0, N), 'edge_dst': jax.random.randint(k[7], (E,), 0, N), 'Ws_sc_a': w(8, (S, S)), 'Wv_sc_a': w(9, (V, V)), 'Ws_sc_c': w(10, (S, S)), 'Wv_sc_c': w(11, (V, V)), 'Ws_l1_a': w(12, (S, S)), 'Wv_l1_a': w(13, (V, V)), 'Ws_l1_c': w(14, (S, S)), 'Wv_l1_c': w(15, (V, V)), 'W_fc1': w(16, (NB, H)), 'W_fc2': w(17, (H, WN)), 'Ws_l2_a': w(18, (MID, MID)), 'Wv_l2_a': w(19, (MID, MID)), 'Ws_l2_c': w(20, (MID, MID)), 'Wv_l2_c': w(21, (MID, MID)), 'Ws_l3': w(22, (MID, S)), 'Wv_l3': w(23, (MID, V))}
    _L1_gnn_all = _L1_gnn_setup()
    _L1_gnn_in = {k: v for k, v in _L1_gnn_all.items() if k in ('Ws_sc_a', 'Wv_sc_a', 'Ws_sc_c', 'Wv_sc_c', 'Ws_l1_a', 'Wv_l1_a', 'Ws_l1_c', 'Wv_l1_c', 'W_fc1', 'W_fc2', 'Ws_l2_a', 'Wv_l2_a', 'Ws_l2_c', 'Wv_l2_c', 'Ws_l3', 'Wv_l3')}
    del _L1_gnn_all

    def _L2_gnn_setup():
        import jax, jax.numpy as jnp
        import numpy as np
        N_NODES = 1250
        N_EDGES = 40000
        MUL0, MUL1 = (64, 32)
        EDGE_DIM = 64
        W_NUMEL = 224
        DENOM = 32.0
        SQRT3 = 3.0 ** 0.5
        INV_SQRT3 = 1.0 / SQRT3
        INV_SQRT2 = 2.0 ** (-0.5)

        def _forward(node_feature, edge_attr, edge_feature, W_skip0, W_skip1, W_nl0, W_nl1, W_fc1, W_fc2, W_out_s, W_out_v, edge_index):
            N = node_feature.shape[0]
            E = edge_attr.shape[0]
            s = node_feature[:, :MUL0]
            v = node_feature[:, MUL0:].reshape(N, MUL1, 3)
            skip_s = s @ W_skip0
            skip_v = jnp.einsum('nmi,mk->nki', v, W_skip1)
            s = s @ W_nl0
            v = jnp.einsum('nmi,mk->nki', v, W_nl1)
            rhat = edge_attr / jnp.linalg.norm(edge_attr, axis=-1, keepdims=True)
            sh1 = SQRT3 * rhat
            w = jax.nn.relu(edge_feature @ W_fc1) @ W_fc2
            w0, w1, w2, w3, w4 = jnp.split(w, [64, 128, 160, 192], axis=-1)
            src, dst = (edge_index[0], edge_index[1])
            xs = s[dst]
            xv = v[dst]
            out0a = w0 * xs
            out0b = w3 * (jnp.einsum('emi,ei->em', xv, sh1) * INV_SQRT3)
            out1a = (w1 * xs)[:, :, None] * sh1[:, None, :]
            out1b = w2[:, :, None] * xv
            out1c = w4[:, :, None] * (jnp.cross(xv, sh1[:, None, :]) * INV_SQRT2)
            tp = jnp.concatenate([out0a, out0b, out1a.reshape(E, -1), out1b.reshape(E, -1), out1c.reshape(E, -1)], axis=-1)
            agg = jax.ops.segment_sum(tp, src, num_segments=N) / DENOM
            agg_s = agg[:, :96]
            agg_v = agg[:, 96:].reshape(N, 128, 3)
            out_s = agg_s @ W_out_s + skip_s
            out_v = jnp.einsum('nmi,mk->nki', agg_v, W_out_v) + skip_v
            fs = jax.nn.silu(out_s[:, :MUL0])
            gate = jax.nn.sigmoid(out_s[:, MUL0:MUL0 + 32])
            gv = gate[:, :, None] * out_v
            return jnp.concatenate([fs, gv.reshape(N, -1)], axis=-1)
        key = jax.random.key(seed)
        ks = jax.random.split(key, 12)

        def lin(k, fi, fo):
            return jax.random.normal(k, (fi, fo), jnp.float32) / np.float32(np.sqrt(fi))
        return {'node_feature': jax.random.normal(ks[0], (N_NODES, MUL0 + 3 * MUL1), jnp.float32), 'edge_attr': jax.random.normal(ks[1], (N_EDGES, 3), jnp.float32), 'edge_feature': jax.random.normal(ks[2], (N_EDGES, EDGE_DIM), jnp.float32), 'W_skip0': lin(ks[3], MUL0, 96), 'W_skip1': lin(ks[4], MUL1, 32), 'W_nl0': lin(ks[5], MUL0, MUL0), 'W_nl1': lin(ks[6], MUL1, MUL1), 'W_fc1': lin(ks[7], EDGE_DIM, 64), 'W_fc2': lin(ks[8], 64, W_NUMEL), 'W_out_s': lin(ks[9], 96, 96), 'W_out_v': lin(ks[10], 128, 32), 'edge_index': jax.random.randint(ks[11], (2, N_EDGES), 0, N_NODES)}
    _L2_gnn_all = _L2_gnn_setup()
    _L2_gnn_in = {k: v for k, v in _L2_gnn_all.items() if k in ('W_skip0', 'W_skip1', 'W_nl0', 'W_nl1', 'W_fc1', 'W_fc2', 'W_out_s', 'W_out_v')}
    del _L2_gnn_all

    def _L3_gnn_setup():
        import jax, jax.numpy as jnp
        import numpy as np
        INV3 = 1.0 / np.sqrt(3.0)

        def _fctp(x_s, x_v, attr, w0, w1):
            s = x_s @ w0 * (1.0 / np.sqrt(x_s.shape[-1])) * attr
            v = jnp.einsum('nud,uw->nwd', x_v, w1) * (1.0 / np.sqrt(x_v.shape[-2])) * attr[..., None]
            return (s, v)
        key = jax.random.key(seed)
        ks = jax.random.split(key, 16)
        N, E = (6250, 100000)
        inp = {'node_input': jax.random.normal(ks[0], (N, 160), jnp.float32), 'node_attr': jnp.ones((N, 1), jnp.float32), 'edge_attr': jax.random.normal(ks[1], (E, 4), jnp.float32), 'edge_scalars': jax.random.normal(ks[2], (E, 8), jnp.float32), 'sc_w0': jax.random.normal(ks[3], (64, 64), jnp.float32), 'sc_w1': jax.random.normal(ks[4], (32, 32), jnp.float32), 'lin1_w0': jax.random.normal(ks[5], (64, 64), jnp.float32), 'lin1_w1': jax.random.normal(ks[6], (32, 32), jnp.float32), 'fc_w1': jax.random.normal(ks[7], (8, 64), jnp.float32), 'fc_w2': jax.random.normal(ks[8], (64, 192), jnp.float32), 'lin2_w0': jax.random.normal(ks[9], (96, 64), jnp.float32), 'lin2_w1': jax.random.normal(ks[10], (96, 32), jnp.float32), 'lin3_w': jax.random.normal(ks[11], (96, 1), jnp.float32), 'edge_src': jax.random.randint(ks[12], (E,), 0, N), 'edge_dst': jax.random.randint(ks[13], (E,), 0, N), 'num_neighbors': 16}
        return inp
    _L3_gnn_all = _L3_gnn_setup()
    _L3_gnn_in = {k: v for k, v in _L3_gnn_all.items() if k in ('sc_w0', 'sc_w1', 'lin1_w0', 'lin1_w1', 'fc_w1', 'fc_w2', 'lin2_w0', 'lin2_w1', 'lin3_w')}
    del _L3_gnn_all
    return {'x': x, 'src': src, 'dst': dst, 'edge_attr_10': edge_attr_10, 'edge_attr_12': edge_attr_12, 'edge_attr_3': edge_attr_3, 'edge_attr_4': edge_attr_4, 'edge_attr_64': edge_attr_64, 'edge_attr_8': edge_attr_8, 'node_vec1': node_vec1, 'node_vec1_n2': node_vec1_n2, 'node_vec1_n3': node_vec1_n3, 'L0_gnn_W_sc0': _L0_gnn_in['W_sc0'], 'L0_gnn_W_sc1': _L0_gnn_in['W_sc1'], 'L0_gnn_W_l1_0': _L0_gnn_in['W_l1_0'], 'L0_gnn_W_l1_1': _L0_gnn_in['W_l1_1'], 'L0_gnn_W_fc1': _L0_gnn_in['W_fc1'], 'L0_gnn_W_fc2': _L0_gnn_in['W_fc2'], 'L0_gnn_W_l2_0': _L0_gnn_in['W_l2_0'], 'L0_gnn_W_l2_1': _L0_gnn_in['W_l2_1'], 'L1_gnn_Ws_sc_a': _L1_gnn_in['Ws_sc_a'], 'L1_gnn_Wv_sc_a': _L1_gnn_in['Wv_sc_a'], 'L1_gnn_Ws_sc_c': _L1_gnn_in['Ws_sc_c'], 'L1_gnn_Wv_sc_c': _L1_gnn_in['Wv_sc_c'], 'L1_gnn_Ws_l1_a': _L1_gnn_in['Ws_l1_a'], 'L1_gnn_Wv_l1_a': _L1_gnn_in['Wv_l1_a'], 'L1_gnn_Ws_l1_c': _L1_gnn_in['Ws_l1_c'], 'L1_gnn_Wv_l1_c': _L1_gnn_in['Wv_l1_c'], 'L1_gnn_W_fc1': _L1_gnn_in['W_fc1'], 'L1_gnn_W_fc2': _L1_gnn_in['W_fc2'], 'L1_gnn_Ws_l2_a': _L1_gnn_in['Ws_l2_a'], 'L1_gnn_Wv_l2_a': _L1_gnn_in['Wv_l2_a'], 'L1_gnn_Ws_l2_c': _L1_gnn_in['Ws_l2_c'], 'L1_gnn_Wv_l2_c': _L1_gnn_in['Wv_l2_c'], 'L1_gnn_Ws_l3': _L1_gnn_in['Ws_l3'], 'L1_gnn_Wv_l3': _L1_gnn_in['Wv_l3'], 'L2_gnn_W_skip0': _L2_gnn_in['W_skip0'], 'L2_gnn_W_skip1': _L2_gnn_in['W_skip1'], 'L2_gnn_W_nl0': _L2_gnn_in['W_nl0'], 'L2_gnn_W_nl1': _L2_gnn_in['W_nl1'], 'L2_gnn_W_fc1': _L2_gnn_in['W_fc1'], 'L2_gnn_W_fc2': _L2_gnn_in['W_fc2'], 'L2_gnn_W_out_s': _L2_gnn_in['W_out_s'], 'L2_gnn_W_out_v': _L2_gnn_in['W_out_v'], 'L3_gnn_sc_w0': _L3_gnn_in['sc_w0'], 'L3_gnn_sc_w1': _L3_gnn_in['sc_w1'], 'L3_gnn_lin1_w0': _L3_gnn_in['lin1_w0'], 'L3_gnn_lin1_w1': _L3_gnn_in['lin1_w1'], 'L3_gnn_fc_w1': _L3_gnn_in['fc_w1'], 'L3_gnn_fc_w2': _L3_gnn_in['fc_w2'], 'L3_gnn_lin2_w0': _L3_gnn_in['lin2_w0'], 'L3_gnn_lin2_w1': _L3_gnn_in['lin2_w1'], 'L3_gnn_lin3_w': _L3_gnn_in['lin3_w']}

def reference(x, src, dst, edge_attr_10, edge_attr_12, edge_attr_3, edge_attr_4, edge_attr_64, edge_attr_8, node_vec1, node_vec1_n2, node_vec1_n3, L0_gnn_W_sc0, L0_gnn_W_sc1, L0_gnn_W_l1_0, L0_gnn_W_l1_1, L0_gnn_W_fc1, L0_gnn_W_fc2, L0_gnn_W_l2_0, L0_gnn_W_l2_1, L1_gnn_Ws_sc_a, L1_gnn_Wv_sc_a, L1_gnn_Ws_sc_c, L1_gnn_Wv_sc_c, L1_gnn_Ws_l1_a, L1_gnn_Wv_l1_a, L1_gnn_Ws_l1_c, L1_gnn_Wv_l1_c, L1_gnn_W_fc1, L1_gnn_W_fc2, L1_gnn_Ws_l2_a, L1_gnn_Wv_l2_a, L1_gnn_Ws_l2_c, L1_gnn_Wv_l2_c, L1_gnn_Ws_l3, L1_gnn_Wv_l3, L2_gnn_W_skip0, L2_gnn_W_skip1, L2_gnn_W_nl0, L2_gnn_W_nl1, L2_gnn_W_fc1, L2_gnn_W_fc2, L2_gnn_W_out_s, L2_gnn_W_out_v, L3_gnn_sc_w0, L3_gnn_sc_w1, L3_gnn_lin1_w0, L3_gnn_lin1_w1, L3_gnn_fc_w1, L3_gnn_fc_w2, L3_gnn_lin2_w0, L3_gnn_lin2_w1, L3_gnn_lin3_w):
    import jax
    import jax.numpy as jnp

    def _L0_gnn_ref(node_input, node_attr, edge_src, edge_dst, edge_attr, edge_features, W_sc0, W_sc1, W_l1_0, W_l1_1, W_fc1, W_fc2, W_l2_0, W_l2_1):
        import jax, jax.numpy as jnp
        import numpy as np
        N = 6250
        E = 50000
        MUL0 = 64
        MUL1 = 32
        NEF = 12
        RN = 100
        NUM_NEIGHBORS = 8.0
        WNUM = MUL0 + MUL0 + MUL1 + MUL1

        def _split(x):
            return (x[:, :MUL0], x[:, MUL0:].reshape(-1, MUL1, 3))

        def _fctp_scalar_attr(x0, x1, z, Ws, Wv):
            s = x0 @ Ws * z / np.sqrt(Ws.shape[0])
            v = jnp.einsum('nuc,uw->nwc', x1, Wv) * z[:, :, None] / np.sqrt(Wv.shape[0])
            return (s, v)
        x0, x1 = _split(node_input)
        z = node_attr
        s0, s1 = _fctp_scalar_attr(x0, x1, z, W_sc0, W_sc1)
        h0, h1 = _fctp_scalar_attr(x0, x1, z, W_l1_0, W_l1_1)
        h = jax.nn.silu(edge_features @ W_fc1 / np.sqrt(NEF))
        w = h @ W_fc2 / np.sqrt(RN)
        w0 = w[:, :MUL0]
        w1 = w[:, MUL0:2 * MUL0]
        w2 = w[:, 2 * MUL0:2 * MUL0 + MUL1]
        w3 = w[:, 2 * MUL0 + MUL1:]
        e0 = h0[edge_src]
        e1 = h1[edge_src]
        y0 = edge_attr[:, :1]
        y1 = edge_attr[:, 1:]
        m0a = w0 * e0 * y0
        m0b = w3 * jnp.einsum('eui,ei->eu', e1, y1) / np.sqrt(3.0)
        m1a = (w1 * e0)[:, :, None] * y1[:, None, :]
        m1b = w2[:, :, None] * (e1 * y0[:, :, None])
        mid_s = jnp.concatenate([m0a, m0b], axis=1)
        mid_v = jnp.concatenate([m1a, m1b], axis=1)
        inv = 1.0 / np.sqrt(NUM_NEIGHBORS)
        ns = jax.ops.segment_sum(mid_s, edge_dst, num_segments=N) * inv
        nv = jax.ops.segment_sum(mid_v, edge_dst, num_segments=N) * inv
        o0, o1 = _fctp_scalar_attr(ns, nv, z, W_l2_0, W_l2_1)
        c_s, c_x = (np.sin(np.pi / 8), np.cos(np.pi / 8))
        out0 = c_s * s0 + c_x * o0
        out1 = c_s * s1 + c_x * o1
        return jnp.concatenate([out0, out1.reshape(N, -1)], axis=1)

    def _L1_gnn_ref(node_input, node_attr, node_crystal_attr, sym_mask, edge_attr, edge_length_embedded, edge_src, edge_dst, Ws_sc_a, Wv_sc_a, Ws_sc_c, Wv_sc_c, Ws_l1_a, Wv_l1_a, Ws_l1_c, Wv_l1_c, W_fc1, W_fc2, Ws_l2_a, Wv_l2_a, Ws_l2_c, Wv_l2_c, Ws_l3, Wv_l3):
        import jax, jax.numpy as jnp
        import numpy as np
        N = 3125
        E = 50000
        S = 64
        V = 32
        NB = 10
        H = 100
        WN = 192
        MID = 96
        NUM_NEIGHBORS = 16.0
        C_S = float(np.sin(np.pi / 8.0))
        C_X = float(np.cos(np.pi / 8.0))
        SQRT3 = float(np.sqrt(3.0))

        def fctp_scalar_attr(xs, xv, attr, Ws, Wv):
            s = xs * attr @ Ws
            v = jnp.einsum('nuc,uo->noc', xv * attr[:, :, None], Wv)
            return (s, v)
        n = node_input.shape[0]
        xs = node_input[:, :S]
        xv = node_input[:, S:].reshape(n, V, 3)
        ssa, sva = fctp_scalar_attr(xs, xv, node_attr, Ws_sc_a, Wv_sc_a)
        ssc, svc = fctp_scalar_attr(xs, xv, node_crystal_attr, Ws_sc_c, Wv_sc_c)
        s_s, s_v = (ssa + ssc, sva + svc)
        l1a_s, l1a_v = fctp_scalar_attr(xs, xv, node_attr, Ws_l1_a, Wv_l1_a)
        l1c_s, l1c_v = fctp_scalar_attr(xs, xv, node_crystal_attr, Ws_l1_c, Wv_l1_c)
        x1s, x1v = (l1a_s + l1c_s, l1a_v + l1c_v)
        weight = jax.nn.silu(edge_length_embedded @ W_fc1) @ W_fc2
        w0 = weight[:, :S]
        w1 = weight[:, S:2 * S]
        w2 = weight[:, 2 * S:2 * S + V]
        w3 = weight[:, 2 * S + V:]
        gs = x1s[edge_src]
        gv = x1v[edge_src]
        e_s = edge_attr[:, :1]
        e_v = edge_attr[:, 1:]
        mid0a = w0 * gs * e_s
        mid0b = w3 * (jnp.einsum('euc,ec->eu', gv, e_v) / SQRT3)
        mid1a = w1[:, :, None] * gs[:, :, None] * e_v[:, None, :]
        mid1b = w2[:, :, None] * gv * e_s[:, :, None]
        edge_feat = jnp.concatenate([mid0a, mid0b, mid1a.reshape(-1, 3 * S), mid1b.reshape(-1, 3 * V)], axis=-1)
        agg = jax.ops.segment_sum(edge_feat, edge_dst, num_segments=n) / np.sqrt(NUM_NEIGHBORS)
        m_s = agg[:, :MID]
        m_v = agg[:, MID:].reshape(n, MID, 3)
        l2a_s, l2a_v = fctp_scalar_attr(m_s, m_v, node_attr, Ws_l2_a, Wv_l2_a)
        l2c_s, l2c_v = fctp_scalar_attr(m_s, m_v, node_crystal_attr, Ws_l2_c, Wv_l2_c)
        m_s, m_v = (l2a_s + l2c_s, l2a_v + l2c_v)
        o_s, o_v = fctp_scalar_attr(m_s, m_v, sym_mask, Ws_l3, Wv_l3)
        out_s = C_S * s_s + C_X * o_s
        out_v = C_S * s_v + C_X * o_v
        return jnp.concatenate([out_s, out_v.reshape(n, 3 * V)], axis=-1)

    def _L2_gnn_ref(node_feature, edge_attr, edge_feature, W_skip0, W_skip1, W_nl0, W_nl1, W_fc1, W_fc2, W_out_s, W_out_v, edge_index):
        import jax, jax.numpy as jnp
        import numpy as np
        N_NODES = 1250
        N_EDGES = 40000
        MUL0, MUL1 = (64, 32)
        EDGE_DIM = 64
        W_NUMEL = 224
        DENOM = 32.0
        SQRT3 = 3.0 ** 0.5
        INV_SQRT3 = 1.0 / SQRT3
        INV_SQRT2 = 2.0 ** (-0.5)

        def _forward(node_feature, edge_attr, edge_feature, W_skip0, W_skip1, W_nl0, W_nl1, W_fc1, W_fc2, W_out_s, W_out_v, edge_index):
            N = node_feature.shape[0]
            E = edge_attr.shape[0]
            s = node_feature[:, :MUL0]
            v = node_feature[:, MUL0:].reshape(N, MUL1, 3)
            skip_s = s @ W_skip0
            skip_v = jnp.einsum('nmi,mk->nki', v, W_skip1)
            s = s @ W_nl0
            v = jnp.einsum('nmi,mk->nki', v, W_nl1)
            rhat = edge_attr / jnp.linalg.norm(edge_attr, axis=-1, keepdims=True)
            sh1 = SQRT3 * rhat
            w = jax.nn.relu(edge_feature @ W_fc1) @ W_fc2
            w0, w1, w2, w3, w4 = jnp.split(w, [64, 128, 160, 192], axis=-1)
            src, dst = (edge_index[0], edge_index[1])
            xs = s[dst]
            xv = v[dst]
            out0a = w0 * xs
            out0b = w3 * (jnp.einsum('emi,ei->em', xv, sh1) * INV_SQRT3)
            out1a = (w1 * xs)[:, :, None] * sh1[:, None, :]
            out1b = w2[:, :, None] * xv
            out1c = w4[:, :, None] * (jnp.cross(xv, sh1[:, None, :]) * INV_SQRT2)
            tp = jnp.concatenate([out0a, out0b, out1a.reshape(E, -1), out1b.reshape(E, -1), out1c.reshape(E, -1)], axis=-1)
            agg = jax.ops.segment_sum(tp, src, num_segments=N) / DENOM
            agg_s = agg[:, :96]
            agg_v = agg[:, 96:].reshape(N, 128, 3)
            out_s = agg_s @ W_out_s + skip_s
            out_v = jnp.einsum('nmi,mk->nki', agg_v, W_out_v) + skip_v
            fs = jax.nn.silu(out_s[:, :MUL0])
            gate = jax.nn.sigmoid(out_s[:, MUL0:MUL0 + 32])
            gv = gate[:, :, None] * out_v
            return jnp.concatenate([fs, gv.reshape(N, -1)], axis=-1)
        return _forward(node_feature, edge_attr, edge_feature, W_skip0, W_skip1, W_nl0, W_nl1, W_fc1, W_fc2, W_out_s, W_out_v, edge_index)

    def _L3_gnn_ref(node_input, node_attr, edge_attr, edge_scalars, sc_w0, sc_w1, lin1_w0, lin1_w1, fc_w1, fc_w2, lin2_w0, lin2_w1, lin3_w, edge_src, edge_dst, num_neighbors):
        import jax, jax.numpy as jnp
        import numpy as np
        INV3 = 1.0 / np.sqrt(3.0)

        def _fctp(x_s, x_v, attr, w0, w1):
            s = x_s @ w0 * (1.0 / np.sqrt(x_s.shape[-1])) * attr
            v = jnp.einsum('nud,uw->nwd', x_v, w1) * (1.0 / np.sqrt(x_v.shape[-2])) * attr[..., None]
            return (s, v)
        N = node_input.shape[0]
        h = jax.nn.silu(edge_scalars @ fc_w1 * (1.0 / np.sqrt(8.0)))
        weight = h @ fc_w2 * (1.0 / np.sqrt(64.0))
        xs, xv = (node_input[:, :64], node_input[:, 64:].reshape(N, 32, 3))
        sc_s, sc_v = _fctp(xs, xv, node_attr, sc_w0, sc_w1)
        f_s, f_v = _fctp(xs, xv, node_attr, lin1_w0, lin1_w1)
        gs = f_s[edge_src]
        gv = f_v[edge_src]
        ys, yv = (edge_attr[:, :1], edge_attr[:, 1:])
        w1_, w2_ = (weight[:, :64], weight[:, 64:128])
        w3_, w4_ = (weight[:, 128:160], weight[:, 160:192])
        m0a = gs * ys * w1_
        m0b = jnp.sum(gv * yv[:, None, :], -1) * INV3 * w4_
        m1a = gs[..., None] * yv[:, None, :] * w2_[..., None]
        m1b = gv * ys[..., None] * w3_[..., None]
        E = m0a.shape[0]
        edge_feat = jnp.concatenate([m0a, m0b, m1a.reshape(E, 192), m1b.reshape(E, 96)], -1)
        mid = jax.ops.segment_sum(edge_feat, edge_dst, num_segments=N)
        mid = mid / np.sqrt(float(num_neighbors))
        mid_s, mid_v = (mid[:, :96], mid[:, 96:].reshape(N, 96, 3))
        c_s, c_v = _fctp(mid_s, mid_v, node_attr, lin2_w0, lin2_w1)
        conv = jnp.concatenate([c_s, c_v.reshape(N, -1)], -1)
        scfeat = jnp.concatenate([sc_s, sc_v.reshape(N, -1)], -1)
        angle = 0.1 * (mid_s @ lin3_w) * (1.0 / np.sqrt(96.0)) * node_attr
        return jnp.cos(angle) * scfeat + jnp.sin(angle) * conv
    edge_index = jnp.stack([src, dst])
    h = jnp.maximum(_layernorm(x, axis=-1), 0.0)
    x = x + _L0_gnn_ref(h, node_vec1, src, dst, edge_attr_4, edge_attr_12, L0_gnn_W_sc0, L0_gnn_W_sc1, L0_gnn_W_l1_0, L0_gnn_W_l1_1, L0_gnn_W_fc1, L0_gnn_W_fc2, L0_gnn_W_l2_0, L0_gnn_W_l2_1)
    h = jnp.maximum(_layernorm(x, axis=-1), 0.0)
    x = x + _L1_gnn_ref(h, node_vec1, node_vec1_n2, node_vec1_n3, edge_attr_4, edge_attr_10, src, dst, L1_gnn_Ws_sc_a, L1_gnn_Wv_sc_a, L1_gnn_Ws_sc_c, L1_gnn_Wv_sc_c, L1_gnn_Ws_l1_a, L1_gnn_Wv_l1_a, L1_gnn_Ws_l1_c, L1_gnn_Wv_l1_c, L1_gnn_W_fc1, L1_gnn_W_fc2, L1_gnn_Ws_l2_a, L1_gnn_Wv_l2_a, L1_gnn_Ws_l2_c, L1_gnn_Wv_l2_c, L1_gnn_Ws_l3, L1_gnn_Wv_l3)
    h = jnp.maximum(_layernorm(x, axis=-1), 0.0)
    x = x + _L2_gnn_ref(h, edge_attr_3, edge_attr_64, L2_gnn_W_skip0, L2_gnn_W_skip1, L2_gnn_W_nl0, L2_gnn_W_nl1, L2_gnn_W_fc1, L2_gnn_W_fc2, L2_gnn_W_out_s, L2_gnn_W_out_v, edge_index)
    h = jnp.maximum(_layernorm(x, axis=-1), 0.0)
    x = x + _L3_gnn_ref(h, node_vec1, edge_attr_4, edge_attr_8, L3_gnn_sc_w0, L3_gnn_sc_w1, L3_gnn_lin1_w0, L3_gnn_lin1_w1, L3_gnn_fc_w1, L3_gnn_fc_w2, L3_gnn_lin2_w0, L3_gnn_lin2_w1, L3_gnn_lin3_w, src, dst, 16)
    return x

_drawn_inputs = setup_inputs


def setup_inputs(seed=0):
    import zlib

    import numpy as np

    out = dict(_drawn_inputs(seed))
    spreads = {}
    factors = {}
    for name, (base, spread) in spreads.items():
        noise = np.random.default_rng([zlib.crc32(name.encode()), seed]).standard_normal(out[name].shape)
        drawn = base * np.exp(spread * noise) if base else spread * noise
        out[name] = jnp.asarray(drawn.astype(out[name].dtype))
    for name, factor in factors.items():
        out[name] = (out[name] * factor).astype(out[name].dtype)
    return out
```

```python
from contextlib import ExitStack

import numpy as np

import concourse.bass as bass
from concourse import mybir

F32 = mybir.dt.float32
I32 = mybir.dt.int32
BF16 = mybir.dt.bfloat16
U16 = mybir.dt.uint16
ALU = mybir.AluOpType
ACT = mybir.ActivationFunctionType

N = 6250
E = 100000
D = 160
BN = 123
NB = 51
NPAD = BN * NB
LAST = N - (NB - 1) * BN
EC = 782
EPAD = 128 * EC
NOKEY = 6399
G = 4
GE = 128 * G
NG = 252
ROWS = NG * GE
RA, RB = 36, 72
CH = 17
NCH = EC // CH
MAGIC = 12582912.0
ZW = 2016
C_S, C_X = float(np.sin(np.pi / 8)), float(np.cos(np.pi / 8))
R3 = float(np.sqrt(3.0))

LAYERS = [
    dict(t="A", kf=12, c0=0, hid=100, wn=192, vb=96, scale=float(1 / np.sqrt(12.0)), fn=ACT.Silu),
    dict(t="A", kf=10, c0=12, hid=100, wn=192, vb=96, scale=1.0, fn=ACT.Silu),
    dict(t="B", kf=64, c0=0, hid=64, wn=224, vb=128, scale=1.0, fn=ACT.Relu),
    dict(t="A", kf=8, c0=22, hid=64, wn=192, vb=96, scale=float(1 / np.sqrt(8.0)), fn=ACT.Silu),
]
YC, SRCC, LOCC = 30, 34, 35
SHC, DSTC, LOCB = 64, 69, 70

_INS = [
    "x", "keya", "keyb", "ea", "eb", "z1", "z2", "z3",
    "L0_gnn_W_sc0", "L0_gnn_W_sc1", "L0_gnn_W_l1_0", "L0_gnn_W_l1_1", "L0_gnn_W_fc1", "L0_gnn_W_fc2",
    "L0_gnn_W_l2_0", "L0_gnn_W_l2_1", "L1_gnn_Ws_sc_a", "L1_gnn_Wv_sc_a", "L1_gnn_Ws_sc_c", "L1_gnn_Wv_sc_c",
    "L1_gnn_Ws_l1_a", "L1_gnn_Wv_l1_a", "L1_gnn_Ws_l1_c", "L1_gnn_Wv_l1_c", "L1_gnn_W_fc1", "L1_gnn_W_fc2",
    "L1_gnn_Ws_l2_a", "L1_gnn_Wv_l2_a", "L1_gnn_Ws_l2_c", "L1_gnn_Wv_l2_c", "L1_gnn_Ws_l3", "L1_gnn_Wv_l3",
    "L2_gnn_W_skip0", "L2_gnn_W_skip1", "L2_gnn_W_nl0", "L2_gnn_W_nl1", "L2_gnn_W_fc1", "L2_gnn_W_fc2",
    "L2_gnn_W_out_s", "L2_gnn_W_out_v", "L3_gnn_sc_w0", "L3_gnn_sc_w1", "L3_gnn_lin1_w0", "L3_gnn_lin1_w1",
    "L3_gnn_fc_w1", "L3_gnn_fc_w2", "L3_gnn_lin2_w0", "L3_gnn_lin2_w1", "L3_gnn_lin3_w",
]


def program(nc, A, out):
    ctx = ExitStack()
    with ctx:
        def sb(name, shape, dt=F32):
            return ctx.enter_context(nc.sbuf_tensor(name, shape, dt))

        def sem(name):
            return ctx.enter_context(nc.semaphore(name))

        TA = nc.dram_tensor("TA", (ROWS + EC, RA), F32).ap()
        TB = nc.dram_tensor("TB", (ROWS + EC, RB), F32).ap()
        HT = nc.dram_tensor("HT", (NPAD, D), F32).ap()
        SC = nc.dram_tensor("SC", (NPAD, 192), F32).ap()

        X = sb("X", [BN, NB, D])
        ACC = sb("ACC", [128, NB * 480])
        WK = sb("WK", [128, 13136])
        NP = WK[:, 9486:13136]
        PS = ctx.enter_context(nc.psum_tensor("PS", [128, 4096], F32))

        ident = sb("ident", [128, 128])
        iota1 = sb("iota1", [128, BN])
        Z1, Z2, Z3 = (sb(f"Z{i}", [BN, NB]) for i in (1, 2, 3))
        SA, SCC = sb("SA", [BN, NB]), sb("SCC", [BN, NB])
        STT = sb("STT", [BN, NB, 6])
        MV = sb("MV", [BN, NB, 2])
        VE, RS, NM = sb("VE", [BN, NB]), sb("RS", [BN, NB]), sb("NM", [BN, NB])
        ANG, KK, SN, CS = sb("ANG", [BN, NB]), sb("KK", [BN, NB]), sb("SN", [BN, NB]), sb("CS", [BN, NB])
        CNT = sb("CNT", [128, NB])
        INC, GRP, OFF = sb("INC", [128, NB]), sb("GRP", [128, NB]), sb("OFF", [128, NB])
        BKF = sb("BKF", [1, 256])
        GI = sb("GI", [1, 256])
        BK = [sb("BKA", [1, 256], I32), sb("BKB", [1, 256], I32)]
        NIF = sb("NIF", [1, 1])
        NI = [sb("NIA", [1, 1], I32), sb("NIB", [1, 1], I32)]

        WS = [sb("WS0", [64, 128]), sb("WS1", [64, 2, 128]), sb("WS2", [64, 160]), sb("WS3", [64, 128])]
        KV = [sb("KV0", [96, 192]), sb("KV1", [96, 2, 192]), sb("KV2", [96, 192]), sb("KV3", [96, 192])]
        F1 = [sb(f"F1_{l}", [p["kf"], p["hid"]]) for l, p in enumerate(LAYERS)]
        F2 = [sb(f"F2_{l}", [p["hid"], p["wn"]]) for l, p in enumerate(LAYERS)]
        OS = [sb("OS0", [96, 64]), sb("OS1", [96, 2, 64]), sb("OS2", [96, 96]), sb("OS3", [96, 64])]
        OV = [sb("OV0", [96, 32]), sb("OV1", [96, 2, 32]), sb("OV2", [128, 32]), sb("OV3", [96, 32])]
        L3W = sb("L3W", [BN, 96])
        RSC = sb("RSC", [128, 2])

        def wk(a, n, p=128):
            return WK[0:p, a:a + n]

        keyA, keyB = wk(0, EC).bitcast(I32), wk(EC, EC).bitcast(I32)
        locA, locB = wk(2 * EC, EC), wk(3 * EC, EC)
        posA, posB = wk(4 * EC, EC).bitcast(I32), wk(5 * EC, EC).bitcast(I32)
        sh = wk(6 * EC, 3 * EC).rearrange("p (c k) -> p c k", k=3)
        stage = [wk(9 * EC + i * CH * RB, CH * RB) for i in range(2)]
        zero = wk(9 * EC, ZW)
        masks = ACC[:, 0:NB * 391].bitcast(BF16).rearrange("p (b c) -> p b c", c=EC)
        tb0 = NB * 391
        kf, bq, cum, pos = (ACC[:, tb0 + i * EC:tb0 + (i + 1) * EC] for i in range(4))
        bb = ACC[:, tb0 + 4 * EC:tb0 + 4 * EC + 391].bitcast(BF16)
        z16 = ACC[:, tb0 + 4 * EC + 391:tb0 + 4 * EC + 782].bitcast(BF16)
        cmp_ = ACC[0:1, tb0:tb0 + 64 * NB].rearrange("p (t b) -> p t b", b=NB)
        LT, ONE = NP[:, 0:128], NP[:, 128:256]

        at = 0

        def take(n, p=128):
            nonlocal at
            v = WK[0:p, at:at + n]
            at += n
            return v

        TT = [take(G * RB) for _ in range(4)]
        GB = [take(G * D).rearrange("p (t f) -> p t f", t=G) for _ in range(2)]
        ET = [take(GE) for _ in range(2)]
        HH = [take(GE) for _ in range(2)]
        OH = [take(G * BN).rearrange("p (t f) -> p t f", t=G) for _ in range(2)]
        MS = [take(G * 480) for _ in range(2)]
        tq = [take(G * 32).rearrange("p (t f) -> p t f", t=G) for _ in range(2)]
        tu = [take(G * 32).rearrange("p (t f) -> p t f", t=G) for _ in range(2)]
        ty = [take(G * 64).rearrange("p (t f) -> p t f", t=G) for _ in range(1)] * 2
        tt_ = [take(G * 64).rearrange("p (t f) -> p t f", t=G) for _ in range(1)] * 2
        tp = [take(G * 96).rearrange("p (t c f) -> p t c f", t=G, c=3) for _ in range(1)] * 2
        tw = take(G * 160).rearrange("p (t c f) -> p t c f", t=G, c=5)
        tx = take(G * 96).rearrange("p (t c f) -> p t c f", t=G, c=3)
        assert at <= 13136, at

        h = [NP[0:BN, i * 160:(i + 1) * 160] for i in range(4)]
        hT = [NP[0:96, 640 + i * 256:896 + i * 256].rearrange("p (a n) -> p a n", a=2) for i in range(2)]
        EV = [NP[0:BN, 1152 + i * 352:1504 + i * 352] for i in range(2)]
        aT = [NP[:, 1856 + i * 512:2368 + i * 512].rearrange("p (a n) -> p a n", a=4) for i in range(2)]
        SK = [NP[0:BN, 2880 + i * 192:3072 + i * 192] for i in range(2)]
        OO = [NP[0:BN, 3264 + i * 192:3456 + i * 192] for i in range(2)]
        SG = [NP[0:BN, 1856 - 352 * 2 + i * 352:1856 - 352 * 2 + i * 352 + 96] for i in range(2)]
        FP = [NP[0:BN, 1856 - 352 * 2 + i * 352 + 96:1856 - 352 * 2 + i * 352 + 256] for i in range(2)]
        RW = [NP[0:96, 1856 + i * 96:1952 + i * 96] for i in range(4)]
        RWT = [NP[0:96, 2368 + i * 96:2464 + i * 96] for i in range(4)]
        RW3s, RW3v = NP[0:96, 2880:2944], NP[0:96, 2944:2976]

        def bank(i, n=512, p=128):
            return PS[0:p, i * 512:i * 512 + n]

        psW = [PS[:, i * 1024:(i + 1) * 1024].rearrange("p (t f) -> p t f", t=G) for i in range(2)]
        psH, psT = bank(4), bank(5)
        psA = [bank(6), bank(7)]
        psN = [bank(0), bank(1)]
        psO = [bank(2), bank(3)]
        psC = [bank(4), bank(5)]

        s_key, s_x, s_ld, s_w, s_ws, s_sh = (sem(n) for n in ("s_key", "s_x", "s_ld", "s_w", "s_ws", "s_sh"))
        s_g, s_gm, s_gp = sem("s_g"), sem("s_gm"), sem("s_gp")
        s_d, s_a, s_p = sem("s_d"), sem("s_a"), sem("s_p")
        s_zf = sem("s_zf")
        s_cn, s_cp, s_pos, s_bk = sem("s_cn"), sem("s_cp"), sem("s_pos"), sem("s_bk")
        s_sq, s_sqd, s_shd = sem("s_sq"), sem("s_sqd"), sem("s_shd")
        s_stg, s_prep = [sem("s_stg0"), sem("s_stg1")], sem("s_prep")
        s_sct = [sem("s_sct0"), sem("s_sct1")]
        s_ve, s_sd, s_st = sem("s_ve"), sem("s_sd"), sem("s_st")
        s_h, s_tp, s_ht, s_po, s_ev, s_xn = (sem(n) for n in ("s_h", "s_tp", "s_ht", "s_po", "s_ev", "s_xn"))
        s_hd = [[sem(f"s_hd{l}{i}") for i in range(2)] for l in range(4)]
        s_at, s_ac, s_oo, s_xo = (sem(n) for n in ("s_at", "s_ac", "s_oo", "s_xo"))
        s_sk = [[sem(f"s_sk{l}{i}") for i in range(2)] for l in (2, 3)]
        s_o, s_sg = sem("s_o"), sem("s_sg")
        s_an, s_sn = sem("s_an"), sem("s_sn")
        s_az, s_le, s_out = sem("s_az"), sem("s_le"), sem("s_out")
        s_go, s_pe, s_sp = sem("s_go"), sem("s_pe"), sem("s_sp")
        s_rt, s_rc, s_rp = sem("s_rt"), sem("s_rc"), sem("s_rp")

        class Edge:
            def __init__(self, l):
                self.L = [sem(f"e{l}_L{i}") for i in range(4)]
                self.G = [sem(f"e{l}_G{i}") for i in range(2)]
                self.T, self.E, self.F1, self.S, self.F2, self.M, self.A, self.V, self.D = (
                    sem(f"e{l}_{n}") for n in ("T", "E", "F1", "S", "F2", "M", "A", "V", "D"))

        EG = [Edge(l) for l in range(4)]

        block = ctx.enter_context(nc.Block())
        NKEYS = 2
        loads = []

        def kron(l, a, col, W, interleaved):
            t = KV[l][:, a, :] if l == 1 else KV[l][:, :]
            for c in range(3):
                if interleaved:
                    loads.append((t[c:96:3, col + c:col + 96:3], W))
                else:
                    loads.append((t[c:96:3, col + 32 * c:col + 32 * c + 32], W))

        w = A
        loads += [(WS[0][:, 0:64], w["L0_gnn_W_l1_0"]), (WS[0][:, 64:128], w["L0_gnn_W_sc0"])]
        kron(0, 0, 0, w["L0_gnn_W_l1_1"], False)
        kron(0, 0, 96, w["L0_gnn_W_sc1"], True)
        for a, s in enumerate("ac"):
            loads += [(WS[1][:, a, 0:64], w[f"L1_gnn_Ws_l1_{s}"]), (WS[1][:, a, 64:128], w[f"L1_gnn_Ws_sc_{s}"])]
            kron(1, a, 0, w[f"L1_gnn_Wv_l1_{s}"], False)
            kron(1, a, 96, w[f"L1_gnn_Wv_sc_{s}"], True)
            loads += [(RW[a], w[f"L1_gnn_Ws_l2_{s}"]), (RW[2 + a], w[f"L1_gnn_Wv_l2_{s}"])]
        loads += [(RW3s, w["L1_gnn_Ws_l3"]), (RW3v, w["L1_gnn_Wv_l3"])]
        loads += [(WS[2][:, 0:64], w["L2_gnn_W_nl0"]), (WS[2][:, 64:160], w["L2_gnn_W_skip0"])]
        kron(2, 0, 0, w["L2_gnn_W_nl1"], False)
        kron(2, 0, 96, w["L2_gnn_W_skip1"], True)
        loads += [(WS[3][:, 0:64], w["L3_gnn_lin1_w0"]), (WS[3][:, 64:128], w["L3_gnn_sc_w0"])]
        kron(3, 0, 0, w["L3_gnn_lin1_w1"], False)
        kron(3, 0, 96, w["L3_gnn_sc_w1"], True)
        for l, n in enumerate(("L0_gnn_W_fc", "L1_gnn_W_fc", "L2_gnn_W_fc", "L3_gnn_fc_w")):
            loads += [(F1[l][:, :], w[n + "1"]), (F2[l][:, :], w[n + "2"])]
        loads += [(OS[0][:, :], w["L0_gnn_W_l2_0"]), (OV[0][:, :], w["L0_gnn_W_l2_1"]),
                  (OS[2][:, :], w["L2_gnn_W_out_s"]), (OV[2][:, :], w["L2_gnn_W_out_v"]),
                  (OS[3][:, :], w["L3_gnn_lin2_w0"]), (OV[3][:, :], w["L3_gnn_lin2_w1"]),
                  (L3W[:, :], w["L3_gnn_lin3_w"].rearrange("k a -> a k").to_broadcast([BN, 96]))]

        def htile(l, j):
            return slice(j * BN, (j + 1) * BN)

        @block.sync
        def _(eng):
            eng.dma_start(keyA, A["keya"].rearrange("(p c) -> p c", p=128)).then_inc(s_key, 16)
            eng.dma_start(keyB, A["keyb"].rearrange("(p c) -> p c", p=128)).then_inc(s_key, 16)
            eng.dma_start(X[:, :, :], A["x"].rearrange("(j p) d -> p j d", p=BN)).then_inc(s_x, 16)
            for t, n in ((Z1, "z1"), (Z2, "z2"), (Z3, "z3")):
                eng.dma_start(t[:, :], A[n]).then_inc(s_x, 16)
            eng.wait_ge(s_gm, 2)
            with nc.allow_non_contiguous_dma(reason="small strided weights"):
                for d, s in loads:
                    eng.dma_start(d, s).then_inc(s_w, 16)
                eng.dma_start(sh, A["eb"].rearrange("(p c) f -> p c f", p=128)[:, :, 64:67]).then_inc(s_sh, 16)
            eng.wait_ge(s_gm, 3)
            for T, R in ((TA, RA), (TB, RB)):
                n = ROWS // 128 * R // ZW
                eng.dma_start(T[0:ROWS, :].rearrange("(p a) f -> p (a f)", p=128).rearrange("p (n z) -> p n z", z=ZW),
                              zero.unsqueeze(1).to_broadcast([128, n, ZW])).then_inc(s_zf, 16)
            eng.wait_ge(s_zf, 32)
            k = 0
            for name, R in (("ea", RA), ("eb", RB)):
                v = A[name].rearrange("(p c) f -> p (c f)", p=128)
                for c in range(NCH):
                    if k >= 2:
                        eng.wait_ge(s_sct[k % 2], 16 * CH * (k // 2))
                    eng.dma_start(stage[k % 2][:, 0:CH * R], v[:, c * CH * R:(c + 1) * CH * R])\
                       .then_inc(s_stg[k % 2], 16)
                    k += 1

            for l, p in enumerate(LAYERS):
                e, b = EG[l], 0 if p["t"] == "A" else 1
                R, T = (RA, TA) if b == 0 else (RB, TB)
                for i in range(2):
                    eng.wait_ge(s_sct[i], 16 * CH * NCH)
                eng.wait_ge(s_xn, NB * (l + 1))
                eng.wait_ge(s_bk, NKEYS)
                n = eng.value_load(NI[b][0:1, 0:1], min_val=49, max_val=NG // 4 - 1)
                with eng.Fori(0, n + 1) as i:
                    for u in range(4):
                        eng.wait_ge(e.M, i * 4 + (u + 1))
                        eng.dma_start(TT[u][:, 0:G * R],
                                      T[bass.ds(i * (4 * GE) + u * GE, GE), :].rearrange("(p t) f -> p (t f)", t=G))\
                           .then_inc(e.L[u], 16)
                for u in range(4):
                    eng.wait_ge(e.L[u], n * 16 + 16)
                eng.sem_inc(s_sp, 1)
                if l >= 2:
                    for j in range(NB):
                        if j >= 2:
                            eng.wait_ge(s_o if l == 2 else s_xo, (j - 1) if l == 2 else NB * 3 + j - 1)
                        else:
                            eng.wait_ge(s_le, l + 1)
                        eng.dma_start(SK[j % 2][:, 0:192 if l == 2 else 160],
                                      SC[htile(l, j), 0:192 if l == 2 else 160]).then_inc(s_sk[l - 2][j % 2], 16)
            for j in range(NB):
                eng.wait_ge(s_xo, NB * 3 + j + 1)
                r = BN if j < NB - 1 else LAST
                eng.dma_start(out[j * BN:j * BN + r, :], X[0:r, j, :]).then_inc(s_out, 16)
            eng.wait_ge(s_out, 16 * NB)

        @block.gpsimd
        def _(eng):
            for l in range(4):
                eng.memset(KV[l][:, :, :] if l == 1 else KV[l][:, :], 0.0).then_inc(s_g, 1)
            eng.memset(RSC[0:64, 0:1], 1.0).then_inc(s_g, 1)
            eng.memset(RSC[0:96, 1:2], 1.0).then_inc(s_g, 1)
            eng.wait_ge(s_g, 6)
            eng.memset(RSC[64:128, 0:1], 1.0 / R3).then_inc(s_g, 1)
            eng.wait_ge(s_g, 7)
            eng.memset(RSC[96:128, 1:2], float(1 / np.sqrt(2.0))).then_inc(s_g, 1)
            eng.wait_ge(s_g, 8)
            eng.memset(ident[:, :], 0.0).then_inc(s_g, 1)
            eng.memset(LT, 1.0).then_inc(s_g, 1)
            eng.wait_ge(s_g, 10)
            eng.affine_select(out=ident[:, :], in_=ident[:, :], compare_op=ALU.not_equal, fill=1.0, base=0,
                              pattern=[[-1, 128]], channel_multiplier=1).then_inc(s_gm, 1)
            eng.affine_select(out=LT, in_=LT, compare_op=ALU.is_gt, fill=0.0, base=0,
                              pattern=[[1, 128]], channel_multiplier=-1).then_inc(s_gm, 1)
            eng.memset(zero, 0.0).then_inc(s_gm, 1)
            eng.memset(ONE, 1.0).then_inc(s_g, 1)
            eng.iota(iota1[:, :], [[1, BN]], base=1, channel_multiplier=0,
                     allow_small_or_imprecise_dtypes=True).then_inc(s_g, 1)
            eng.iota(GI[:, :], [[1, 256]], base=-1, channel_multiplier=0,
                     allow_small_or_imprecise_dtypes=True).then_inc(s_gm, 1)

            k = 0
            prep = 0
            eng.wait_ge(s_zf, 32)
            for b, (T, R, val, loc, ps) in enumerate(((TA, RA, keyB, locA, posA), (TB, RB, keyA, locB, posB))):
                eng.wait_ge(s_pos, b + 1)
                if b == 1:
                    eng.wait_ge(s_shd, 1)
                for c in range(NCH):
                    eng.wait_ge(s_stg[k % 2], 16 * (k // 2 + 1))
                    st = stage[k % 2][:, 0:CH * R].rearrange("p (c f) -> p c f", f=R)
                    sl = slice(c * CH, (c + 1) * CH)
                    vc, lc = (SRCC, LOCC) if b == 0 else (DSTC, LOCB)
                    eng.tensor_copy(st[:, :, vc:vc + 1].bitcast(I32), val[:, sl].unsqueeze(2)).then_inc(s_prep, 1)
                    eng.tensor_copy(st[:, :, lc:lc + 1], loc[:, sl].unsqueeze(2)).then_inc(s_prep, 1)
                    prep += 2
                    if b == 1:
                        eng.tensor_copy(st[:, :, SHC:SHC + 3], sh[:, sl, :]).then_inc(s_prep, 1)
                        eng.tensor_copy(st[:, :, SHC + 3:SHC + 5], sh[:, sl, 0:2]).then_inc(s_prep, 1)
                        prep += 2
                    eng.wait_ge(s_prep, prep)
                    for q in range(CH):
                        eng.indirect_dma_start(
                            out=T[:, :], out_offset=bass.IndirectOffsetOnAxis(ap=ps[:, c * CH + q:c * CH + q + 1], axis=0),
                            in_=st[:, q, :], in_offset=None).then_inc(s_sct[k % 2], 16)
                    k += 1

            for l, p in enumerate(LAYERS):
                e, b = EG[l], 0 if p["t"] == "A" else 1
                R, vc = (RA, SRCC) if b == 0 else (RB, DSTC)
                nacc = NB * (96 + 3 * p["vb"])
                if l == 0:
                    eng.wait_ge(s_bk, NKEYS)
                else:
                    eng.wait_ge(s_at, NB * l)
                eng.memset(ACC[:, 0:nacc], 0.0).then_inc(s_az, 1)
                eng.wait_ge(s_bk, NKEYS)
                n = eng.value_load(NI[b][0:1, 0:1], min_val=49, max_val=NG // 4 - 1)
                m = 32 if l >= 2 else 16
                eng.wait_ge(s_hd[l][0], m * (NB - NB // 2))
                eng.wait_ge(s_hd[l][1], m * (NB // 2))
                with eng.Fori(0, n) as i:
                    for u in range(4):
                        idx = TT[u][:, 0:G * R].rearrange("p (t f) -> p t f", t=G)
                        eng.wait_ge(e.L[u], i * 16 + 16)
                        eng.wait_ge(e.M, i * 4 + (u + 3))
                        eng.sem_inc(s_go, 1)
                        for t in range(G):
                            eng.indirect_dma_start(
                                out=GB[u % 2][:, t, :], out_offset=None, in_=HT[:, :],
                                in_offset=bass.IndirectOffsetOnAxis(ap=idx[:, t, vc:vc + 1].bitcast(I32), axis=0))\
                               .then_inc(e.G[u % 2], 16)

        @block.tensor
        def _(eng):
            eng.wait_ge(s_gm, 2)
            eng.wait_ge(s_g, 11)
            for b in range(NKEYS):
                eng.wait_ge(s_cn, b + 1)
                eng.matmul(psO[0][:, 0:NB], LT, CNT[:, :], start=True, stop=True)
                eng.matmul(psO[1][:, 0:NB], ONE, CNT[:, :], start=True, stop=True).then_inc(s_cp, 1)
            eng.wait_ge(s_w, 16 * len(loads))
            for i in range(4):
                m = eng.transpose(psN[0][0:96, i * 96:(i + 1) * 96], RW[i], ident[0:96, 0:96])
            m.then_inc(s_rt, 1)
            eng.wait_ge(s_rc, 1)
            for a in range(2):
                eng.matmul(psN[1][0:96, a * 96:a * 96 + 64], RWT[a], RW3s, start=True, stop=True)
                m = eng.matmul(psN[1][0:96, a * 96 + 64:a * 96 + 96], RWT[2 + a], RW3v, start=True, stop=True)
            m.then_inc(s_rp, 1)

            for l, p in enumerate(LAYERS):
                kf_, hid, wn, vb = p["kf"], p["hid"], p["wn"], p["vb"]
                nm = 96 + 3 * vb
                base = l * NB
                n2 = 2 if l == 1 else 1

                def tnode(j):
                    eng.wait_ge(s_h, base + j + 1)
                    if base + j >= 2:
                        eng.wait_ge(s_ht, base + j - 1)
                    eng.transpose(psN[j % 2][0:64, 0:BN], h[j % 4][:, 0:64], ident[0:BN, 0:BN])
                    eng.transpose(psN[j % 2][0:96, 128:128 + BN], h[j % 4][:, 64:160], ident[0:BN, 0:BN]).then_inc(s_tp, 1)

                def mnode(j):
                    eng.wait_ge(s_ht, base + j + 1)
                    if base + j >= 2:
                        eng.wait_ge(s_xn, base + j - 1)
                        eng.wait_ge(s_ev, base + j - 1)
                    for a in range(n2):
                        o = (psO, psC)[a][j % 2]
                        ws = WS[l][:, a, :] if l == 1 else WS[l][:, :]
                        kv = KV[l][:, a, :] if l == 1 else KV[l][:, :]
                        ns = 96 if l == 2 else 64
                        hs, hv = hT[j % 2][0:64, 0, 0:BN], hT[j % 2][0:96, 1, 0:BN]
                        eng.matmul(o[0:BN, 0:64], hs, ws[:, 0:64], start=True, stop=True)
                        eng.matmul(o[0:BN, 64:160], hv, kv[:, 0:96], start=True, stop=True)
                        o = psC[j % 2] if l == 0 else o
                        eng.matmul(o[0:BN, 160:160 + ns], hs, ws[:, 64:64 + ns], start=True, stop=True)
                        m = eng.matmul(o[0:BN, 160 + ns:256 + ns], hv, kv[:, 96:192], start=True, stop=True)
                    m.then_inc(s_po, 1)

                if l == 0:
                    eng.wait_ge(s_ws, 1)
                    eng.wait_ge(s_bk, NKEYS)
                tnode(0)
                for j in range(NB):
                    if j + 1 < NB:
                        tnode(j + 1)
                    mnode(j)

                e, b = EG[l], 0 if p["t"] == "A" else 1
                R = RA if b == 0 else RB
                eng.wait_ge(s_xn, base + NB)
                eng.wait_ge(s_ev, base + NB)
                eng.wait_ge(s_bk, NKEYS)
                n = eng.value_load(NI[b][0:1, 0:1], min_val=49, max_val=NG // 4 - 1)

                def edge_t(i, u, d):
                    u2, c = (u + d) % 4, (u + d) // 4
                    ef = TT[u2][:, 0:G * R].rearrange("p (t f) -> p t f", t=G)
                    eng.wait_ge(e.L[u2], i * 16 + (16 * c + 16))
                    if not (isinstance(i, int) and i * 4 + u + d == 0):
                        eng.wait_ge(e.E, i * 4 + (u + d))
                    eng.sem_inc(s_pe, 1)
                    for t in range(G):
                        m = eng.transpose(psT[0:kf_, t * 128:(t + 1) * 128], ef[:, t, p["c0"]:p["c0"] + kf_], ident[:, :])
                    m.then_inc(e.T, 1)

                def edge_f1(i, u, d):
                    q = (u + d) % 2
                    eng.wait_ge(e.E, i * 4 + (u + d + 1))
                    if not (isinstance(i, int) and i * 4 + u + d == 0):
                        eng.wait_ge(e.S, i * 4 + (u + d))
                    eng.sem_inc(s_pe, 1)
                    eng.matmul(psH[0:hid, :], F1[l][:, :], ET[q][0:kf_, :], start=True, stop=True).then_inc(e.F1, 1)

                def edge_f2(i, u, d):
                    q = (u + d) % 2
                    eng.wait_ge(e.S, i * 4 + (u + d + 1))
                    eng.wait_ge(e.M, i * 4 + (u + d + 3))
                    for t in range(G):
                        m = eng.matmul(psW[q][:, t, 0:wn], HH[q][0:hid, t * 128:(t + 1) * 128], F2[l][:, :],
                                       start=True, stop=True)
                    m.then_inc(e.F2, 1)

                def edge_a(i, u):
                    q = u % 2
                    ms = MS[q][:, 0:G * nm].rearrange("p (t f) -> p t f", t=G)
                    eng.wait_ge(e.M, i * 4 + (u + 5))
                    eng.wait_ge(e.V, i * 4 + (u + 1))
                    for t in range(G):
                        m = eng.matmul(psA[q][0:BN, 0:nm], OH[q][:, t, :], ms[:, t, :], start=(t == 0), stop=(t == G - 1))
                    m.then_inc(e.A, 1)

                edge_t(0, 0, 0)
                edge_t(0, 0, 1)
                edge_t(0, 0, 2)
                edge_f1(0, 0, 0)
                edge_f1(0, 0, 1)
                edge_f2(0, 0, 0)
                eng.wait_ge(s_az, l + 1)
                eng.matmul(psA[1][0:BN, 0:nm], ACC[0:1, 0:BN], ACC[0:1, 0:nm], start=True, stop=True).then_inc(e.A, 1)
                with eng.Fori(0, n) as i:
                    for u in range(4):
                        edge_f2(i, u, 1)
                        edge_a(i, u)
                        edge_f1(i, u, 2)
                        edge_t(i, u, 3)
                eng.wait_ge(e.T, n * 4 + 3)
                eng.wait_ge(e.F1, n * 4 + 2)
                eng.wait_ge(e.F2, n * 4 + 1)
                eng.wait_ge(e.E, n * 4 + 3)
                eng.wait_ge(e.S, n * 4 + 2)
                eng.wait_ge(s_le, l + 1)

                acc = ACC[0:BN, 0:NB * nm].rearrange("p (j f) -> p j f", j=NB)

                def tout(j):
                    if base + j >= 2:
                        eng.wait_ge(s_ac, base + j - 1)
                    eng.transpose(psN[j % 2][0:96, 0:BN], acc[:, j, 0:96], ident[0:BN, 0:BN])
                    for c in range(3):
                        m = eng.transpose(psN[j % 2][0:vb, 128 * (c + 1):128 * (c + 1) + BN],
                                          acc[:, j, 96 + c * vb:96 + (c + 1) * vb], ident[0:BN, 0:BN])
                    m.then_inc(s_at, 1)

                def mout(j):
                    eng.wait_ge(s_ac, base + j + 1)
                    if base + j >= 2:
                        eng.wait_ge(s_xo, base + j - 1)
                    ns = 96 if l == 2 else 64
                    for a in range(n2):
                        o = psO[j % 2][0:BN, a * 160:a * 160 + ns + 96]
                        os_ = OS[l][:, a, :] if l == 1 else OS[l][:, :]
                        ov = OV[l][:, a, :] if l == 1 else OV[l][:, :]
                        eng.matmul(o[:, 0:ns], aT[j % 2][0:96, 0, 0:BN], os_, start=True, stop=True)
                        for c in range(3):
                            m = eng.matmul(o[:, ns + c:ns + 96:3], aT[j % 2][0:vb, c + 1, 0:BN], ov, start=True, stop=True)
                    m.then_inc(s_oo, 1)

                tout(0)
                for j in range(NB):
                    if j + 1 < NB:
                        tout(j + 1)
                    mout(j)

        @block.scalar
        def _(eng):
            own = 0
            eng.wait_ge(s_sq, 1)
            eng.activation(bq, bq, ACT.Sqrt, scale=1.0 / 3.0).then_inc(s_sqd, 1)
            for l, p in enumerate(LAYERS):
                kf_, hid, vb = p["kf"], p["hid"], p["vb"]
                base = l * NB
                eng.wait_ge(s_ve, l + 1)
                eng.activation(VE[:, :], VE[:, :], ACT.Sqrt).then_inc(s_sd, 1)
                eng.wait_ge(s_st, l + 1)

                def hid_(j):
                    if base + j >= 4:
                        eng.wait_ge(s_tp, base + j - 3 if j >= 4 else base)
                    eng.activation(h[j % 4], X[:, j, :], ACT.Relu, bias=NM[:, j:j + 1], scale=RS[:, j:j + 1])\
                       .then_inc(s_h, 1)

                def evac(j):
                    eng.wait_ge(s_po, base + j + 1)
                    if j >= 2:
                        eng.wait_ge(s_hd[l][j % 2], (32 if l >= 2 else 16) * (j // 2))
                    o = psO[j % 2][0:BN, :]
                    if l == 0:
                        m = eng.activation(EV[j % 2][:, 0:160], o[:, 0:160], ACT.Copy, scale=Z1[:, j:j + 1])
                    elif l == 1:
                        m = eng.activation(EV[j % 2][:, 0:320], o[:, 0:320], ACT.Copy, scale=Z1[:, j:j + 1])
                    elif l == 2:
                        m = eng.activation(EV[j % 2][:, 0:352], o[:, 0:352], ACT.Copy)
                    else:
                        m = eng.activation(EV[j % 2][:, 0:320], o[:, 0:320], ACT.Copy, scale=Z1[:, j:j + 1])
                    m.then_inc(s_ev, 1)

                def store(j):
                    eng.wait_ge(s_xn if l == 1 else s_ev, base + j + 1)
                    eng.dma_start(HT[htile(l, j), :], EV[j % 2][:, 0:160]).then_inc(s_hd[l][j % 2], 16)
                    if l >= 2:
                        k = 192 if l == 2 else 160
                        eng.dma_start(SC[htile(l, j), 0:k], EV[j % 2][:, 160:160 + k]).then_inc(s_hd[l][j % 2], 16)

                for j in range(3):
                    hid_(j)
                for j in range(NB):
                    if j + 3 < NB:
                        hid_(j + 3)
                    evac(j)
                    if j >= 1:
                        store(j - 1)
                store(NB - 1)

                e, b = EG[l], 0 if p["t"] == "A" else 1
                eng.wait_ge(s_bk, NKEYS)
                n = eng.value_load(NI[b][0:1, 0:1], min_val=49, max_val=NG // 4 - 1)

                def edge_e(i, u, d):
                    eng.wait_ge(e.T, i * 4 + (u + d + 1))
                    if not (isinstance(i, int) and i * 4 + u + d < 2):
                        eng.wait_ge(e.F1, i * 4 + (u + d - 1))
                    eng.activation(ET[(u + d) % 2][0:kf_, :], psT[0:kf_, :], ACT.Copy).then_inc(e.E, 1)

                def edge_s(i, u, d):
                    eng.wait_ge(e.F1, i * 4 + (u + d + 1))
                    if not (isinstance(i, int) and i * 4 + u + d < 2):
                        eng.wait_ge(e.F2, i * 4 + (u + d - 1))
                    eng.activation(HH[(u + d) % 2][0:hid, :], psH[0:hid, :], p["fn"], scale=p["scale"]).then_inc(e.S, 1)

                edge_e(0, 0, 0)
                edge_e(0, 0, 1)
                edge_e(0, 0, 2)
                edge_s(0, 0, 0)
                edge_s(0, 0, 1)
                with eng.Fori(0, n) as i:
                    for u in range(4):
                        edge_s(i, u, 2)
                        edge_e(i, u, 3)
                eng.wait_ge(s_le, l + 1)

                def acopy(j):
                    eng.wait_ge(s_at, base + j + 1)
                    if base + j >= 2:
                        eng.wait_ge(s_oo, base + j - 1)
                    eng.activation(aT[j % 2][0:96, 0, 0:BN], psN[j % 2][0:96, 0:BN], ACT.Copy)
                    v = psN[j % 2].rearrange("p (a n) -> p a n", a=4)
                    eng.activation(aT[j % 2][0:vb, 1:4, 0:BN], v[0:vb, 1:4, 0:BN], ACT.Copy).then_inc(s_ac, 1)

                def gate(j):
                    eng.wait_ge(s_o, j + 1)
                    if j >= 2:
                        eng.wait_ge(s_xo, base + j - 1)
                    eng.activation(SG[j % 2], OO[j % 2][:, 0:96], ACT.Sigmoid).then_inc(s_sg, 1)

                if l == 3:
                    eng.wait_ge(s_an, 1)
                    eng.activation(SN[:, :], SN[:, :], ACT.Sin).then_inc(s_sn, 1)
                    eng.activation(CS[:, :], CS[:, :], ACT.Sin).then_inc(s_sn, 1)
                for j in range(NB):
                    acopy(j)
                    if l == 2 and j >= 1:
                        gate(j - 1)
                if l == 2:
                    gate(NB - 1)

        @block.vector
        def _(eng):
            own = 0

            def v(ins):
                nonlocal own
                own += 1
                ins.then_inc(s_d, 1)
                return own

            def w_(k=None):
                eng.wait_ge(s_d, own if k is None else k)

            eng.wait_ge(s_key, 32)
            v(eng.memset(z16, 0.0))
            for b, (key, loc, ps) in enumerate(((keyA, locA, posA), (keyB, locB, posB))):
                if b == 1:
                    eng.wait_ge(s_bk, 1)
                v(eng.tensor_scalar(kf, key, 1.0, None, ALU.add))
                w_()
                v(eng.tensor_scalar(bq, kf, float(-(BN + 1) // 2), 1.0 / BN, ALU.add, ALU.mult))
                w_()
                v(eng.tensor_scalar(bq, bq, MAGIC, -MAGIC, ALU.add, ALU.add))
                w_()
                v(eng.tensor_copy(bb, bq))
                v(eng.scalar_tensor_tensor(out=loc, in0=bq, scalar=-float(BN), in1=kf, op0=ALU.mult, op1=ALU.add))
                w_()
                for q in range(NB):
                    m = eng.tensor_scalar(masks[:, q, :], bb, float(q), None, ALU.is_equal, ALU.add,
                                          accum_out=CNT[:, q:q + 1])
                m.then_inc(s_cn, 1)
                eng.wait_ge(s_cn, b + 1)
                eng.wait_ge(s_cp, b + 1)
                v(eng.tensor_scalar(GRP[:, :], psO[1][:, 0:NB], GE / 2 - 0.5, 1.0 / GE, ALU.add, ALU.mult))
                w_()
                v(eng.tensor_scalar(GRP[:, :], GRP[:, :], MAGIC, -MAGIC, ALU.add, ALU.add))
                v(eng.memset(pos, 0.0))
                w_()
                v(eng.tensor_tensor_scan(INC[:, :], GRP[:, :], pos[:, 0:NB], 0.0, ALU.add, ALU.add))
                w_()
                v(eng.tensor_tensor(OFF[:, :], INC[:, :], GRP[:, :], ALU.subtract))
                w_()
                v(eng.tensor_scalar(OFF[:, :], OFF[:, :], float(GE), -1.0, ALU.mult, ALU.add))
                w_()
                v(eng.tensor_tensor(OFF[:, :], OFF[:, :], psO[0][:, 0:NB], ALU.add))
                v(eng.tensor_tensor_scan(cum, z16, z16, float(ROWS), ALU.add, ALU.add)) if False else None
                v(eng.memset(bq, 1.0))
                w_()
                v(eng.tensor_tensor_scan(pos, bq, z16, float(ROWS - 1), ALU.add, ALU.add))
                w_()
                for q in range(NB):
                    t = (cum, kf)[q % 2]
                    v(eng.tensor_tensor_scan(t, masks[:, q, :], z16, OFF[:, q:q + 1], ALU.add, ALU.add))
                    w_()
                    v(eng.copy_predicated(pos, masks[:, q, :].bitcast(U16), t))
                w_()
                eng.tensor_copy(ps, pos).then_inc(s_pos, 1)
                eng.wait_ge(s_gm, 4)
                eng.wait_ge(s_pos, b + 1)
                for q in range(4):
                    v(eng.tensor_tensor(cmp_, INC[0:1, :].unsqueeze(1).to_broadcast([1, 64, NB]),
                                        GI[:, q * 64:(q + 1) * 64].unsqueeze(2).to_broadcast([1, 64, NB]), ALU.is_le))
                    w_()
                    v(eng.tensor_reduce(BKF[:, q * 64:(q + 1) * 64], cmp_, mybir.AxisListType.X, ALU.add))
                    w_()
                v(eng.tensor_scalar(BK[b][:, :], BKF[:, :], float(NB - 1), None, ALU.min))
                v(eng.tensor_scalar(NIF[:, :], INC[0:1, NB - 1:NB], 1.5, 0.25, ALU.add, ALU.mult))
                w_()
                v(eng.tensor_scalar(NIF[:, :], NIF[:, :], MAGIC, -MAGIC, ALU.add, ALU.add))
                w_()
                eng.tensor_copy(NI[b][:, :], NIF[:, :]).then_inc(s_bk, 1)

            eng.wait_ge(s_sh, 16)
            v(eng.tensor_tensor(kf, sh[:, :, 0], sh[:, :, 0], ALU.mult))
            v(eng.tensor_tensor(cum, sh[:, :, 1], sh[:, :, 1], ALU.mult))
            v(eng.tensor_tensor(pos, sh[:, :, 2], sh[:, :, 2], ALU.mult))
            eng.wait_ge(s_bk, 2)
            w_()
            v(eng.tensor_tensor(kf, kf, cum, ALU.add))
            w_()
            eng.tensor_tensor(bq, kf, pos, ALU.add).then_inc(s_sq, 1)
            eng.wait_ge(s_sqd, 1)
            v(eng.reciprocal(cum, bq))
            w_()
            eng.tensor_tensor(sh, sh, cum.unsqueeze(2).to_broadcast([128, EC, 3]), ALU.mult).then_inc(s_shd, 1)

            eng.wait_ge(s_w, 16 * len(loads))
            eng.wait_ge(s_g, 12)
            r32 = float(1 / np.sqrt(32.0))
            r96 = float(1 / np.sqrt(96.0))

            def mul(t, c):
                v(eng.tensor_scalar(t, t, float(c), None, ALU.mult))

            mul(WS[0][:, 0:64], 1 / 8)
            mul(WS[0][:, 64:128], C_S / 8)
            mul(KV[0][:, 0:96], r32)
            mul(KV[0][:, 96:192], C_S * r32)
            mul(WS[1][:, :, 64:128], C_S)
            mul(KV[1][:, :, 96:192], C_S)
            mul(WS[3][:, :], 1 / 8)
            mul(KV[3][:, :], r32)
            c = C_X * r96 / np.sqrt(8.0) / 10
            v(eng.tensor_scalar(OS[0][:, :], OS[0][:, :], RSC[0:96, 0:1], float(c), ALU.mult, ALU.mult))
            mul(OV[0][:, :], c)
            v(eng.tensor_scalar(OS[2][:, :], OS[2][:, :], RSC[0:96, 0:1], 1 / 32, ALU.mult, ALU.mult))
            v(eng.tensor_scalar(OV[2][:, :], OV[2][:, :], RSC[:, 1:2], 1 / 32, ALU.mult, ALU.mult))
            c = r96 / 4 / 8
            v(eng.tensor_scalar(OS[3][:, :], OS[3][:, :], RSC[0:96, 0:1], float(c), ALU.mult, ALU.mult))
            mul(OV[3][:, :], c)
            mul(L3W[:, 0:64], 0.1 * c)
            mul(L3W[:, 64:96], 0.1 * c / R3)
            eng.wait_ge(s_rt, 1)
            eng.tensor_copy(NP[0:96, 2368:2752], psN[0][0:96, 0:384]).then_inc(s_rc, 1)
            eng.wait_ge(s_rp, 1)
            for a in range(2):
                v(eng.tensor_scalar(OS[1][:, a, :], psN[1][0:96, a * 96:a * 96 + 64], RSC[0:96, 0:1], C_X / 4, ALU.mult, ALU.mult))
                v(eng.tensor_scalar(OV[1][:, a, :], psN[1][0:96, a * 96 + 64:a * 96 + 96], C_X / 4, None, ALU.mult))
            eng.wait_ge(s_x, 64)
            v(eng.tensor_tensor(SA[:, :], Z1[:, :], Z3[:, :], ALU.mult))
            v(eng.tensor_tensor(SCC[:, :], Z2[:, :], Z3[:, :], ALU.mult))
            w_()
            eng.sem_inc(s_ws, 1)

            for l, p in enumerate(LAYERS):
                vb = p["vb"]
                nm = 96 + 3 * vb
                base = l * NB
                for j in range(NB):
                    v(eng.bn_stats(STT[:, j, :], X[:, j, :]))
                w_()
                for j in range(NB):
                    v(eng.bn_aggr(MV[:, j, :], STT[:, j, :]))
                w_()
                eng.tensor_scalar(VE[:, :], MV[:, :, 1], 1e-5, None, ALU.add).then_inc(s_ve, 1)
                eng.wait_ge(s_sd, l + 1)
                v(eng.reciprocal(RS[:, :], VE[:, :]))
                w_()
                eng.scalar_tensor_tensor(out=NM[:, :], in0=MV[:, :, 0], scalar=-1.0, in1=RS[:, :],
                                         op0=ALU.mult, op1=ALU.mult).then_inc(s_st, 1)

                def hcopy(j):
                    eng.wait_ge(s_tp, base + j + 1)
                    if base + j >= 2:
                        eng.wait_ge(s_po, base + j - 1)
                    eng.tensor_copy(hT[j % 2][0:64, 0, 0:BN], psN[j % 2][0:64, 0:BN])
                    eng.tensor_copy(hT[j % 2][0:96, 1, 0:BN], psN[j % 2][0:96, 128:128 + BN]).then_inc(s_ht, 1)

                def xnode(j):
                    eng.wait_ge(s_po, base + j + 1)
                    if l == 0:
                        eng.scalar_tensor_tensor(out=X[:, j, :], in0=psC[j % 2][0:BN, 160:320], scalar=Z1[:, j:j + 1],
                                                 in1=X[:, j, :], op0=ALU.mult, op1=ALU.add).then_inc(s_xn, 1)
                    elif l == 1:
                        eng.wait_ge(s_ev, base + j + 1)
                        v(eng.scalar_tensor_tensor(out=EV[j % 2][:, 0:320], in0=psC[j % 2][0:BN, 0:320],
                                                   scalar=Z2[:, j:j + 1], in1=EV[j % 2][:, 0:320],
                                                   op0=ALU.mult, op1=ALU.add))
                        w_()
                        eng.tensor_tensor(X[:, j, :], X[:, j, :], EV[j % 2][:, 160:320], ALU.add).then_inc(s_xn, 1)
                    else:
                        eng.sem_inc(s_xn, 1)

                hcopy(0)
                for j in range(NB):
                    if j + 1 < NB:
                        hcopy(j + 1)
                    xnode(j)

                e, b = EG[l], 0 if p["t"] == "A" else 1
                R = RA if b == 0 else RB
                yc, lc = (YC, LOCC) if b == 0 else (SHC, LOCB)
                eng.wait_ge(s_az, l + 1)
                eng.wait_ge(s_bk, NKEYS)
                n = eng.value_load(NI[b][0:1, 0:1], min_val=49, max_val=NG // 4 - 1)
                acc = ACC[0:BN, 0:NB * nm].rearrange("p (j f) -> p j f", j=NB)
                eng.sem_inc(e.M, 4)
                eng.sem_inc(e.V, 1)
                eng.sem_inc(e.A, 1)
                ND = 10 if l != 2 else 14

                def add(i, u, q):
                    j = eng.value_load(BK[b][0:1, bass.ds(i * 4 + u, 1)], min_val=0, max_val=NB - 1)
                    eng.wait_ge(e.A, i * 4 + (u + 2))
                    eng.tensor_tensor(acc[:, bass.ds(j, 1), :], acc[:, bass.ds(j, 1), :],
                                      psA[q][0:BN, 0:nm].unsqueeze(1), ALU.add).then_inc(e.V, 1)

                with eng.Fori(0, n) as i:
                    for u in range(4):
                        q = u % 2
                        tb = TT[u][:, 0:G * R].rearrange("p (t f) -> p t f", t=G)
                        m4 = MS[q][:, 0:G * nm].rearrange("p (t f) -> p t f", t=G)
                        mv = m4[:, :, 96:nm].rearrange("p t (c f) -> p t c f", c=3)
                        e0 = GB[q][:, :, 0:64]
                        e1 = GB[q][:, :, 64:160].rearrange("p t (c f) -> p t c f", c=3)
                        W = psW[q]
                        done = 0

                        def op(ins):
                            nonlocal done
                            ins.then_inc(e.D, 1)
                            done += 1
                            return done

                        def need(k):
                            eng.wait_ge(e.D, i * (4 * ND) + (u * ND + k))

                        y1 = tb[:, :, yc + 1:yc + 4] if l != 2 else tb[:, :, yc:yc + 3]
                        y1b = y1.unsqueeze(3)
                        eng.wait_ge(e.L[u], i * 16 + 16)
                        eng.wait_ge(e.A, i * 4 + (u + 1))
                        op(eng.tensor_tensor(OH[q], iota1[:, :].unsqueeze(1).to_broadcast([128, G, BN]),
                                             tb[:, :, lc:lc + 1].to_broadcast([128, G, BN]), ALU.is_equal))
                        eng.wait_ge(e.G[q], i * 128 + (u // 2 * 64 + 64))
                        if l != 2:
                            y0 = tb[:, :, yc:yc + 1]
                            need(1)
                            kp = op(eng.tensor_tensor(tp[q], e1, y1b.to_broadcast([128, G, 3, 32]), ALU.mult))
                            ky = op(eng.tensor_tensor(ty[q], e0, y0.to_broadcast([128, G, 64]), ALU.mult))
                            eng.wait_ge(e.F2, i * 4 + (u + 1))
                            kt = op(eng.tensor_tensor(tt_[q], W[:, :, 64:128], e0, ALU.mult))
                            ku = op(eng.tensor_tensor(tu[q], W[:, :, 128:160], y0.to_broadcast([128, G, 32]), ALU.mult))
                            need(kp)
                            kq = op(eng.tensor_tensor(tq[q], tp[q][:, :, 0, :], tp[q][:, :, 1, :], ALU.add))
                            need(ky)
                            op(eng.tensor_tensor(m4[:, :, 0:64], W[:, :, 0:64], ty[q], ALU.mult))
                            need(kq)
                            kr = op(eng.tensor_tensor(tq[q], tq[q], tp[q][:, :, 2, :], ALU.add))
                            need(kt)
                            op(eng.tensor_tensor(mv[:, :, :, 0:64], tt_[q].unsqueeze(2).to_broadcast([128, G, 3, 64]),
                                                 y1b.to_broadcast([128, G, 3, 64]), ALU.mult))
                            need(kr)
                            op(eng.tensor_tensor(m4[:, :, 64:96], W[:, :, 160:192], tq[q], ALU.mult))
                            need(ku)
                            op(eng.engine_nop()) if False else None
                            eng.tensor_tensor(mv[:, :, :, 64:96], tu[q].unsqueeze(2).to_broadcast([128, G, 3, 32]),
                                              e1, ALU.mult).then_inc(e.M, 1)
                        else:
                            need(1)
                            kp = op(eng.tensor_tensor(tp[q], e1, y1b.to_broadcast([128, G, 3, 32]), ALU.mult))
                            eng.wait_ge(e.F2, i * 4 + (u + 1))
                            kw = op(eng.tensor_tensor(tw[:, :, 0:3, :], e1,
                                                      W[:, :, 192:224].unsqueeze(2).to_broadcast([128, G, 3, 32]), ALU.mult))
                            kt = op(eng.tensor_tensor(tt_[q], W[:, :, 64:128], e0, ALU.mult))
                            op(eng.tensor_tensor(m4[:, :, 0:64], W[:, :, 0:64], e0, ALU.mult))
                            need(kp)
                            kq = op(eng.tensor_tensor(tq[q], tp[q][:, :, 0, :], tp[q][:, :, 1, :], ALU.add))
                            need(kw)
                            kx = op(eng.tensor_copy(tw[:, :, 3:5, :], tw[:, :, 0:2, :]))
                            need(kq)
                            kr = op(eng.tensor_tensor(tq[q], tq[q], tp[q][:, :, 2, :], ALU.add))
                            need(kt)
                            op(eng.tensor_tensor(mv[:, :, :, 0:64], tt_[q].unsqueeze(2).to_broadcast([128, G, 3, 64]),
                                                 y1b.to_broadcast([128, G, 3, 64]), ALU.mult))
                            need(kx)
                            k1 = op(eng.tensor_tensor(mv[:, :, :, 96:128], tw[:, :, 1:4, :],
                                                      tb[:, :, yc + 2:yc + 5].unsqueeze(3).to_broadcast([128, G, 3, 32]),
                                                      ALU.mult))
                            k2 = op(eng.tensor_tensor(tx, tw[:, :, 2:5, :],
                                                      tb[:, :, yc + 1:yc + 4].unsqueeze(3).to_broadcast([128, G, 3, 32]),
                                                      ALU.mult))
                            need(kr)
                            op(eng.tensor_tensor(m4[:, :, 64:96], W[:, :, 160:192], tq[q], ALU.mult))
                            op(eng.tensor_tensor(mv[:, :, :, 64:96], e1,
                                                 W[:, :, 128:160].unsqueeze(2).to_broadcast([128, G, 3, 32]), ALU.mult))
                            need(k2)
                            op(eng.tensor_tensor(mv[:, :, :, 96:128], mv[:, :, :, 96:128], tx, ALU.subtract))
                            need(done)
                            eng.sem_inc(e.M, 1)
                        assert done == ND, done
                        add(i, u, 1 - q)
                j = eng.value_load(BK[b][0:1, bass.ds(n * 4, 1)], min_val=0, max_val=NB - 1)
                eng.wait_ge(e.A, n * 4 + 2)
                eng.wait_ge(e.V, n * 4 + 1)
                eng.tensor_tensor(acc[:, bass.ds(j, 1), :], acc[:, bass.ds(j, 1), :],
                                  psA[1][0:BN, 0:nm].unsqueeze(1), ALU.add).then_inc(s_le, 1)
                eng.wait_ge(s_le, l + 1)

                if l == 3:
                    for j in range(NB):
                        t = FP[0][:, 0:96]
                        v(eng.scalar_tensor_tensor(out=t, in0=acc[:, j, 0:96], scalar=1.0, in1=L3W[:, :], op0=ALU.mult,
                                                   op1=ALU.mult, accum_out=ANG[:, j:j + 1]))
                        w_()
                    v(eng.tensor_tensor(ANG[:, :], ANG[:, :], Z1[:, :], ALU.mult))
                    w_()
                    for T, ph in ((SN, 0.0), (CS, 0.25)):
                        v(eng.tensor_scalar(KK[:, :], ANG[:, :], float(1 / (2 * np.pi)), ph, ALU.mult, ALU.add))
                        w_()
                        v(eng.tensor_scalar(KK[:, :], KK[:, :], MAGIC, -MAGIC, ALU.add, ALU.add))
                        w_()
                        v(eng.scalar_tensor_tensor(out=T[:, :], in0=KK[:, :], scalar=-6.28125, in1=ANG[:, :],
                                                   op0=ALU.mult, op1=ALU.add))
                        w_()
                        v(eng.scalar_tensor_tensor(out=T[:, :], in0=KK[:, :], scalar=-float(2 * np.pi - 6.28125),
                                                   in1=T[:, :], op0=ALU.mult, op1=ALU.add))
                        w_()
                        if ph:
                            v(eng.tensor_scalar(T[:, :], T[:, :], float(np.pi / 2), None, ALU.add))
                            w_()
                        v(eng.tensor_scalar(T[:, :], T[:, :], float(np.float32(np.pi)) * (1 - 1e-7),
                                            -float(np.float32(np.pi)) * (1 - 1e-7), ALU.min, ALU.max))
                        w_()
                    eng.sem_inc(s_an, 1)
                    eng.wait_ge(s_sn, 2)
                    v(eng.tensor_tensor(SN[:, :], SN[:, :], Z1[:, :], ALU.mult))
                    w_()

                def fin2(j):
                    eng.wait_ge(s_sg, j + 1)
                    o, s, f = OO[j % 2], SG[j % 2], FP[j % 2]
                    v(eng.tensor_tensor(f[:, 0:64], o[:, 0:64], s[:, 0:64], ALU.mult))
                    v(eng.tensor_tensor(f[:, 64:160].rearrange("p (w c) -> p w c", c=3),
                                        o[:, 96:192].rearrange("p (w c) -> p w c", c=3),
                                        s[:, 64:96].unsqueeze(2).to_broadcast([BN, 32, 3]), ALU.mult))
                    w_()
                    eng.tensor_tensor(X[:, j, :], X[:, j, :], f, ALU.add).then_inc(s_xo, 1)

                for j in range(NB):
                    eng.wait_ge(s_oo, base + j + 1)
                    o = psO[j % 2][0:BN, :]
                    if l == 0:
                        eng.scalar_tensor_tensor(out=X[:, j, :], in0=o[:, 0:160], scalar=Z1[:, j:j + 1], in1=X[:, j, :],
                                                 op0=ALU.mult, op1=ALU.add).then_inc(s_xo, 1)
                    elif l == 1:
                        v(eng.scalar_tensor_tensor(out=X[:, j, :], in0=o[:, 0:160], scalar=SA[:, j:j + 1], in1=X[:, j, :],
                                                   op0=ALU.mult, op1=ALU.add))
                        w_()
                        eng.scalar_tensor_tensor(out=X[:, j, :], in0=o[:, 160:320], scalar=SCC[:, j:j + 1], in1=X[:, j, :],
                                                 op0=ALU.mult, op1=ALU.add).then_inc(s_xo, 1)
                    elif l == 2:
                        eng.wait_ge(s_sk[0][j % 2], 16 * (j // 2 + 1))
                        if j >= 2:
                            eng.wait_ge(s_xo, base + j - 1)
                        eng.tensor_tensor(OO[j % 2], o[:, 0:192], SK[j % 2], ALU.add).then_inc(s_o, 1)
                        if j >= 1:
                            fin2(j - 1)
                    else:
                        eng.wait_ge(s_sk[1][j % 2], 16 * (j // 2 + 1))
                        v(eng.scalar_tensor_tensor(out=X[:, j, :], in0=SK[j % 2][:, 0:160], scalar=CS[:, j:j + 1],
                                                   in1=X[:, j, :], op0=ALU.mult, op1=ALU.add))
                        w_()
                        eng.scalar_tensor_tensor(out=X[:, j, :], in0=o[:, 0:160], scalar=SN[:, j:j + 1], in1=X[:, j, :],
                                                 op0=ALU.mult, op1=ALU.add).then_inc(s_xo, 1)
                if l == 2:
                    fin2(NB - 1)
                eng.wait_ge(s_xo, base + NB)


def kernel(**inputs):
    import numpy as _np
    import concourse.bacc as _bacc
    from concourse import mybir as _mybir
    from concourse.bass_utils import run_bass_kernel_spmd as _run

    a = {k: _np.ascontiguousarray(v) for k, v in inputs.items()}

    def rows(t, n):
        return _np.concatenate([t, _np.zeros((n - t.shape[0],) + t.shape[1:], t.dtype)])

    def key(t):
        return _np.concatenate([t, _np.full((EPAD - E,), NOKEY, t.dtype)])

    host = dict(a)
    host["x"] = rows(a["x"], NPAD)
    host["keya"], host["keyb"] = key(a["dst"]), key(a["src"])
    ea = _np.concatenate([a["edge_attr_12"], a["edge_attr_10"], a["edge_attr_8"], a["edge_attr_4"],
                          _np.zeros((E, 2), a["x"].dtype)], axis=1)
    eb = _np.concatenate([a["edge_attr_64"], a["edge_attr_3"], _np.zeros((E, RB - 67), a["x"].dtype)], axis=1)
    host["ea"] = rows(ea, EPAD)
    host["eb"] = _np.concatenate([eb, _np.ones((EPAD - E, RB), eb.dtype)])
    for n, s in (("z1", "node_vec1"), ("z2", "node_vec1_n2"), ("z3", "node_vec1_n3")):
        host[n] = _np.ascontiguousarray(rows(a[s], NPAD).reshape(NB, BN).T)
    nc = _bacc.Bacc("TRN2", target_bir_lowering=False, num_devices=1)
    arrays, args = {}, {}
    for name in _INS:
        t = host[name]
        arrays[f"in_{name}"] = t
        args[name] = nc.dram_tensor(f"in_{name}", t.shape, _mybir.dt.from_np(t.dtype), kind="ExternalInput").ap()
    o = nc.dram_tensor("out_0", (N, D), _mybir.dt.float32, kind="ExternalOutput").ap()
    program(nc, args, o)
    r = _run(nc, [arrays], core_ids=[0])
    return r.results[0]["out_0"]
```

```python
from contextlib import ExitStack

import numpy as np

import concourse.bass as bass
from concourse import mybir

F32 = mybir.dt.float32
I32 = mybir.dt.int32
BF16 = mybir.dt.bfloat16
U16 = mybir.dt.uint16
ALU = mybir.AluOpType
ACT = mybir.ActivationFunctionType

N = 6250
E = 100000
D = 160
BN = 123
NB = 51
NPAD = BN * NB
LAST = N - (NB - 1) * BN
EC = 782
EPAD = 128 * EC
NOKEY = NPAD - 1
G = 4
GE = 128 * G
NG = 252
ROWS = EPAD + GE
RA, RB = 36, 72
CHA, CHB = 34, 16
NCHA = EC // CHA
SB0, SB1 = 102, 144
SBU = (2, 0, 2, 0)
NT0 = 49
SLOOP = NT0 * sum(SBU)
assert SB0 + 2 * SLOOP + 2 * SB1 == EC and EC % CHA == 0
BLK, LAG = 4, 10
ND2, KT2 = 13, 3
NBK = -(-NB // BLK)


def chunks(c0, n):
    return [(c, min(CHB, c0 + n - c)) for c in range(c0, c0 + n, CHB)]


BCH = [chunks(0, SB0), chunks(SB0 + SLOOP, SB1), chunks(SB0 + 2 * SLOOP + SB1, SB1)]
BL0 = [SB0, SB0 + SLOOP + SB1]

MAGIC = 12582912.0
C_S, C_X = float(np.sin(np.pi / 8)), float(np.cos(np.pi / 8))
R3 = float(np.sqrt(3.0))

LAYERS = [
    dict(t="A", kf=12, c0=0, hid=100, wn=192, vb=96, scale=float(1 / np.sqrt(12.0)), fn=ACT.Silu),
    dict(t="A", kf=10, c0=12, hid=100, wn=192, vb=96, scale=1.0, fn=ACT.Silu),
    dict(t="B", kf=64, c0=0, hid=64, wn=224, vb=128, scale=1.0, fn=ACT.Relu),
    dict(t="A", kf=8, c0=22, hid=64, wn=192, vb=96, scale=float(1 / np.sqrt(8.0)), fn=ACT.Silu),
]
YC, SRCC, LOCC = 30, 34, 35
SHC, DSTC, LOCB, POSC = 64, 69, 70, 71

_INS = [
    "x", "keya", "keyb", "keyn", "ea", "eb", "e3", "z1", "z2", "z3",
    "L0_gnn_W_sc0", "L0_gnn_W_sc1", "L0_gnn_W_l1_0", "L0_gnn_W_l1_1", "L0_gnn_W_fc1", "L0_gnn_W_fc2",
    "L0_gnn_W_l2_0", "L0_gnn_W_l2_1", "L1_gnn_Ws_sc_a", "L1_gnn_Wv_sc_a", "L1_gnn_Ws_sc_c", "L1_gnn_Wv_sc_c",
    "L1_gnn_Ws_l1_a", "L1_gnn_Wv_l1_a", "L1_gnn_Ws_l1_c", "L1_gnn_Wv_l1_c", "L1_gnn_W_fc1", "L1_gnn_W_fc2",
    "L1_gnn_Ws_l2_a", "L1_gnn_Wv_l2_a", "L1_gnn_Ws_l2_c", "L1_gnn_Wv_l2_c", "L1_gnn_Ws_l3", "L1_gnn_Wv_l3",
    "L2_gnn_W_skip0", "L2_gnn_W_skip1", "L2_gnn_W_nl0", "L2_gnn_W_nl1", "L2_gnn_W_fc1", "L2_gnn_W_fc2",
    "L2_gnn_W_out_s", "L2_gnn_W_out_v", "L3_gnn_sc_w0", "L3_gnn_sc_w1", "L3_gnn_lin1_w0", "L3_gnn_lin1_w1",
    "L3_gnn_fc_w1", "L3_gnn_fc_w2", "L3_gnn_lin2_w0", "L3_gnn_lin2_w1", "L3_gnn_lin3_w",
]


def program(nc, A, out):
    ctx = ExitStack()
    with ctx:
        def sb(name, shape, dt=F32):
            return ctx.enter_context(nc.sbuf_tensor(name, shape, dt))

        def sem(name):
            return ctx.enter_context(nc.semaphore(name))

        TA = nc.dram_tensor("TA", (ROWS, RA), F32).ap()
        TB = nc.dram_tensor("TB", (ROWS, RB), F32).ap()
        PB = nc.dram_tensor("PB", (EPAD, RB - 64), F32).ap()
        HT = nc.dram_tensor("HT", (NPAD, D), F32).ap()
        SC = nc.dram_tensor("SC", (NPAD, 192), F32).ap()

        X = sb("X", [BN, NB, D])
        ACC = sb("ACC", [128, NB * 480])
        WK = sb("WK", [128, 13136])
        NP = WK[:, 9486:13136]
        PS = ctx.enter_context(nc.psum_tensor("PS", [128, 4096], F32))

        ident = sb("ident", [128, 128])
        iota1 = sb("iota1", [128, BN])
        ZZ, Z3 = sb("ZZ", [BN, 2, NB]), sb("Z3", [BN, NB])
        Z1, Z2 = ZZ[:, 0, :], ZZ[:, 1, :]
        SA, SCC = sb("SA", [BN, NB]), sb("SCC", [BN, NB])
        STT = sb("STT", [BN, NB, 6])
        MV = sb("MV", [BN, NB, 2])
        VE, RS, NM = sb("VE", [BN, NB]), sb("RS", [BN, NB]), sb("NM", [BN, NB])
        ANG, KK, SN, CS = sb("ANG", [BN, NB]), sb("KK", [BN, NB]), sb("SN", [BN, NB]), sb("CS", [BN, NB])
        TI = [sb("TIA", [64, 256], I32), sb("TIB", [64, 256], I32)]
        BKO = [sb("BKOA", [128, 256]), sb("BKOB", [128, 256])]
        NIF = sb("NIF", [1, 1])
        NI = [sb("NIA", [1, 1], I32), sb("NIB", [1, 1], I32)]
        FLG = sb("FLG", [1, 1], I32)

        WS = [sb("WS0", [64, 128]), sb("WS1", [128, 128]), sb("WS2", [64, 160]), sb("WS3", [64, 128])]
        KV = [sb("KV0", [96, 192]), sb("KV1", [96, 2, 192]), sb("KV2", [96, 192]), sb("KV3", [96, 192])]
        F1 = [sb(f"F1_{l}", [p["kf"], p["hid"]]) for l, p in enumerate(LAYERS)]
        F2 = [sb(f"F2_{l}", [p["hid"], p["wn"]]) for l, p in enumerate(LAYERS)]
        OS = [sb("OS0", [96, 64]), sb("OS1", [96, 2, 64]), sb("OS2", [96, 96]), sb("OS3", [96, 64])]
        OV = [sb("OV0", [96, 32]), sb("OV1", [96, 2, 32]), sb("OV2", [128, 32]), sb("OV3", [96, 32])]
        L3W = sb("L3W", [BN, 96])
        RSC = sb("RSC", [128, 2])

        def wk(a, n, p=128):
            return WK[0:p, a:a + n]

        keyA, keyB = wk(0, EC).bitcast(I32), wk(EC, EC).bitcast(I32)
        nxt = wk(2 * EC, EC).bitcast(I32)
        rec = wk(3 * EC, EC)
        posA = wk(4 * EC, EC).bitcast(I32)
        sh = wk(6 * EC, 3 * EC).rearrange("p (c k) -> p c k", k=3)
        stage = [wk(9 * EC + i * CHA * RA, CHA * RA) for i in range(2)]
        PX = ACC[:, 0:EC * (RB - 64)].rearrange("p (c f) -> p c f", f=RB - 64)
        zero = wk(9 * EC, G * RB)
        masks = ACC[:, 0:NB * 391].bitcast(BF16).rearrange("p (b c) -> p b c", c=EC)
        tb0 = NB * 391
        kf, bq, cum, pos = (ACC[:, tb0 + i * EC:tb0 + (i + 1) * EC] for i in range(4))
        bb = ACC[:, tb0 + 4 * EC:tb0 + 4 * EC + 391].bitcast(BF16)
        z16 = ACC[:, tb0 + 4 * EC + 391:tb0 + 4 * EC + 782].bitcast(BF16)
        LT, ONE = NP[:, 0:128], NP[:, 128:256]
        CNT, INC, OFF = (NP[:, 256 + i * NB:256 + (i + 1) * NB] for i in range(3))
        CF = NP[:, 410:411]
        GI, CMP, BASF = NP[:, 640:896], NP[0:NB, 896:1152], NP[:, 1152:1408]
        GRP, DD, DDB, NGF = NP[0:NB, 411:412], NP[0:NB, 412:413], NP[0:NB, 1408:1536], NP[0:1, 413:414]
        ICC = NP[0:NB, 414:415]

        at = 0

        def take(n, p=128):
            nonlocal at
            v = WK[0:p, at:at + n]
            at += n
            return v

        TT = [take(G * RB) for _ in range(4)]
        GB = [take(G * D).rearrange("p (t f) -> p t f", t=G) for _ in range(2)]
        ET = [take(GE) for _ in range(2)]
        HH = [take(GE) for _ in range(2)]
        OH = [take(G * BN).rearrange("p (t f) -> p t f", t=G) for _ in range(2)]
        MS = [take(G * 480) for _ in range(2)]
        tq = [take(G * 32).rearrange("p (t f) -> p t f", t=G) for _ in range(2)]
        tu = [take(G * 32).rearrange("p (t f) -> p t f", t=G) for _ in range(2)]
        ty = [take(G * 64).rearrange("p (t f) -> p t f", t=G) for _ in range(1)] * 2
        tt_ = [take(G * 64).rearrange("p (t f) -> p t f", t=G) for _ in range(1)] * 2
        tp = [take(G * 96).rearrange("p (t c f) -> p t c f", t=G, c=3) for _ in range(1)] * 2
        tw = take(G * 160).rearrange("p (t c f) -> p t c f", t=G, c=5)
        tx = take(G * 96).rearrange("p (t c f) -> p t c f", t=G, c=3)
        assert at + 1280 <= 13136, at
        SL = [tw.rearrange("p t c f -> p (t c f)")[:, i * 2 * RB:(i + 1) * 2 * RB] for i in range(4)]
        stageM = [WK[:, 5464 + i * CHB * RB:5464 + (i + 1) * CHB * RB] for i in range(2)]

        h = [NP[0:BN, i * 160:(i + 1) * 160] for i in range(4)]
        hT = [NP[:, 640 + i * 384:1024 + i * 384].rearrange("p (a n) -> p a n", a=3) for i in range(2)]
        EV = [NP[0:BN, 1408 + i * 352:1760 + i * 352] for i in range(2)]
        aT = [NP[:, 2112 + i * 512:2624 + i * 512].rearrange("p (a n) -> p a n", a=4) for i in range(2)]
        SK = [NP[0:BN, 3136 + i * 192:3328 + i * 192] for i in range(2)]
        OO = [WK[0:BN, 2432 + i * 192:2624 + i * 192] for i in range(2)]
        SG = [WK[0:BN, 2816 + i * 96:2912 + i * 96] for i in range(2)]
        FP = [WK[0:BN, 3008 + i * 160:3168 + i * 160] for i in range(2)]
        hz = [WK[0:BN, 3328 + i * 320:3648 + i * 320] for i in range(2)]
        RW = [NP[0:96, 1856 + i * 96:1952 + i * 96] for i in range(4)]
        RWT = [NP[0:96, 2368 + i * 96:2464 + i * 96] for i in range(4)]
        RW3s, RW3v = NP[0:96, 2880:2944], NP[0:96, 2944:2976]

        def bank(i, n=512, p=128):
            return PS[0:p, i * 512:i * 512 + n]

        psW = [PS[:, i * 1024:(i + 1) * 1024].rearrange("p (t f) -> p t f", t=G) for i in range(2)]
        psH, psT = bank(4), bank(5)
        psA = [bank(6), bank(7)]
        psN = [bank(0), bank(1)]
        psO = [bank(2), bank(3)]
        psC = [bank(4), bank(5)]
        nT, nR = [bank(4), bank(5)], [bank(6), bank(7)]

        s_key, s_x, s_ld, s_w, s_ws, s_sh = (sem(n) for n in ("s_key", "s_x", "s_ld", "s_w", "s_ws", "s_sh"))
        s_g, s_gm = sem("s_g"), sem("s_gm")
        s_d, s_a, s_p = sem("s_d"), sem("s_a"), sem("s_p")
        s_zf = sem("s_zf")
        s_cn, s_cp, s_pos, s_bk = sem("s_cn"), sem("s_cp"), sem("s_pos"), sem("s_bk")
        s_sq, s_sqd, s_shd = sem("s_sq"), sem("s_sqd"), sem("s_shd")
        s_fl, s_gc, s_gi, s_gd, s_gq, s_rk = (sem(n) for n in ("s_fl", "s_gc", "s_gi", "s_gd", "s_gq", "s_rk"))
        s_nx, s_tb, s_free, s_tab = sem("s_nx"), sem("s_tb"), sem("s_free"), sem("s_tab")
        s_stg, s_prep = [sem("s_stg0"), sem("s_stg1")], sem("s_prep")
        s_ra, s_rb = [sem("s_ra0"), sem("s_ra1")], [sem("s_rb0"), sem("s_rb1")]
        s_bl, s_bs = ([sem(f"{n}{i}") for i in range(4)] for n in ("s_bl", "s_bs"))
        s_px = sem("s_px")
        s_ve, s_sd, s_st = sem("s_ve"), sem("s_sd"), sem("s_st")
        s_h, s_tp, s_ht, s_po, s_ev, s_xn = (sem(n) for n in ("s_h", "s_tp", "s_ht", "s_po", "s_ev", "s_xn"))
        s_hd = [[sem(f"s_hd{l}{i}") for i in range(2)] for l in range(4)]
        s_at, s_ac, s_oo, s_xo = (sem(n) for n in ("s_at", "s_ac", "s_oo", "s_xo"))
        s_sk = [[sem(f"s_sk{l}{i}") for i in range(2)] for l in (2, 3)]
        s_o, s_sg, s_hz = sem("s_o"), sem("s_sg"), sem("s_hz")
        s_an, s_sn = sem("s_an"), sem("s_sn")
        s_az, s_le, s_out = sem("s_az"), sem("s_le"), sem("s_out")
        s_go, s_pe, s_sp = sem("s_go"), sem("s_pe"), sem("s_sp")
        s_rt, s_rc, s_rp = sem("s_rt"), sem("s_rc"), sem("s_rp")

        class Edge:
            def __init__(self, l):
                self.L = [sem(f"e{l}_L{i}") for i in range(4)]
                self.G = [sem(f"e{l}_G{i}") for i in range(2)]
                self.T, self.E, self.F1, self.S, self.F2, self.M, self.A, self.V, self.D, self.N = (
                    sem(f"e{l}_{n}") for n in ("T", "E", "F1", "S", "F2", "M", "A", "V", "D", "N"))

        EG = [Edge(l) for l in range(4)]

        block = ctx.enter_context(nc.Block())
        NKEYS = 2
        loads = []

        def kron(l, a, col, W, interleaved):
            t = KV[l][:, a, :] if l == 1 else KV[l][:, :]
            for c in range(3):
                if interleaved:
                    loads.append((t[c:96:3, col + c:col + 96:3], W))
                else:
                    loads.append((t[c:96:3, col + 32 * c:col + 32 * c + 32], W))

        w = A
        loads += [(WS[0][:, 0:64], w["L0_gnn_W_l1_0"]), (WS[0][:, 64:128], w["L0_gnn_W_sc0"])]
        kron(0, 0, 0, w["L0_gnn_W_l1_1"], False)
        kron(0, 0, 96, w["L0_gnn_W_sc1"], True)
        for a, s in enumerate("ac"):
            loads += [(WS[1][64 * a:64 * a + 64, 0:64], w[f"L1_gnn_Ws_l1_{s}"]),
                      (WS[1][64 * a:64 * a + 64, 64:128], w[f"L1_gnn_Ws_sc_{s}"])]
            kron(1, a, 0, w[f"L1_gnn_Wv_l1_{s}"], False)
            kron(1, a, 96, w[f"L1_gnn_Wv_sc_{s}"], True)
            loads += [(RW[a], w[f"L1_gnn_Ws_l2_{s}"]), (RW[2 + a], w[f"L1_gnn_Wv_l2_{s}"])]
        loads += [(RW3s, w["L1_gnn_Ws_l3"]), (RW3v, w["L1_gnn_Wv_l3"])]
        loads += [(WS[2][:, 0:64], w["L2_gnn_W_nl0"]), (WS[2][:, 64:160], w["L2_gnn_W_skip0"])]
        kron(2, 0, 0, w["L2_gnn_W_nl1"], False)
        kron(2, 0, 96, w["L2_gnn_W_skip1"], True)
        loads += [(WS[3][:, 0:64], w["L3_gnn_lin1_w0"]), (WS[3][:, 64:128], w["L3_gnn_sc_w0"])]
        kron(3, 0, 0, w["L3_gnn_lin1_w1"], False)
        kron(3, 0, 96, w["L3_gnn_sc_w1"], True)
        for l, n in enumerate(("L0_gnn_W_fc", "L1_gnn_W_fc", "L2_gnn_W_fc", "L3_gnn_fc_w")):
            loads += [(F1[l][:, :], w[n + "1"]), (F2[l][:, :], w[n + "2"])]
        loads += [(OS[0][:, :], w["L0_gnn_W_l2_0"]), (OV[0][:, :], w["L0_gnn_W_l2_1"]),
                  (OS[2][:, :], w["L2_gnn_W_out_s"]), (OV[2][:, :], w["L2_gnn_W_out_v"]),
                  (OS[3][:, :], w["L3_gnn_lin2_w0"]), (OV[3][:, :], w["L3_gnn_lin2_w1"]),
                  (L3W[:, :], w["L3_gnn_lin3_w"].rearrange("k a -> a k").to_broadcast([BN, 96]))]

        def ended(lo, t):
            j = t - 1 if lo == 2 else t
            return j // BLK if 0 <= j < NB and (j % BLK == BLK - 1 or j == NB - 1) else None

        def htile(l, j):
            return slice(j * BN, (j + 1) * BN)

        @block.sync
        def _(eng):
            eng.dma_start(keyA, A["keya"].rearrange("(p c) -> p c", p=128)).then_inc(s_key, 16)
            eng.dma_start(nxt, A["keyn"].rearrange("(p c) -> p c", p=128)).then_inc(s_nx, 16)
            eng.dma_start(keyB, A["keyb"].rearrange("(p c) -> p c", p=128)).then_inc(s_key, 16)
            eng.dma_start(X[:, :, :], A["x"].rearrange("(j p) d -> p j d", p=BN)).then_inc(s_x, 16)
            for t, n in ((Z1, "z1"), (Z2, "z2"), (Z3[:, :], "z3")):
                eng.dma_start(t, A[n]).then_inc(s_x, 16)
            eng.wait_ge(s_gm, 2)
            with nc.allow_non_contiguous_dma(reason="small strided weights"):
                for d, s in loads:
                    eng.dma_start(d, s).then_inc(s_w, 16)
                eng.dma_start(sh, A["e3"].rearrange("(p c) f -> p c f", p=128)).then_inc(s_sh, 16)
            eng.wait_ge(s_gm, 3)
            for T, R in ((TA, RA), (TB, RB)):
                eng.dma_start(T[EPAD:ROWS, :].rearrange("(p t) f -> p (t f)", p=128), zero[:, 0:G * R]).then_inc(s_zf, 16)
            eng.wait_ge(s_zf, 32)
            k = 0
            v = A["ea"].rearrange("(p c) f -> p (c f)", p=128)
            for c in range(0, EC, CHA):
                if k >= 2:
                    eng.wait_ge(s_free, k - 1)
                eng.dma_start(stage[k % 2][:, 0:CHA * RA], v[:, c * RA:(c + CHA) * RA]).then_inc(s_stg[k % 2], 16)
                k += 1
            eng.wait_ge(s_tb, 1)
            eng.dma_start(PB.rearrange("(p c) f -> p (c f)", p=128), ACC[:, 0:EC * (RB - 64)]).then_inc(s_px, 16)
            eng.wait_ge(s_px, 16)
            ev = A["eb"].rearrange("(p c) f -> p c f", p=128)
            pv = PB.rearrange("(p c) f -> p c f", p=128)

            def rows_b(t, c, m, sm):
                st = t[:, 0:m * RB].rearrange("p (c f) -> p c f", f=RB)
                eng.dma_start(st[:, :, 0:64], ev[:, c:c + m, :] if isinstance(c, int) else ev[:, bass.ds(c, m), :])\
                   .then_inc(sm, 16)
                eng.dma_start(st[:, :, 64:RB], pv[:, c:c + m, :] if isinstance(c, int) else pv[:, bass.ds(c, m), :])\
                   .then_inc(sm, 16)

            for c, m in BCH[0]:
                eng.wait_ge(s_free, k - 1)
                rows_b(stage[k % 2], c, m, s_stg[k % 2])
                k += 1

            for l, p in enumerate(LAYERS):
                e, b = EG[l], 0 if p["t"] == "A" else 1
                R, T = (RA, TA) if b == 0 else (RB, TB)
                eng.wait_ge(s_tab, 1 if b == 0 else 2)
                eng.wait_ge(s_tb, 1)
                if l == 0:
                    eng.wait_ge(s_free, k)
                eng.wait_ge(s_xn, NB * (l + 1))
                m = 32 if l >= 2 else 16
                eng.wait_ge(s_hd[l][0], m * (NB - NB // 2))
                eng.wait_ge(s_hd[l][1], m * (NB // 2))
                eng.wait_ge(s_bk, NKEYS)
                n = eng.value_load(NI[b][0:1, 0:1], min_val=NT0 + 1, max_val=NG // 4 - 1)

                def load(i, u):
                    eng.wait_ge(e.M, i * 4 + (u + 1))
                    if l == 2:
                        eng.wait_ge(e.N, i * 4 + (u + 1))
                    r = eng.value_load(TI[b][32:33, bass.ds(i * 4 + (u + 1), 1)], min_val=0, max_val=EPAD)
                    eng.dma_start(TT[u][:, 0:G * R], T[bass.ds(r, GE), :].rearrange("(p t) f -> p (t f)", t=G))\
                       .then_inc(e.L[u], 16)

                if l < 2:
                    def slots(i):
                        o = 0
                        for u in range(4):
                            load(i, u)
                            if not SBU[u]:
                                continue
                            if not isinstance(i, int) or l:
                                eng.wait_ge(s_bs[u], i * (16 * SBU[u]) + 16 * SBU[u] * NT0 * l)
                                eng.sem_inc(s_sp, 1)
                            rows_b(SL[u], i * sum(SBU) + (BL0[l] + o), SBU[u], s_bl[u])
                            o += SBU[u]

                    slots(0)
                    with eng.Fori(1, NT0) as i:
                        slots(i)
                with eng.Fori(NT0 if l < 2 else 0, n + 1) as i:
                    for u in range(4):
                        load(i, u)
                for u in range(4):
                    eng.wait_ge(e.L[u], n * 16 + 16)
                eng.sem_inc(s_sp, 1)
                if l < 2:
                    eng.wait_ge(s_le, l + 1)
                    for c, m in BCH[l + 1]:
                        eng.wait_ge(s_free, k - 1)
                        rows_b(stageM[k % 2], c, m, s_stg[k % 2])
                        k += 1
                if l >= 2:
                    for j in range(NB):
                        if j >= 2:
                            eng.wait_ge(s_o if l == 2 else s_xo, (j - 1) if l == 2 else NB * 3 + j - 1)
                        else:
                            eng.wait_ge(s_le, l + 1)
                        eng.dma_start(SK[j % 2][:, 0:192 if l == 2 else 160],
                                      SC[htile(l, j), 0:192 if l == 2 else 160]).then_inc(s_sk[l - 2][j % 2], 16)
            for j in range(NB):
                eng.wait_ge(s_xo, NB * 3 + j + 1)
                r = BN if j < NB - 1 else LAST
                eng.dma_start(out[j * BN:j * BN + r, :], X[0:r, j, :]).then_inc(s_out, 16)
            eng.wait_ge(s_out, 16 * NB)

        @block.gpsimd
        def _(eng):
            for l in range(4):
                eng.memset(KV[l][:, :, :] if l == 1 else KV[l][:, :], 0.0).then_inc(s_g, 1)
            eng.memset(RSC[0:64, 0:1], 1.0).then_inc(s_g, 1)
            eng.memset(RSC[0:96, 1:2], 1.0).then_inc(s_g, 1)
            eng.wait_ge(s_g, 6)
            eng.memset(RSC[64:128, 0:1], 1.0 / R3).then_inc(s_g, 1)
            eng.wait_ge(s_g, 7)
            eng.memset(RSC[96:128, 1:2], float(1 / np.sqrt(2.0))).then_inc(s_g, 1)
            eng.wait_ge(s_g, 8)
            eng.memset(ident[:, :], 0.0).then_inc(s_g, 1)
            eng.memset(LT, 1.0).then_inc(s_g, 1)
            eng.wait_ge(s_g, 10)
            eng.affine_select(out=ident[:, :], in_=ident[:, :], compare_op=ALU.not_equal, fill=1.0, base=0,
                              pattern=[[-1, 128]], channel_multiplier=1).then_inc(s_gm, 1)
            eng.affine_select(out=LT, in_=LT, compare_op=ALU.is_gt, fill=0.0, base=0,
                              pattern=[[1, 128]], channel_multiplier=-1).then_inc(s_gm, 1)
            eng.memset(zero, 0.0).then_inc(s_gm, 1)
            eng.memset(ONE, 1.0).then_inc(s_g, 1)
            eng.iota(iota1[:, :], [[1, BN]], base=1, channel_multiplier=0,
                     allow_small_or_imprecise_dtypes=True).then_inc(s_g, 1)
            eng.iota(GI[:, :], [[1, 256]], base=-1, channel_multiplier=0,
                     allow_small_or_imprecise_dtypes=True).then_inc(s_gm, 1)

            k = 0

            def fill(st, sl):
                eng.tensor_copy(st[:, :, SRCC:SRCC + 1].bitcast(I32), keyB[:, sl].unsqueeze(2)).then_inc(s_prep, 1)
                eng.tensor_scalar(st[:, :, LOCC:LOCC + 1], keyA[:, sl].unsqueeze(2), 1.0, None, ALU.add).then_inc(s_prep, 1)

            def place(T, ps, st, sm):
                for q in range(st.shape[1]):
                    eng.indirect_dma_start(out=T[:, :], out_offset=bass.IndirectOffsetOnAxis(ap=ps(q), axis=0),
                                           in_=st[:, q, :], in_offset=None).then_inc(sm, 16)

            eng.wait_ge(s_key, 32)
            eng.wait_ge(s_fl, 1)
            flag = eng.value_load(FLG[0:1, 0:1], min_val=0, max_val=EPAD)
            TAv = TA[0:EPAD, :].rearrange("(p c) f -> p (c f)", p=128)
            for case in range(2):
                with eng.If_eq(flag.val, 0) if case == 0 else eng.If_ne(flag.val, 0):
                    if case == 1:
                        eng.wait_ge(s_pos, 1)
                    for k in range(NCHA):
                        eng.wait_ge(s_stg[k % 2], 16 * (k // 2 + 1))
                        st = stage[k % 2][:, 0:CHA * RA].rearrange("p (c f) -> p c f", f=RA)
                        fill(st, slice(k * CHA, (k + 1) * CHA))
                        eng.wait_ge(s_prep, 2 * (k + 1))
                        if case == 0:
                            eng.dma_start(TAv[:, k * CHA * RA:(k + 1) * CHA * RA], stage[k % 2][:, 0:CHA * RA])\
                               .then_inc(s_ra[k % 2], 16)
                        else:
                            place(TA, lambda q: posA[:, k * CHA + q:k * CHA + q + 1], st, s_ra[k % 2])
                        if k >= 1:
                            eng.wait_ge(s_ra[(k - 1) % 2], 16 * ((k - 1) // 2 + 1) * (1 if case == 0 else CHA))
                            eng.sem_inc(s_free, 1)
                    k = NCHA - 1
                    eng.wait_ge(s_ra[k % 2], 16 * (k // 2 + 1) * (1 if case == 0 else CHA))
                    eng.sem_inc(s_free, 1)
            eng.wait_ge(s_zf, 32)
            eng.sem_inc(s_tab, 1)
            k = NCHA
            cnt = [0, 0]
            stg_ = [16 * ((NCHA + 1) // 2), 16 * (NCHA // 2)]

            def move(cs, stg):
                nonlocal k
                for n, (c, m) in enumerate(cs):
                    stg_[k % 2] += 32
                    eng.wait_ge(s_stg[k % 2], stg_[k % 2])
                    st = stg[k % 2][:, 0:m * RB].rearrange("p (c f) -> p c f", f=RB)
                    place(TB, lambda q: st[:, q, POSC:POSC + 1].bitcast(I32), st, s_rb[k % 2])
                    cnt[k % 2] += 16 * m
                    if n >= 1:
                        eng.wait_ge(s_rb[(k - 1) % 2], cnt[(k - 1) % 2])
                        eng.sem_inc(s_free, 1)
                    k += 1
                eng.wait_ge(s_rb[(k - 1) % 2], cnt[(k - 1) % 2])
                eng.sem_inc(s_free, 1)

            move(BCH[0], stage)

            for l, p in enumerate(LAYERS):
                e, b = EG[l], 0 if p["t"] == "A" else 1
                R, vc = (RA, SRCC) if b == 0 else (RB, DSTC)
                nacc = NB * (96 + 3 * p["vb"])
                if l == 0:
                    eng.wait_ge(s_bk, NKEYS)
                    eng.wait_ge(s_px, 16)
                else:
                    if l <= 2:
                        move(BCH[l], stageM)
                    eng.wait_ge(s_at, NB * l)
                if l == 2:
                    for u in (0, 2):
                        eng.wait_ge(s_bs[u], 16 * SBU[u] * NT0 * 2)
                    eng.sem_inc(s_tab, 1)
                eng.memset(ACC[:, 0:nacc], 0.0).then_inc(s_az, 1)
                eng.wait_ge(s_bk, NKEYS)
                n = eng.value_load(NI[b][0:1, 0:1], min_val=NT0 + 1, max_val=NG // 4 - 1)
                m = 32 if l >= 2 else 16
                eng.wait_ge(s_hd[l][0], m * (NB - NB // 2))
                eng.wait_ge(s_hd[l][1], m * (NB // 2))

                def gather(i, u):
                    idx = TT[u][:, 0:G * R].rearrange("p (t f) -> p t f", t=G)
                    eng.wait_ge(e.L[u], i * 16 + 16)
                    eng.wait_ge(e.M, i * 4 + (u + 3))
                    eng.sem_inc(s_go, 1)
                    for t in range(G):
                        eng.indirect_dma_start(
                            out=GB[u % 2][:, t, :], out_offset=None, in_=HT[:, :],
                            in_offset=bass.IndirectOffsetOnAxis(ap=idx[:, t, vc:vc + 1].bitcast(I32), axis=0))\
                           .then_inc(e.G[u % 2], 16)

                def scatter(i, u):
                    r = SBU[u]
                    st = SL[u][:, 0:r * RB].rearrange("p (c f) -> p c f", f=RB)
                    eng.wait_ge(s_bl[u], i * 32 + (32 * NT0 * l + 32))
                    eng.sem_inc(s_go, 1)
                    place(TB, lambda q: st[:, q, POSC:POSC + 1].bitcast(I32), st, s_bs[u])

                if l < 2:
                    with eng.Fori(0, NT0) as i:
                        for u in range(4):
                            gather(i, u)
                            if SBU[u]:
                                scatter(i, u)
                with eng.Fori(NT0 if l < 2 else 0, n) as i:
                    for u in range(4):
                        gather(i, u)

        @block.tensor
        def _(eng):
            eng.wait_ge(s_gm, 2)
            eng.wait_ge(s_g, 11)
            eng.wait_ge(s_gm, 4)
            for b in range(NKEYS):
                eng.wait_ge(s_cn, b + 1)
                eng.matmul(psO[0][:, 0:NB], LT, CNT, start=True, stop=True)
                eng.matmul(psO[1][:, 0:NB], ONE, CNT, start=True, stop=True)
                if b == 0:
                    eng.matmul(psO[1][:, 72:73], ONE, CF, start=True, stop=True)
                eng.matmul(psO[1][0:NB, 64:65], CNT, ONE[:, 0:1], start=True, stop=True).then_inc(s_cp, 1)
                eng.wait_ge(s_gc, b + 1)
                eng.matmul(psC[1][0:NB, 0:1], LT[0:NB, 0:NB], GRP, start=True, stop=True)
                eng.matmul(psC[1][:, 1:2], ONE[0:NB, :], GRP, start=True, stop=True).then_inc(s_gi, 1)
                eng.wait_ge(s_gd, b + 1)
                eng.matmul(psC[0][:, 0:256], ONE[0:NB, :], CMP, start=True, stop=True)
                eng.matmul(psC[0][:, 256:512], DDB, CMP, start=True, stop=True).then_inc(s_gq, 1)
            eng.wait_ge(s_w, 16 * len(loads))
            for i in range(4):
                m = eng.transpose(psN[0][0:96, i * 96:(i + 1) * 96], RW[i], ident[0:96, 0:96])
            m.then_inc(s_rt, 1)
            eng.wait_ge(s_rc, 1)
            for a in range(2):
                eng.matmul(psN[1][0:96, a * 96:a * 96 + 64], RWT[a], RW3s, start=True, stop=True)
                m = eng.matmul(psN[1][0:96, a * 96 + 64:a * 96 + 96], RWT[2 + a], RW3v, start=True, stop=True)
            m.then_inc(s_rp, 1)

            def phase(lo, ln):
                def tnode(j):
                    base = ln * NB
                    if ln == 1:
                        eng.wait_ge(s_hz, j + 1)
                    else:
                        eng.wait_ge(s_h, base + j + 1)
                    if base + j >= 2:
                        eng.wait_ge(s_ht, base + j - 1)
                    o, i_ = nT[j % 2], ident[0:BN, 0:BN]
                    if ln == 1:
                        eng.transpose(o[:, 0:BN], hz[j % 2][:, 0:128], i_)
                        eng.transpose(o[0:96, 128:128 + BN], hz[j % 2][:, 128:224], i_)
                        m = eng.transpose(o[0:96, 256:256 + BN], hz[j % 2][:, 224:320], i_)
                    else:
                        eng.transpose(o[0:64, 0:BN], h[j % 4][:, 0:64], i_)
                        m = eng.transpose(o[0:96, 128:128 + BN], h[j % 4][:, 64:160], i_)
                    m.then_inc(s_tp, 1)

                def mnode(j):
                    base = ln * NB
                    eng.wait_ge(s_ht, base + j + 1)
                    if base + j >= 2:
                        eng.wait_ge(s_ev, base + j - 1)
                    o = nR[j % 2][0:BN, :]
                    t = hT[j % 2]
                    if ln == 2:
                        eng.matmul(o[:, 0:64], t[0:64, 0, 0:BN], WS[2][:, 0:64], start=True, stop=True)
                        eng.matmul(o[:, 160:256], t[0:64, 0, 0:BN], WS[2][:, 64:160], start=True, stop=True)
                        eng.matmul(o[:, 64:160], t[0:96, 1, 0:BN], KV[2][:, 0:96], start=True, stop=True)
                        m = eng.matmul(o[:, 256:352], t[0:96, 1, 0:BN], KV[2][:, 96:192], start=True, stop=True)
                    else:
                        v = o[:, 0:320].rearrange("p (a f) -> p a f", a=2)
                        r = 128 if ln == 1 else 64
                        eng.matmul(v[:, :, 0:64], t[0:r, 0, 0:BN], WS[ln][:, :], start=True, stop=True)
                        if ln == 1:
                            for a in range(2):
                                m = eng.matmul(v[:, :, 64:160], t[0:96, 1 + a, 0:BN], KV[1][:, a, :], start=(a == 0), stop=(a == 1))
                        else:
                            m = eng.matmul(v[:, :, 64:160], t[0:96, 1, 0:BN], KV[ln][:, :], start=True, stop=True)
                    m.then_inc(s_po, 1)

                vb = LAYERS[lo]["vb"] if lo is not None else 0
                nm = 96 + 3 * vb
                acc = ACC[0:BN, 0:NB * nm].rearrange("p (j f) -> p j f", j=NB)

                def tout(j):
                    base = lo * NB
                    if base + j >= 2:
                        eng.wait_ge(s_ac, base + j - 1)
                    eng.transpose(psN[j % 2][0:96, 0:BN], acc[:, j, 0:96], ident[0:BN, 0:BN])
                    for c in range(3):
                        m = eng.transpose(psN[j % 2][0:vb, 128 * (c + 1):128 * (c + 1) + BN],
                                          acc[:, j, 96 + c * vb:96 + (c + 1) * vb], ident[0:BN, 0:BN])
                    m.then_inc(s_at, 1)

                def mout(j):
                    base = lo * NB
                    eng.wait_ge(s_ac, base + j + 1)
                    if lo == 2 and j >= 2:
                        eng.wait_ge(s_o, j - 1)
                    elif base + j >= 2:
                        eng.wait_ge(s_xo, base + j - 1)
                    t = aT[j % 2]
                    if lo == 1:
                        o = psO[j % 2][0:BN, 0:320].rearrange("p (a f) -> p a f", a=2)
                        eng.matmul(o[:, :, 0:64], t[0:96, 0, 0:BN], OS[1][:, :, :], start=True, stop=True)
                        for c in range(3):
                            m = eng.matmul(o[:, :, 64 + c:160:3], t[0:vb, c + 1, 0:BN], OV[1][:, :, :], start=True, stop=True)
                    else:
                        ns = 96 if lo == 2 else 64
                        o = psO[j % 2][0:BN, 0:ns + 96]
                        eng.matmul(o[:, 0:ns], t[0:96, 0, 0:BN], OS[lo][:, :], start=True, stop=True)
                        for c in range(3):
                            m = eng.matmul(o[:, ns + c:ns + 96:3], t[0:vb, c + 1, 0:BN], OV[lo][:, :], start=True, stop=True)
                    m.then_inc(s_oo, 1)

                if lo is not None:
                    tout(0)
                for t in range(NB + (LAG if ln is not None else 0)):
                    n = t - LAG
                    if lo is not None:
                        if t + 1 < NB:
                            tout(t + 1)
                        if t < NB:
                            mout(t)
                    if ln is not None:
                        if 0 <= n + 1 < NB:
                            tnode(n + 1)
                        if n >= 0:
                            mnode(n)

            eng.wait_ge(s_ws, 1)
            eng.wait_ge(s_bk, NKEYS)
            phase(None, 0)
            for l, p in enumerate(LAYERS):
                kf_, hid, wn, vb = p["kf"], p["hid"], p["wn"], p["vb"]
                nm = 96 + 3 * vb
                base = l * NB
                e, b = EG[l], 0 if p["t"] == "A" else 1
                R = RA if b == 0 else RB
                eng.wait_ge(s_xn, base + NB)
                eng.wait_ge(s_ev, base + NB)
                eng.wait_ge(s_bk, NKEYS)
                n = eng.value_load(NI[b][0:1, 0:1], min_val=NT0 + 1, max_val=NG // 4 - 1)

                def edge_t(i, u, d):
                    u2, c = (u + d) % 4, (u + d) // 4
                    ef = TT[u2][:, 0:G * R].rearrange("p (t f) -> p t f", t=G)
                    eng.wait_ge(e.L[u2], i * 16 + (16 * c + 16))
                    if not (isinstance(i, int) and i * 4 + u + d == 0):
                        eng.wait_ge(e.E, i * 4 + (u + d))
                    eng.sem_inc(s_pe, 1)
                    for t in range(G):
                        m = eng.transpose(psT[0:kf_, t * 128:(t + 1) * 128], ef[:, t, p["c0"]:p["c0"] + kf_], ident[:, :])
                    m.then_inc(e.T, 1)

                def edge_f1(i, u, d):
                    q = (u + d) % 2
                    eng.wait_ge(e.E, i * 4 + (u + d + 1))
                    if not (isinstance(i, int) and i * 4 + u + d == 0):
                        eng.wait_ge(e.S, i * 4 + (u + d))
                    eng.sem_inc(s_pe, 1)
                    eng.matmul(psH[0:hid, :], F1[l][:, :], ET[q][0:kf_, :], start=True, stop=True).then_inc(e.F1, 1)

                def edge_f2(i, u, d):
                    q = (u + d) % 2
                    eng.wait_ge(e.S, i * 4 + (u + d + 1))
                    eng.wait_ge(e.M, i * 4 + (u + d + 3))
                    for t in range(G):
                        m = eng.matmul(psW[q][:, t, 0:wn], HH[q][0:hid, t * 128:(t + 1) * 128], F2[l][:, :],
                                       start=True, stop=True)
                    m.then_inc(e.F2, 1)

                def edge_a(i, u):
                    q = u % 2
                    ms = MS[q][:, 0:G * nm].rearrange("p (t f) -> p t f", t=G)
                    eng.wait_ge(e.M, i * 4 + (u + 5))
                    if l == 2:
                        eng.wait_ge(e.N, i * 4 + (u + 5))
                    eng.wait_ge(e.V, i * 4 + (u + 1))
                    for t in range(G):
                        m = eng.matmul(psA[q][0:BN, 0:nm], OH[q][:, t, :], ms[:, t, :], start=(t == 0), stop=(t == G - 1))
                    m.then_inc(e.A, 1)

                edge_t(0, 0, 0)
                edge_t(0, 0, 1)
                edge_t(0, 0, 2)
                edge_f1(0, 0, 0)
                edge_f1(0, 0, 1)
                edge_f2(0, 0, 0)
                eng.wait_ge(s_az, l + 1)
                eng.matmul(psA[1][0:BN, 0:nm], ACC[0:1, 0:BN], ACC[0:1, 0:nm], start=True, stop=True).then_inc(e.A, 1)
                with eng.Fori(0, n) as i:
                    for u in range(4):
                        edge_f2(i, u, 1)
                        edge_f1(i, u, 2)
                        edge_a(i, u)
                        edge_t(i, u, 3)
                eng.wait_ge(e.T, n * 4 + 3)
                eng.wait_ge(e.F1, n * 4 + 2)
                eng.wait_ge(e.F2, n * 4 + 1)
                eng.wait_ge(e.E, n * 4 + (2 if l == 2 else 3))
                eng.wait_ge(e.S, n * 4 + 2)
                eng.wait_ge(s_le, l + 1)

                phase(l, l + 1 if l < 3 else None)

        @block.scalar
        def _(eng):
            own = 0
            eng.wait_ge(s_sq, 1)
            eng.activation(bq, bq, ACT.Sqrt, scale=1.0 / 3.0).then_inc(s_sqd, 1)
            def phase(lo, ln):
                def root(k):
                    eng.wait_ge(s_ve, ln * NBK + k + 1)
                    sl = slice(k * BLK, min(NB, (k + 1) * BLK))
                    eng.activation(VE[:, sl], VE[:, sl], ACT.Sqrt).then_inc(s_sd, 1)

                def hid_(j):
                    base = ln * NB
                    eng.wait_ge(s_st, ln * NBK + j // BLK + 1)
                    if ln == 1 and j >= 4:
                        eng.wait_ge(s_hz, j - 3)
                    elif j >= 4:
                        eng.wait_ge(s_tp, base + j - 3)
                    elif ln:
                        eng.wait_ge(s_tp, base)
                        if ln == 2:
                            eng.wait_ge(s_hz, NB)
                    eng.activation(h[j % 4], X[:, j, :], ACT.Relu, bias=NM[:, j:j + 1], scale=RS[:, j:j + 1])\
                       .then_inc(s_h, 1)

                def evac(j):
                    base = ln * NB
                    eng.wait_ge(s_po, base + j + 1)
                    if j >= 2:
                        eng.wait_ge(s_hd[ln][j % 2], (32 if ln >= 2 else 16) * (j // 2))
                    if base + j >= 2:
                        eng.wait_ge(s_xn, base + j - 1)
                    w = 352 if ln == 2 else 320
                    eng.activation(EV[j % 2][:, 0:w], nR[j % 2][0:BN, 0:w], ACT.Copy,
                                   scale=Z1[:, j:j + 1] if ln in (0, 3) else 1.0).then_inc(s_ev, 1)

                def store(j):
                    eng.wait_ge(s_ev, ln * NB + j + 1)
                    eng.dma_start(HT[htile(ln, j), :], EV[j % 2][:, 0:160]).then_inc(s_hd[ln][j % 2], 16)
                    if ln >= 2:
                        k = 192 if ln == 2 else 160
                        eng.dma_start(SC[htile(ln, j), 0:k], EV[j % 2][:, 160:160 + k]).then_inc(s_hd[ln][j % 2], 16)

                def acopy(j):
                    base = lo * NB
                    vb = LAYERS[lo]["vb"]
                    eng.wait_ge(s_at, base + j + 1)
                    if base + j >= 2:
                        eng.wait_ge(s_oo, base + j - 1)
                    v = psN[j % 2].rearrange("p (a n) -> p a n", a=4)
                    if vb == 96:
                        m = eng.activation(aT[j % 2][0:96, :, 0:BN], v[0:96, :, 0:BN], ACT.Copy)
                    else:
                        eng.activation(aT[j % 2][0:96, 0, 0:BN], v[0:96, 0, 0:BN], ACT.Copy)
                        m = eng.activation(aT[j % 2][0:vb, 1:4, 0:BN], v[0:vb, 1:4, 0:BN], ACT.Copy)
                    m.then_inc(s_ac, 1)

                def gate(j):
                    eng.wait_ge(s_o, j + 1)
                    if j >= 2:
                        eng.wait_ge(s_xo, 2 * NB + j - 1)
                    eng.activation(SG[j % 2], OO[j % 2][:, 0:96], ACT.Sigmoid).then_inc(s_sg, 1)

                if lo == 3:
                    eng.wait_ge(s_an, 1)
                    eng.activation(SN[:, :], SN[:, :], ACT.Sin).then_inc(s_sn, 1)
                    eng.activation(CS[:, :], CS[:, :], ACT.Sin).then_inc(s_sn, 1)
                for t in range(NB + (LAG + 1 if ln is not None else 0)):
                    n = t - LAG
                    if lo is not None and t < NB:
                        acopy(t)
                    if lo == 2 and 1 <= t <= NB:
                        gate(t - 1)
                    if ln is not None:
                        k = ended(lo, t - 1)
                        if k is not None:
                            root(k)
                        if 0 <= n + 3 < NB:
                            hid_(n + 3)
                        if n >= 1:
                            evac(n - 1)
                        if n >= 2:
                            store(n - 2)
                if ln is not None:
                    store(NB - 1)

            phase(None, 0)
            for l, p in enumerate(LAYERS):
                kf_, hid, vb = p["kf"], p["hid"], p["vb"]
                base = l * NB
                e, b = EG[l], 0 if p["t"] == "A" else 1
                eng.wait_ge(s_bk, NKEYS)
                n = eng.value_load(NI[b][0:1, 0:1], min_val=NT0 + 1, max_val=NG // 4 - 1)

                def edge_e(i, u, d):
                    eng.wait_ge(e.T, i * 4 + (u + d + 1))
                    if not (isinstance(i, int) and i * 4 + u + d < 2):
                        eng.wait_ge(e.F1, i * 4 + (u + d - 1))
                    eng.activation(ET[(u + d) % 2][0:kf_, :], psT[0:kf_, :], ACT.Copy).then_inc(e.E, 1)

                def edge_s(i, u, d):
                    eng.wait_ge(e.F1, i * 4 + (u + d + 1))
                    if not (isinstance(i, int) and i * 4 + u + d < 2):
                        eng.wait_ge(e.F2, i * 4 + (u + d - 1))
                    eng.activation(HH[(u + d) % 2][0:hid, :], psH[0:hid, :], p["fn"], scale=p["scale"]).then_inc(e.S, 1)

                if l == 2:
                    eng.sem_inc(e.N, 4)
                edge_e(0, 0, 0)
                edge_e(0, 0, 1)
                if l != 2:
                    edge_e(0, 0, 2)
                edge_s(0, 0, 0)
                edge_s(0, 0, 1)
                def edge_n(i, u):
                    q = u % 2
                    tb = TT[u][:, 0:G * RB].rearrange("p (t f) -> p t f", t=G)
                    m4 = MS[q][:, 0:G * 480].rearrange("p (t f) -> p t f", t=G)
                    eng.wait_ge(e.D, i * (4 * ND2) + (u * ND2 + KT2))
                    for t in range(G):
                        for c in range(3):
                            m = eng.activation(m4[:, t, 96 + 128 * c:160 + 128 * c], tt_[q][:, t, :], ACT.Copy,
                                               scale=tb[:, t, SHC + c:SHC + c + 1])
                    m.then_inc(e.N, 1)

                with eng.Fori(0, n) as i:
                    for u in range(4):
                        if l == 2:
                            edge_n(i, u)
                            edge_e(i, u, 2)
                            edge_s(i, u, 2)
                        else:
                            edge_s(i, u, 2)
                            edge_e(i, u, 3)
                eng.wait_ge(s_le, l + 1)

                phase(l, l + 1 if l < 3 else None)

        @block.vector
        def _(eng):
            own = 0

            def v(ins):
                nonlocal own
                own += 1
                ins.then_inc(s_d, 1)
                return own

            def w_(k=None):
                eng.wait_ge(s_d, own if k is None else k)

            eng.wait_ge(s_key, 32)
            eng.wait_ge(s_nx, 16)
            v(eng.memset(z16, 0.0))

            def rank(ps, b, sm):
                k = 0
                v_ = 0
                for q in range(NB):
                    t = (cum, kf)[q % 2]
                    eng.tensor_tensor_scan(t, masks[:, q, :], z16, OFF[:, q:q + 1], ALU.add, ALU.add).then_inc(sm, 1)
                    v_ += 1
                    eng.wait_ge(sm, v_)
                    eng.copy_predicated(pos, masks[:, q, :].bitcast(U16), t).then_inc(sm, 1)
                    v_ += 1
                eng.wait_ge(sm, v_)
                eng.tensor_copy(ps, pos).then_inc(s_pos, 1)

            for b, key in enumerate((keyA, keyB)):
                v(eng.tensor_scalar(kf, key, 1.0, None, ALU.add))
                w_()
                if b == 0:
                    v(eng.scalar_tensor_tensor(out=cum, in0=nxt, scalar=1.0, in1=kf, op0=ALU.add, op1=ALU.is_lt,
                                               accum_out=CF))
                v(eng.tensor_scalar(bq, kf, float(-(BN + 1) // 2), 1.0 / BN, ALU.add, ALU.mult))
                w_()
                v(eng.tensor_scalar(bq, bq, MAGIC, -MAGIC, ALU.add, ALU.add))
                w_()
                v(eng.tensor_copy(bb, bq))
                w_()
                for q in range(NB):
                    m = eng.tensor_scalar(masks[:, q, :], bb, float(q), None, ALU.is_equal, ALU.add,
                                          accum_out=CNT[:, q:q + 1])
                m.then_inc(s_cn, 1)
                v(eng.memset(pos, 0.0))
                eng.wait_ge(s_cn, b + 1)
                w_()
                eng.wait_ge(s_cp, b + 1)
                if b == 0:
                    eng.tensor_copy(FLG[:, :], psO[1][0:1, 72:73]).then_inc(s_fl, 1)
                v(eng.tensor_scalar(GRP, psO[1][0:NB, 64:65], GE / 2 - 0.5, 1.0 / GE, ALU.add, ALU.mult))
                w_()
                eng.tensor_scalar(GRP, GRP, MAGIC, -MAGIC, ALU.add, ALU.add).then_inc(s_gc, 1)
                v(eng.tensor_tensor_scan(INC, psO[1][:, 0:NB], pos[:, 0:NB], 0.0, ALU.add, ALU.add))
                w_()
                v(eng.tensor_tensor(OFF, INC, psO[1][:, 0:NB], ALU.subtract))
                w_()
                v(eng.scalar_tensor_tensor(out=OFF, in0=OFF, scalar=-1.0, in1=psO[0][:, 0:NB], op0=ALU.add, op1=ALU.add))
                eng.wait_ge(s_gm, 4)
                eng.wait_ge(s_gi, b + 1)
                v(eng.tensor_tensor(ICC, psC[1][0:NB, 0:1], GRP, ALU.add))
                v(eng.scalar_tensor_tensor(out=DD, in0=GRP, scalar=-float(GE), in1=psO[1][0:NB, 64:65], op0=ALU.mult,
                                           op1=ALU.add))
                v(eng.tensor_scalar(NGF, psC[1][0:1, 1:2], 1.5, 0.25, ALU.add, ALU.mult))
                w_()
                v(eng.tensor_scalar(CMP, GI[0:NB, :], ICC, None, ALU.is_ge))
                v(eng.tensor_copy(DDB, DD.to_broadcast([NB, 128])))
                v(eng.tensor_scalar(NIF[:, :], NGF, MAGIC, -MAGIC, ALU.add, ALU.add))
                w_()
                eng.tensor_scalar(NI[b][:, :], NIF[:, :], float(NT0 + 1), None, ALU.max).then_inc(s_gd, 1)
                eng.wait_ge(s_gd, b + 1)
                eng.wait_ge(s_gq, b + 1)
                v(eng.scalar_tensor_tensor(out=BASF, in0=GI, scalar=float(GE), in1=psC[0][:, 256:512], op0=ALU.mult,
                                           op1=ALU.add))
                v(eng.tensor_scalar(BKO[b][:, :], psC[0][:, 0:256], float(NB - 1), float(BN), ALU.min, ALU.mult))
                v(eng.tensor_scalar(TI[b][0:1, :], psC[0][0:1, 0:256], float(NB - 1), None, ALU.min))
                w_()
                eng.tensor_scalar(TI[b][32:33, :], BASF[32:33, :], 0.0, float(EPAD), ALU.max, ALU.min).then_inc(s_bk, 1)
                eng.wait_ge(s_bk, b + 1)
                if b == 0:
                    flag = eng.value_load(FLG[0:1, 0:1], min_val=0, max_val=EPAD)
                    with eng.If_ne(flag.val, 0):
                        rank(posA, 0, s_rk)
                        eng.wait_ge(s_pos, 1)
                    pass
                else:
                    for q in range(NB):
                        t = (cum, kf)[q % 2]
                        v(eng.tensor_tensor_scan(t, masks[:, q, :], z16, OFF[:, q:q + 1], ALU.add, ALU.add))
                        w_()
                        v(eng.copy_predicated(pos, masks[:, q, :].bitcast(U16), t))
                    w_()
                    v(eng.tensor_copy(PX[:, :, POSC - 64].bitcast(I32), pos))
                    w_()

            eng.wait_ge(s_sh, 16)
            v(eng.tensor_tensor(kf, sh[:, :, 0], sh[:, :, 0], ALU.mult))
            v(eng.tensor_tensor(cum, sh[:, :, 1], sh[:, :, 1], ALU.mult))
            v(eng.tensor_tensor(rec, sh[:, :, 2], sh[:, :, 2], ALU.mult))
            w_()
            v(eng.tensor_tensor(kf, kf, cum, ALU.add))
            w_()
            eng.tensor_tensor(bq, kf, rec, ALU.add).then_inc(s_sq, 1)
            eng.wait_ge(s_sqd, 1)
            v(eng.reciprocal(rec, bq))
            w_()
            v(eng.tensor_copy(PX[:, :, DSTC - 64].bitcast(I32), keyA))
            v(eng.tensor_scalar(PX[:, :, LOCB - 64], keyB, 1.0, None, ALU.add))
            v(eng.tensor_tensor(PX[:, :, 0:3], sh, rec.unsqueeze(2).to_broadcast([128, EC, 3]), ALU.mult))
            v(eng.tensor_tensor(PX[:, :, 3:5], sh[:, :, 0:2], rec.unsqueeze(2).to_broadcast([128, EC, 2]), ALU.mult))
            w_()
            eng.sem_inc(s_tb, 1)

            eng.wait_ge(s_w, 16 * len(loads))
            eng.wait_ge(s_g, 12)
            r32 = float(1 / np.sqrt(32.0))
            r96 = float(1 / np.sqrt(96.0))

            def mul(t, c):
                v(eng.tensor_scalar(t, t, float(c), None, ALU.mult))

            mul(WS[0][:, 0:64], 1 / 8)
            mul(WS[0][:, 64:128], C_S / 8)
            mul(KV[0][:, 0:96], r32)
            mul(KV[0][:, 96:192], C_S * r32)
            mul(WS[1][:, 64:128], C_S)
            mul(KV[1][:, :, 96:192], C_S)
            mul(WS[3][:, :], 1 / 8)
            mul(KV[3][:, :], r32)
            c = C_X * r96 / np.sqrt(8.0) / 10
            v(eng.tensor_scalar(OS[0][:, :], OS[0][:, :], RSC[0:96, 0:1], float(c), ALU.mult, ALU.mult))
            mul(OV[0][:, :], c)
            v(eng.tensor_scalar(OS[2][:, :], OS[2][:, :], RSC[0:96, 0:1], 1 / 32, ALU.mult, ALU.mult))
            v(eng.tensor_scalar(OV[2][:, :], OV[2][:, :], RSC[:, 1:2], 1 / 32, ALU.mult, ALU.mult))
            c = r96 / 4 / 8
            v(eng.tensor_scalar(OS[3][:, :], OS[3][:, :], RSC[0:96, 0:1], float(c), ALU.mult, ALU.mult))
            mul(OV[3][:, :], c)
            mul(L3W[:, 0:64], 0.1 * c)
            mul(L3W[:, 64:96], 0.1 * c / R3)
            eng.wait_ge(s_rt, 1)
            eng.tensor_copy(NP[0:96, 2368:2752], psN[0][0:96, 0:384]).then_inc(s_rc, 1)
            eng.wait_ge(s_rp, 1)
            for a in range(2):
                v(eng.tensor_scalar(OS[1][:, a, :], psN[1][0:96, a * 96:a * 96 + 64], RSC[0:96, 0:1], C_X / 4, ALU.mult, ALU.mult))
                v(eng.tensor_scalar(OV[1][:, a, :], psN[1][0:96, a * 96 + 64:a * 96 + 96], C_X / 4, None, ALU.mult))
            eng.wait_ge(s_x, 64)
            v(eng.tensor_tensor(SA[:, :], Z1, Z3[:, :], ALU.mult))
            v(eng.tensor_tensor(SCC[:, :], Z2, Z3[:, :], ALU.mult))
            w_()
            eng.sem_inc(s_ws, 1)

            def phase(lo, ln):
                vb = LAYERS[lo]["vb"] if lo is not None else 0
                nm = 96 + 3 * vb
                acc = ACC[0:BN, 0:NB * nm].rearrange("p (j f) -> p j f", j=NB)

                def stats(k):
                    js = range(k * BLK, min(NB, (k + 1) * BLK))
                    sl = slice(js[0], js[-1] + 1)
                    if lo is not None:
                        eng.wait_ge(s_xo, lo * NB + js[-1] + 1)
                    for j in js:
                        v(eng.bn_stats(STT[:, j, :], X[:, j, :]))
                    w_()
                    for j in js:
                        v(eng.bn_aggr(MV[:, j, :], STT[:, j, :]))
                    w_()
                    eng.tensor_scalar(VE[:, sl], MV[:, sl, 1], 1e-5, None, ALU.add).then_inc(s_ve, 1)

                def norm(k):
                    sl = slice(k * BLK, min(NB, (k + 1) * BLK))
                    eng.wait_ge(s_sd, ln * NBK + k + 1)
                    v(eng.reciprocal(RS[:, sl], VE[:, sl]))
                    w_()
                    eng.scalar_tensor_tensor(out=NM[:, sl], in0=MV[:, sl, 0], scalar=-1.0, in1=RS[:, sl],
                                             op0=ALU.mult, op1=ALU.mult).then_inc(s_st, 1)

                def hscale(j):
                    eng.wait_ge(s_h, NB + j + 1)
                    if j >= 2:
                        eng.wait_ge(s_tp, NB + j - 1)
                    for c0, m in ((0, 64), (64, 96)):
                        o = hz[j % 2][:, 2 * c0:2 * c0 + 2 * m].rearrange("p (a f) -> p a f", a=2)
                        x = eng.tensor_tensor(o, h[j % 4][:, c0:c0 + m].unsqueeze(1).to_broadcast([BN, 2, m]),
                                              ZZ[:, :, j:j + 1].to_broadcast([BN, 2, m]), ALU.mult)
                    x.then_inc(s_hz, 1)

                def hcopy(j):
                    base = ln * NB
                    eng.wait_ge(s_tp, base + j + 1)
                    if base + j >= 2:
                        eng.wait_ge(s_po, base + j - 1)
                    t, o = hT[j % 2], nT[j % 2].rearrange("p (a n) -> p a n", a=4)
                    r, a = (128, 3) if ln == 1 else (64, 2)
                    eng.tensor_copy(t[0:r, 0, 0:BN], o[0:r, 0, 0:BN])
                    eng.tensor_copy(t[0:96, 1:a, 0:BN], o[0:96, 1:a, 0:BN]).then_inc(s_ht, 1)

                def xnode(j):
                    eng.wait_ge(s_ev, ln * NB + j + 1)
                    if ln < 2:
                        eng.tensor_tensor(X[:, j, :], X[:, j, :], EV[j % 2][:, 160:320], ALU.add).then_inc(s_xn, 1)
                    else:
                        eng.sem_inc(s_xn, 1)

                if lo == 3:
                    for j in range(NB):
                        t = FP[0][:, 0:96]
                        v(eng.scalar_tensor_tensor(out=t, in0=acc[:, j, 0:96], scalar=1.0, in1=L3W[:, :], op0=ALU.mult,
                                                   op1=ALU.mult, accum_out=ANG[:, j:j + 1]))
                        w_()
                    v(eng.tensor_tensor(ANG[:, :], ANG[:, :], Z1, ALU.mult))
                    w_()
                    for T, ph in ((SN, 0.0), (CS, 0.25)):
                        v(eng.tensor_scalar(KK[:, :], ANG[:, :], float(1 / (2 * np.pi)), ph, ALU.mult, ALU.add))
                        w_()
                        v(eng.tensor_scalar(KK[:, :], KK[:, :], MAGIC, -MAGIC, ALU.add, ALU.add))
                        w_()
                        v(eng.scalar_tensor_tensor(out=T[:, :], in0=KK[:, :], scalar=-6.28125, in1=ANG[:, :],
                                                   op0=ALU.mult, op1=ALU.add))
                        w_()
                        v(eng.scalar_tensor_tensor(out=T[:, :], in0=KK[:, :], scalar=-float(2 * np.pi - 6.28125),
                                                   in1=T[:, :], op0=ALU.mult, op1=ALU.add))
                        w_()
                        if ph:
                            v(eng.tensor_scalar(T[:, :], T[:, :], float(np.pi / 2), None, ALU.add))
                            w_()
                        v(eng.tensor_scalar(T[:, :], T[:, :], float(np.float32(np.pi)) * (1 - 1e-7),
                                            -float(np.float32(np.pi)) * (1 - 1e-7), ALU.min, ALU.max))
                        w_()
                    eng.sem_inc(s_an, 1)
                    eng.wait_ge(s_sn, 2)
                    v(eng.tensor_tensor(SN[:, :], SN[:, :], Z1, ALU.mult))
                    w_()

                def fin2(j):
                    eng.wait_ge(s_sg, j + 1)
                    o, s, f = OO[j % 2], SG[j % 2], FP[j % 2]
                    v(eng.tensor_tensor(f[:, 0:64], o[:, 0:64], s[:, 0:64], ALU.mult))
                    v(eng.tensor_tensor(f[:, 64:160].rearrange("p (w c) -> p w c", c=3),
                                        o[:, 96:192].rearrange("p (w c) -> p w c", c=3),
                                        s[:, 64:96].unsqueeze(2).to_broadcast([BN, 32, 3]), ALU.mult))
                    w_()
                    eng.tensor_tensor(X[:, j, :], X[:, j, :], f, ALU.add).then_inc(s_xo, 1)

                def xout(j):
                    base = lo * NB
                    eng.wait_ge(s_oo, base + j + 1)
                    o = psO[j % 2][0:BN, :]
                    if lo == 0:
                        eng.scalar_tensor_tensor(out=X[:, j, :], in0=o[:, 0:160], scalar=Z1[:, j:j + 1], in1=X[:, j, :],
                                                 op0=ALU.mult, op1=ALU.add).then_inc(s_xo, 1)
                    elif lo == 1:
                        v(eng.scalar_tensor_tensor(out=X[:, j, :], in0=o[:, 0:160], scalar=SA[:, j:j + 1], in1=X[:, j, :],
                                                   op0=ALU.mult, op1=ALU.add))
                        w_()
                        eng.scalar_tensor_tensor(out=X[:, j, :], in0=o[:, 160:320], scalar=SCC[:, j:j + 1], in1=X[:, j, :],
                                                 op0=ALU.mult, op1=ALU.add).then_inc(s_xo, 1)
                    elif lo == 2:
                        eng.wait_ge(s_sk[0][j % 2], 16 * (j // 2 + 1))
                        if j >= 2:
                            eng.wait_ge(s_xo, base + j - 1)
                        eng.tensor_tensor(OO[j % 2], o[:, 0:192], SK[j % 2], ALU.add).then_inc(s_o, 1)
                    else:
                        eng.wait_ge(s_sk[1][j % 2], 16 * (j // 2 + 1))
                        v(eng.scalar_tensor_tensor(out=X[:, j, :], in0=SK[j % 2][:, 0:160], scalar=CS[:, j:j + 1],
                                                   in1=X[:, j, :], op0=ALU.mult, op1=ALU.add))
                        w_()
                        eng.scalar_tensor_tensor(out=X[:, j, :], in0=o[:, 0:160], scalar=SN[:, j:j + 1], in1=X[:, j, :],
                                                 op0=ALU.mult, op1=ALU.add).then_inc(s_xo, 1)

                for t in range(NB + (LAG + 1 if ln is not None else 0)):
                    n = t - LAG
                    if lo is not None and t < NB:
                        xout(t)
                    if lo == 2 and 1 <= t <= NB:
                        fin2(t - 1)
                    if ln is not None:
                        k = ended(lo, t)
                        if k is not None:
                            stats(k)
                        k = ended(lo, t - 2)
                        if k is not None:
                            norm(k)
                        if ln == 1 and 0 <= n + 2 < NB:
                            hscale(n + 2)
                        if 0 <= n + 1 < NB:
                            hcopy(n + 1)
                        if n >= 1:
                            xnode(n - 1)
                if lo == 2 and ln is None:
                    fin2(NB - 1)
                if lo is not None:
                    eng.wait_ge(s_xo, (lo + 1) * NB)

            phase(None, 0)
            for l, p in enumerate(LAYERS):
                vb = p["vb"]
                nm = 96 + 3 * vb
                base = l * NB
                e, b = EG[l], 0 if p["t"] == "A" else 1
                R = RA if b == 0 else RB
                yc, lc = (YC, LOCC) if b == 0 else (SHC, LOCB)
                eng.wait_ge(s_az, l + 1)
                eng.wait_ge(s_bk, NKEYS)
                n = eng.value_load(NI[b][0:1, 0:1], min_val=NT0 + 1, max_val=NG // 4 - 1)
                acc = ACC[0:BN, 0:NB * nm].rearrange("p (j f) -> p j f", j=NB)
                eng.sem_inc(e.M, 4)
                eng.sem_inc(e.V, 1)
                eng.sem_inc(e.A, 1)
                ND = 10 if l != 2 else ND2

                def bucket(i, u):
                    return eng.value_load(TI[b][0:1, bass.ds(i * 4 + u, 1)], min_val=0, max_val=NB - 1)

                def add(i, u, q, j):
                    eng.wait_ge(e.A, i * 4 + (u + 2))
                    eng.tensor_tensor(acc[:, bass.ds(j, 1), :], acc[:, bass.ds(j, 1), :],
                                      psA[q][0:BN, 0:nm].unsqueeze(1), ALU.add).then_inc(e.V, 1)

                with eng.Fori(0, n) as i:
                    for u in range(4):
                        q = u % 2
                        tb = TT[u][:, 0:G * R].rearrange("p (t f) -> p t f", t=G)
                        m4 = MS[q][:, 0:G * nm].rearrange("p (t f) -> p t f", t=G)
                        mv = m4[:, :, 96:nm].rearrange("p t (c f) -> p t c f", c=3)
                        e0 = GB[q][:, :, 0:64]
                        e1 = GB[q][:, :, 64:160].rearrange("p t (c f) -> p t c f", c=3)
                        W = psW[q]
                        done = 0

                        def op(ins):
                            nonlocal done
                            ins.then_inc(e.D, 1)
                            done += 1
                            return done

                        def need(k):
                            eng.wait_ge(e.D, i * (4 * ND) + (u * ND + k))

                        y1 = tb[:, :, yc + 1:yc + 4] if l != 2 else tb[:, :, yc:yc + 3]
                        y1b = y1.unsqueeze(3)
                        eng.wait_ge(e.L[u], i * 16 + 16)
                        eng.wait_ge(e.A, i * 4 + (u + 1))
                        op(eng.scalar_tensor_tensor(out=OH[q], in0=iota1[:, :].unsqueeze(1).to_broadcast([128, G, BN]),
                                                    scalar=BKO[b][:, bass.ds(i * 4 + (u + 1), 1)],
                                                    in1=tb[:, :, lc:lc + 1].to_broadcast([128, G, BN]),
                                                    op0=ALU.add, op1=ALU.is_equal))
                        eng.wait_ge(e.G[q], i * 128 + (u // 2 * 64 + 64))
                        if l != 2:
                            y0 = tb[:, :, yc:yc + 1]
                            need(1)
                            kp = op(eng.tensor_tensor(tp[q], e1, y1b.to_broadcast([128, G, 3, 32]), ALU.mult))
                            ky = op(eng.tensor_tensor(ty[q], e0, y0.to_broadcast([128, G, 64]), ALU.mult))
                            eng.wait_ge(e.F2, i * 4 + (u + 1))
                            kt = op(eng.tensor_tensor(tt_[q], W[:, :, 64:128], e0, ALU.mult))
                            ku = op(eng.tensor_tensor(tu[q], W[:, :, 128:160], y0.to_broadcast([128, G, 32]), ALU.mult))
                            j = bucket(i, u)
                            need(kp)
                            kq = op(eng.tensor_tensor(tq[q], tp[q][:, :, 0, :], tp[q][:, :, 1, :], ALU.add))
                            need(ky)
                            op(eng.tensor_tensor(m4[:, :, 0:64], W[:, :, 0:64], ty[q], ALU.mult))
                            need(kq)
                            kr = op(eng.tensor_tensor(tq[q], tq[q], tp[q][:, :, 2, :], ALU.add))
                            need(kt)
                            op(eng.tensor_tensor(mv[:, :, :, 0:64], tt_[q].unsqueeze(2).to_broadcast([128, G, 3, 64]),
                                                 y1b.to_broadcast([128, G, 3, 64]), ALU.mult))
                            need(kr)
                            op(eng.tensor_tensor(m4[:, :, 64:96], W[:, :, 160:192], tq[q], ALU.mult))
                            need(ku)
                            op(eng.engine_nop()) if False else None
                            eng.tensor_tensor(mv[:, :, :, 64:96], tu[q].unsqueeze(2).to_broadcast([128, G, 3, 32]),
                                              e1, ALU.mult).then_inc(e.M, 1)
                        else:
                            need(1)
                            kp = op(eng.tensor_tensor(tp[q], e1, y1b.to_broadcast([128, G, 3, 32]), ALU.mult))
                            eng.wait_ge(e.F2, i * 4 + (u + 1))
                            eng.wait_ge(e.N, i * 4 + (u + 4))
                            kt = op(eng.tensor_tensor(tt_[q], W[:, :, 64:128], e0, ALU.mult))
                            assert kt == KT2
                            kw = op(eng.tensor_tensor(tw[:, :, 0:3, :], e1,
                                                      W[:, :, 192:224].unsqueeze(2).to_broadcast([128, G, 3, 32]), ALU.mult))
                            op(eng.tensor_tensor(m4[:, :, 0:64], W[:, :, 0:64], e0, ALU.mult))
                            j = bucket(i, u)
                            need(kp)
                            kq = op(eng.tensor_tensor(tq[q], tp[q][:, :, 0, :], tp[q][:, :, 1, :], ALU.add))
                            need(kw)
                            kx = op(eng.tensor_copy(tw[:, :, 3:5, :], tw[:, :, 0:2, :]))
                            need(kq)
                            kr = op(eng.tensor_tensor(tq[q], tq[q], tp[q][:, :, 2, :], ALU.add))
                            need(kx)
                            k1 = op(eng.tensor_tensor(mv[:, :, :, 96:128], tw[:, :, 1:4, :],
                                                      tb[:, :, yc + 2:yc + 5].unsqueeze(3).to_broadcast([128, G, 3, 32]),
                                                      ALU.mult))
                            k2 = op(eng.tensor_tensor(tx, tw[:, :, 2:5, :],
                                                      tb[:, :, yc + 1:yc + 4].unsqueeze(3).to_broadcast([128, G, 3, 32]),
                                                      ALU.mult))
                            need(kr)
                            op(eng.tensor_tensor(m4[:, :, 64:96], W[:, :, 160:192], tq[q], ALU.mult))
                            op(eng.tensor_tensor(mv[:, :, :, 64:96], e1,
                                                 W[:, :, 128:160].unsqueeze(2).to_broadcast([128, G, 3, 32]), ALU.mult))
                            need(k2)
                            op(eng.tensor_tensor(mv[:, :, :, 96:128], mv[:, :, :, 96:128], tx, ALU.subtract))
                            need(done)
                            eng.sem_inc(e.M, 1)
                        assert done == ND, done
                        add(i, u, 1 - q, j)
                j = eng.value_load(TI[b][0:1, bass.ds(n * 4, 1)], min_val=0, max_val=NB - 1)
                eng.wait_ge(e.A, n * 4 + 2)
                eng.wait_ge(e.V, n * 4 + 1)
                eng.wait_ge(e.F1, n * 4 + 2)
                eng.wait_ge(e.F2, n * 4 + 1)
                if l < 2:
                    for u in (0, 2):
                        eng.wait_ge(s_bs[u], 16 * SBU[u] * NT0 * (l + 1))
                eng.tensor_tensor(acc[:, bass.ds(j, 1), :], acc[:, bass.ds(j, 1), :],
                                  psA[1][0:BN, 0:nm].unsqueeze(1), ALU.add).then_inc(s_le, 1)
                eng.wait_ge(s_le, l + 1)

                phase(l, l + 1 if l < 3 else None)


def kernel(**inputs):
    import numpy as _np
    import concourse.bacc as _bacc
    from concourse import mybir as _mybir
    from concourse.bass_utils import run_bass_kernel_spmd as _run

    a = {k: _np.ascontiguousarray(v) for k, v in inputs.items()}

    def rows(t, n):
        return _np.concatenate([t, _np.zeros((n - t.shape[0],) + t.shape[1:], t.dtype)])

    def key(t):
        return _np.concatenate([t, _np.full((EPAD - E,), NOKEY, t.dtype)])

    host = dict(a)
    host["x"] = rows(a["x"], NPAD)
    host["keya"], host["keyb"] = key(a["dst"]), key(a["src"])
    host["keyn"] = _np.concatenate([host["keya"][1:], host["keya"][-1:]])
    ea = _np.concatenate([a["edge_attr_12"], a["edge_attr_10"], a["edge_attr_8"], a["edge_attr_4"],
                          _np.zeros((E, 2), a["x"].dtype)], axis=1)
    host["ea"] = rows(ea, EPAD)
    host["eb"] = rows(a["edge_attr_64"], EPAD)
    host["e3"] = _np.concatenate([a["edge_attr_3"], _np.ones((EPAD - E, 3), a["x"].dtype)])
    for n, s in (("z1", "node_vec1"), ("z2", "node_vec1_n2"), ("z3", "node_vec1_n3")):
        host[n] = _np.ascontiguousarray(rows(a[s], NPAD).reshape(NB, BN).T)
    nc = _bacc.Bacc("TRN2", target_bir_lowering=False, num_devices=1)
    arrays, args = {}, {}
    for name in _INS:
        t = host[name]
        arrays[f"in_{name}"] = t
        args[name] = nc.dram_tensor(f"in_{name}", t.shape, _mybir.dt.from_np(t.dtype), kind="ExternalInput").ap()
    o = nc.dram_tensor("out_0", (N, D), _mybir.dt.float32, kind="ExternalOutput").ap()
    program(nc, args, o)
    r = _run(nc, [arrays], core_ids=[0])
    return r.results[0]["out_0"]
```

```python
from contextlib import ExitStack

import numpy as np

import concourse.bass as bass
from concourse import mybir

F32 = mybir.dt.float32
I32 = mybir.dt.int32
BF16 = mybir.dt.bfloat16
U16 = mybir.dt.uint16
ALU = mybir.AluOpType
ACT = mybir.ActivationFunctionType

N = 6250
E = 100000
D = 160
BN = 123
NB = 51
NPAD = BN * NB
LAST = N - (NB - 1) * BN
EC = 782
EPAD = 128 * EC
NOKEY = NPAD - 1
G = 4
GE = 128 * G
NG = 252
ROWS = EPAD + GE
RA, RB = 36, 72
CHA, CHB = 34, 16
NCHA = EC // CHA
SB0, SB1 = 102, 144
SBU = (2, 0, 2, 0)
NT0 = 49
SLOOP = NT0 * sum(SBU)
assert SB0 + 2 * SLOOP + 2 * SB1 == EC and EC % CHA == 0
BLK, LAG = 4, 10
ND, KT = 13, 3
NBK = -(-NB // BLK)


def chunks(c0, n):
    return [(c, min(CHB, c0 + n - c)) for c in range(c0, c0 + n, CHB)]


BCH = [chunks(0, SB0), chunks(SB0 + SLOOP, SB1), chunks(SB0 + 2 * SLOOP + SB1, SB1)]
BL0 = [SB0, SB0 + SLOOP + SB1]

MAGIC = 12582912.0
C_S, C_X = float(np.sin(np.pi / 8)), float(np.cos(np.pi / 8))
R3 = float(np.sqrt(3.0))

LAYERS = [
    dict(t="A", kf=12, c0=0, hid=100, wn=192, vb=96, ch=128, nch=3, scale=float(1 / np.sqrt(12.0)), fn=ACT.Silu),
    dict(t="A", kf=10, c0=12, hid=100, wn=192, vb=96, ch=128, nch=3, scale=1.0, fn=ACT.Silu),
    dict(t="B", kf=64, c0=0, hid=64, wn=224, vb=128, ch=120, nch=4, scale=1.0, fn=ACT.Relu),
    dict(t="A", kf=8, c0=22, hid=64, wn=192, vb=96, ch=128, nch=3, scale=float(1 / np.sqrt(8.0)), fn=ACT.Silu),
]
YC, SRCC, LOCC = 30, 34, 35
SHC, DSTC, LOCB, POSC = 64, 69, 70, 71

_INS = [
    "x", "keya", "keyb", "keyn", "ea", "eb", "e3", "z1", "z2", "z3",
    "L0_gnn_W_sc0", "L0_gnn_W_sc1", "L0_gnn_W_l1_0", "L0_gnn_W_l1_1", "L0_gnn_W_fc1", "L0_gnn_W_fc2",
    "L0_gnn_W_l2_0", "L0_gnn_W_l2_1", "L1_gnn_Ws_sc_a", "L1_gnn_Wv_sc_a", "L1_gnn_Ws_sc_c", "L1_gnn_Wv_sc_c",
    "L1_gnn_Ws_l1_a", "L1_gnn_Wv_l1_a", "L1_gnn_Ws_l1_c", "L1_gnn_Wv_l1_c", "L1_gnn_W_fc1", "L1_gnn_W_fc2",
    "L1_gnn_Ws_l2_a", "L1_gnn_Wv_l2_a", "L1_gnn_Ws_l2_c", "L1_gnn_Wv_l2_c", "L1_gnn_Ws_l3", "L1_gnn_Wv_l3",
    "L2_gnn_W_skip0", "L2_gnn_W_skip1", "L2_gnn_W_nl0", "L2_gnn_W_nl1", "L2_gnn_W_fc1", "L2_gnn_W_fc2",
    "L2_gnn_W_out_s", "L2_gnn_W_out_v", "L3_gnn_sc_w0", "L3_gnn_sc_w1", "L3_gnn_lin1_w0", "L3_gnn_lin1_w1",
    "L3_gnn_fc_w1", "L3_gnn_fc_w2", "L3_gnn_lin2_w0", "L3_gnn_lin2_w1", "L3_gnn_lin3_w",
]


def program(nc, A, out):
    ctx = ExitStack()
    with ctx:
        def sb(name, shape, dt=F32):
            return ctx.enter_context(nc.sbuf_tensor(name, shape, dt))

        def sem(name):
            return ctx.enter_context(nc.semaphore(name))

        TA = nc.dram_tensor("TA", (ROWS, RA), F32).ap()
        TB = nc.dram_tensor("TB", (ROWS, RB), F32).ap()
        PB = nc.dram_tensor("PB", (EPAD, RB - 64), F32).ap()
        HT = nc.dram_tensor("HT", (NPAD, D), F32).ap()
        SC = nc.dram_tensor("SC", (NPAD, 192), F32).ap()

        X = sb("X", [BN, NB, D])
        ACC = sb("ACC", [128, NB * 4 * BN])
        WK = sb("WK", [128, 11736])
        NP = WK[:, 8704:11736]
        PS = ctx.enter_context(nc.psum_tensor("PS", [128, 4096], F32))

        ident = sb("ident", [128, 128])
        iota1 = sb("iota1", [128, BN])
        ZZ, Z3 = sb("ZZ", [BN, 2, NB]), sb("Z3", [BN, NB])
        Z1, Z2 = ZZ[:, 0, :], ZZ[:, 1, :]
        SA, SCC = sb("SA", [BN, NB]), sb("SCC", [BN, NB])
        STT = sb("STT", [BN, NB, 6])
        MV = sb("MV", [BN, NB, 2])
        VE, RS, NM = sb("VE", [BN, NB]), sb("RS", [BN, NB]), sb("NM", [BN, NB])
        ANG, KK, SN, CS = sb("ANG", [BN, NB]), sb("KK", [BN, NB]), sb("SN", [BN, NB]), sb("CS", [BN, NB])
        TI = [sb("TIA", [64, 256], I32), sb("TIB", [64, 256], I32)]
        BKO = [sb("BKOA", [128, 256]), sb("BKOB", [128, 256])]
        NIF = sb("NIF", [1, 1])
        NI = [sb("NIA", [1, 1], I32), sb("NIB", [1, 1], I32)]
        FLG = sb("FLG", [1, 1], I32)

        WS = [sb("WS0", [64, 128]), sb("WS1", [128, 128]), sb("WS2", [64, 160]), sb("WS3", [64, 128])]
        KV = [sb("KV0", [96, 192]), sb("KV1", [96, 2, 192]), sb("KV2", [96, 192]), sb("KV3", [96, 192])]
        F1 = [sb(f"F1_{l}", [p["kf"], p["hid"]]) for l, p in enumerate(LAYERS)]
        FB = [sb(f"FB{l}", [6 * p["kf"], p["hid"]], BF16) if l != 2 else None for l, p in enumerate(LAYERS)]
        at3 = {0: (24512, 24662), 1: (24762, 24912), 3: (23860, 25012)}
        FP3, FR = {}, {}
        for l, (a3, ar) in at3.items():
            nf, hid = LAYERS[l]["kf"], LAYERS[l]["hid"]
            FP3[l] = [ACC[0:nf, a3 + i * hid // 2:a3 + (i + 1) * hid // 2].bitcast(BF16) for i in range(3)]
            FR[l] = ACC[0:nf, ar:ar + hid]
        identb = sb("identb", [128, 128], BF16)
        F2 = [sb(f"F2_{l}", [p["hid"], p["wn"]]) for l, p in enumerate(LAYERS)]
        OS = [ACC[0:96, 24000 + o:24000 + o + n] for o, n in ((0, 64), (64, 128), (192, 96), (288, 64))]
        OV = [ACC[0:p, 24352 + o:24352 + o + n] for o, n, p in ((0, 32, 96), (32, 64, 96), (96, 32, 128), (128, 32, 96))]
        OS[1], OV[1] = (t.rearrange("p (a n) -> p a n", a=2) for t in (OS[1], OV[1]))
        WO = [sb(f"WO{l}", [p["ch"], p["nch"], (160, 320, 192, 160)[l]]) for l, p in enumerate(LAYERS)]
        L3W = sb("L3W", [96, 1])
        ZERO = sb("ZERO", [128, 1])
        RSC = sb("RSC", [128, 2])

        def wk(a, n, p=128):
            return WK[0:p, a:a + n]

        keyA, keyB = wk(0, EC).bitcast(I32), wk(EC, EC).bitcast(I32)
        nxt = wk(2 * EC, EC).bitcast(I32)
        rec = wk(3 * EC, EC)
        posA = wk(4 * EC, EC).bitcast(I32)
        sh = wk(5 * EC, 3 * EC).rearrange("p (c k) -> p c k", k=3)
        stage = [wk(8 * EC + i * CHA * RA, CHA * RA) for i in range(2)]
        PX = ACC[:, 0:EC * (RB - 64)].rearrange("p (c f) -> p c f", f=RB - 64)
        zero = wk(8 * EC, G * RB)
        masks = ACC[:, 0:NB * 391].bitcast(BF16).rearrange("p (b c) -> p b c", c=EC)
        tb0 = NB * 391
        kf, bq, cum, pos = (ACC[:, tb0 + i * EC:tb0 + (i + 1) * EC] for i in range(4))
        bb = ACC[:, tb0 + 4 * EC:tb0 + 4 * EC + 391].bitcast(BF16)
        z16 = ACC[:, tb0 + 4 * EC + 391:tb0 + 4 * EC + 782].bitcast(BF16)
        LT, ONE = NP[:, 0:128], NP[:, 128:256]
        CNT, INC, OFF = (NP[:, 256 + i * NB:256 + (i + 1) * NB] for i in range(3))
        CF = NP[:, 410:411]
        GI, CMP, BASF = NP[:, 640:896], NP[0:NB, 896:1152], NP[:, 1152:1408]
        GRP, DD, DDB, NGF = NP[0:NB, 411:412], NP[0:NB, 412:413], NP[0:NB, 1408:1536], NP[0:1, 413:414]
        ICC = NP[0:NB, 414:415]

        at = 0

        def take(n, p=128):
            nonlocal at
            v = WK[0:p, at:at + n]
            at += n
            return v

        TT = [take(G * RB) for _ in range(4)]
        GB = [take(G * D).rearrange("p (t f) -> p t f", t=G) for _ in range(2)]
        ET = [take(GE) for _ in range(2)]
        HH = [take(GE) for _ in range(2)]
        OH = [take(G * BN).rearrange("p (t f) -> p t f", t=G) for _ in range(2)]
        MS = [take(G * 480) for _ in range(2)]
        tq = [take(G * 32).rearrange("p (t f) -> p t f", t=G) for _ in range(2)]
        tu = [take(G * 32).rearrange("p (t f) -> p t f", t=G) for _ in range(2)]
        ty = [take(G * 64).rearrange("p (t f) -> p t f", t=G) for _ in range(1)] * 2
        tt_ = [take(G * 64).rearrange("p (t f) -> p t f", t=G) for _ in range(1)] * 2
        tp = [take(G * 96).rearrange("p (t c f) -> p t c f", t=G, c=3) for _ in range(1)] * 2
        tw = take(G * 160).rearrange("p (t c f) -> p t c f", t=G, c=5)
        tx = take(G * 96).rearrange("p (t c f) -> p t c f", t=G, c=3)
        assert at <= 11736, at
        twf = tw.rearrange("p t c f -> p (t c f)")
        XS = [twf[:, i * 144:(i + 1) * 144].bitcast(BF16).rearrange("p (t f) -> p t f", t=G) for i in range(4)]
        XR = twf[:, 576:624].rearrange("p (t f) -> p t f", t=G)
        SL = [tx.rearrange("p t c f -> p (t c f)")[:, u * RB:(u + 2) * RB] for u in range(4)]
        stageM = [WK[:, 5464 + i * CHB * RB:5464 + (i + 1) * CHB * RB] for i in range(2)]

        h = [NP[0:BN, i * 160:(i + 1) * 160] for i in range(4)]
        hT = [NP[:, 640 + i * 384:1024 + i * 384].rearrange("p (a n) -> p a n", a=3) for i in range(2)]
        EV = [NP[0:BN, 1408 + i * 352:1760 + i * 352] for i in range(2)]
        SK = [NP[0:BN, 2112 + i * 192:2304 + i * 192] for i in range(2)]
        OUTB = WK[0:BN, 0:NB * D].rearrange("p (j d) -> p j d", j=NB)
        SB = 10
        SK3 = [WK[0:BN, NB * D + i * SB * D:NB * D + (i + 1) * SB * D].rearrange("p (j d) -> p j d", j=SB) for i in range(2)]
        OO = [WK[0:BN, 2432 + i * 192:2624 + i * 192] for i in range(2)]
        SG = [WK[0:BN, 2816 + i * 96:2912 + i * 96] for i in range(2)]
        FP = [WK[0:BN, 3008 + i * 160:3168 + i * 160] for i in range(2)]
        hz = [WK[0:BN, 3328 + i * 320:3648 + i * 320] for i in range(2)]
        RW = [NP[0:96, 1856 + i * 96:1952 + i * 96] for i in range(4)]
        RWT = [NP[0:96, 2368 + i * 96:2464 + i * 96] for i in range(4)]
        RW3s, RW3v = NP[0:96, 2880:2944], NP[0:96, 2944:2976]

        def bank(i, n=512, p=128):
            return PS[0:p, i * 512:i * 512 + n]

        psW = [PS[:, i * 1024:(i + 1) * 1024].rearrange("p (t f) -> p t f", t=G) for i in range(2)]
        psH, psT = bank(4), bank(5)
        psTb = bank(5).bitcast(BF16)
        psA = [bank(6), bank(7)]
        psN = [bank(0), bank(1)]
        psO = [bank(i) for i in (2, 3, 0, 1)]
        psC = [bank(4), bank(5)]
        nT, nR = [bank(4), bank(5)], [bank(6), bank(7)]

        s_key, s_x, s_ld, s_w, s_ws, s_sh = (sem(n) for n in ("s_key", "s_x", "s_ld", "s_w", "s_ws", "s_sh"))
        s_g, s_gm = sem("s_g"), sem("s_gm")
        s_d, s_a, s_p = sem("s_d"), sem("s_a"), sem("s_p")
        s_zf = sem("s_zf")
        s_cn, s_cp, s_pos, s_bk = sem("s_cn"), sem("s_cp"), sem("s_pos"), sem("s_bk")
        s_sq, s_sqd, s_shd = sem("s_sq"), sem("s_sqd"), sem("s_shd")
        s_fl, s_gc, s_gi, s_gd, s_gq, s_rk = (sem(n) for n in ("s_fl", "s_gc", "s_gi", "s_gd", "s_gq", "s_rk"))
        s_nx, s_tb, s_free, s_tab = sem("s_nx"), sem("s_tb"), sem("s_free"), sem("s_tab")
        s_stg, s_prep = [sem("s_stg0"), sem("s_stg1")], sem("s_prep")
        s_ra, s_rb = [sem("s_ra0"), sem("s_ra1")], [sem("s_rb0"), sem("s_rb1")]
        s_bl, s_bs = ([sem(f"{n}{i}") for i in range(4)] for n in ("s_bl", "s_bs"))
        s_px = sem("s_px")
        s_ve, s_sd, s_st = sem("s_ve"), sem("s_sd"), sem("s_st")
        s_h, s_tp, s_ht, s_po, s_ev, s_xn = (sem(n) for n in ("s_h", "s_tp", "s_ht", "s_po", "s_ev", "s_xn"))
        s_hd = [[sem(f"s_hd{l}{i}") for i in range(2)] for l in range(4)]
        s_oo, s_xo, s_wz, s_wo, s_pa, s_ox, s_tl = (sem(n) for n in ("s_oo", "s_xo", "s_wz", "s_wo", "s_pa", "s_ox", "s_tl"))
        s_sk = [[sem(f"s_sk{l}{i}") for i in range(2)] for l in (2, 3)]
        s_o, s_sg, s_hz = sem("s_o"), sem("s_sg"), sem("s_hz")
        s_an, s_sn = sem("s_an"), sem("s_sn")
        s_az, s_le, s_out = sem("s_az"), sem("s_le"), sem("s_out")
        s_go, s_pe, s_sp = sem("s_go"), sem("s_pe"), sem("s_sp")
        s_rt, s_rc, s_rp = sem("s_rt"), sem("s_rc"), sem("s_rp")

        class Edge:
            def __init__(self, l):
                self.L = [sem(f"e{l}_L{i}") for i in range(4)]
                self.G = [sem(f"e{l}_G{i}") for i in range(2)]
                self.T, self.E, self.F1, self.S, self.F2, self.M, self.A, self.V, self.D, self.N, self.X = (
                    sem(f"e{l}_{n}") for n in ("T", "E", "F1", "S", "F2", "M", "A", "V", "D", "N", "X"))

        EG = [Edge(l) for l in range(4)]

        block = ctx.enter_context(nc.Block())
        NKEYS = 2
        loads = []

        def kron(l, a, col, W):
            t = KV[l][:, a, :] if l == 1 else KV[l][:, :]
            for c in range(3):
                loads.append((t[32 * c:32 * c + 32, col + 32 * c:col + 32 * c + 32], W))

        w = A
        loads += [(WS[0][:, 0:64], w["L0_gnn_W_l1_0"]), (WS[0][:, 64:128], w["L0_gnn_W_sc0"])]
        kron(0, 0, 0, w["L0_gnn_W_l1_1"])
        kron(0, 0, 96, w["L0_gnn_W_sc1"])
        for a, s in enumerate("ac"):
            loads += [(WS[1][64 * a:64 * a + 64, 0:64], w[f"L1_gnn_Ws_l1_{s}"]),
                      (WS[1][64 * a:64 * a + 64, 64:128], w[f"L1_gnn_Ws_sc_{s}"])]
            kron(1, a, 0, w[f"L1_gnn_Wv_l1_{s}"])
            kron(1, a, 96, w[f"L1_gnn_Wv_sc_{s}"])
            loads += [(RW[a], w[f"L1_gnn_Ws_l2_{s}"]), (RW[2 + a], w[f"L1_gnn_Wv_l2_{s}"])]
        loads += [(RW3s, w["L1_gnn_Ws_l3"]), (RW3v, w["L1_gnn_Wv_l3"])]
        loads += [(WS[2][:, 0:64], w["L2_gnn_W_nl0"]), (WS[2][:, 64:160], w["L2_gnn_W_skip0"])]
        kron(2, 0, 0, w["L2_gnn_W_nl1"])
        kron(2, 0, 96, w["L2_gnn_W_skip1"])
        loads += [(WS[3][:, 0:64], w["L3_gnn_lin1_w0"]), (WS[3][:, 64:128], w["L3_gnn_sc_w0"])]
        kron(3, 0, 0, w["L3_gnn_lin1_w1"])
        kron(3, 0, 96, w["L3_gnn_sc_w1"])
        for l, n in enumerate(("L0_gnn_W_fc", "L1_gnn_W_fc", "L2_gnn_W_fc", "L3_gnn_fc_w")):
            loads += [(F1[l][:, :], w[n + "1"]), (F2[l][:, :], w[n + "2"])]
        loads += [(OS[0], w["L0_gnn_W_l2_0"]), (OV[0], w["L0_gnn_W_l2_1"]),
                  (OS[2], w["L2_gnn_W_out_s"]), (OV[2], w["L2_gnn_W_out_v"]),
                  (OS[3], w["L3_gnn_lin2_w0"]), (OV[3], w["L3_gnn_lin2_w1"]),
                  (L3W[:, :], w["L3_gnn_lin3_w"])]

        places = []
        for l, p in enumerate(LAYERS):
            ns = 96 if l == 2 else 64
            for a in range(2 if l == 1 else 1):
                o_s = OS[l][:, a, :] if l == 1 else OS[l]
                o_v = OV[l][:, a, :] if l == 1 else OV[l]
                blocks = [(0, 96, a * 160, ns, o_s)]
                blocks += [(96 + c * p["vb"], p["vb"], a * 160 + ns + 32 * c, 32, o_v) for c in range(3)]
                for f0, m, col, nn, src in blocks:
                    for k in range(p["nch"]):
                        x0, x1 = max(f0, k * p["ch"]), min(f0 + m, (k + 1) * p["ch"])
                        if x0 < x1:
                            places.append((WO[l][x0 - k * p["ch"]:x1 - k * p["ch"], k, col:col + nn],
                                           src[x0 - f0:x1 - f0, :]))

        def ended(lo, t):
            j = t - 1 if lo == 2 else t
            return j // BLK if 0 <= j < NB and (j % BLK == BLK - 1 or j == NB - 1) else None

        for l in (0, 1, 3):
            nf = LAYERS[l]["kf"]
            for i, k in enumerate((0, 1, 2, 0, 1, 0)):
                places.append((FB[l][nf * i:nf * (i + 1), :], FP3[l][k]))

        def htile(l, j):
            return slice(j * BN, (j + 1) * BN)

        @block.sync
        def _(eng):
            eng.dma_start(keyA, A["keya"].rearrange("(p c) -> p c", p=128)).then_inc(s_key, 16)
            eng.dma_start(nxt, A["keyn"].rearrange("(p c) -> p c", p=128)).then_inc(s_nx, 16)
            eng.dma_start(keyB, A["keyb"].rearrange("(p c) -> p c", p=128)).then_inc(s_key, 16)
            eng.dma_start(X[:, :, :], A["x"].rearrange("(j p) d -> p j d", p=BN)).then_inc(s_x, 16)
            for t, n in ((Z1, "z1"), (Z2, "z2"), (Z3[:, :], "z3")):
                eng.dma_start(t, A[n]).then_inc(s_x, 16)
            eng.wait_ge(s_gm, 2)
            with nc.allow_non_contiguous_dma(reason="small strided weights"):
                for d, s in loads:
                    eng.dma_start(d, s).then_inc(s_w, 16)
                eng.dma_start(sh, A["e3"].rearrange("(p c) f -> p c f", p=128)).then_inc(s_sh, 16)
            eng.wait_ge(s_gm, 3)
            for T, R in ((TA, RA), (TB, RB)):
                eng.dma_start(T[EPAD:ROWS, :].rearrange("(p t) f -> p (t f)", p=128), zero[:, 0:G * R]).then_inc(s_zf, 16)
            eng.wait_ge(s_zf, 32)
            k = 0
            v = A["ea"].rearrange("(p c) f -> p (c f)", p=128)
            for c in range(0, EC, CHA):
                if k >= 2:
                    eng.wait_ge(s_free, k - 1)
                eng.dma_start(stage[k % 2][:, 0:CHA * RA], v[:, c * RA:(c + CHA) * RA]).then_inc(s_stg[k % 2], 16)
                k += 1
            eng.wait_ge(s_tb, 1)
            eng.dma_start(PB.rearrange("(p c) f -> p (c f)", p=128), ACC[:, 0:EC * (RB - 64)]).then_inc(s_px, 16)
            eng.wait_ge(s_px, 16)
            ev = A["eb"].rearrange("(p c) f -> p c f", p=128)
            pv = PB.rearrange("(p c) f -> p c f", p=128)

            def rows_b(t, c, m, sm):
                st = t[:, 0:m * RB].rearrange("p (c f) -> p c f", f=RB)
                eng.dma_start(st[:, :, 0:64], ev[:, c:c + m, :] if isinstance(c, int) else ev[:, bass.ds(c, m), :])\
                   .then_inc(sm, 16)
                eng.dma_start(st[:, :, 64:RB], pv[:, c:c + m, :] if isinstance(c, int) else pv[:, bass.ds(c, m), :])\
                   .then_inc(sm, 16)

            for c, m in BCH[0]:
                eng.wait_ge(s_free, k - 1)
                rows_b(stage[k % 2], c, m, s_stg[k % 2])
                k += 1

            eng.wait_ge(s_ws, 1)
            eng.wait_ge(s_wz, 5)
            for d, o in places:
                eng.dma_start(d, o).then_inc(s_wo, 16)

            def put(j):
                eng.wait_ge(s_xo, NB * 3 + j + 1)
                r = BN if j < NB - 1 else LAST
                eng.dma_start(out[j * BN:j * BN + r, :], X[0:r, j, :]).then_inc(s_out, 16)

            for l, p in enumerate(LAYERS):
                e, b = EG[l], 0 if p["t"] == "A" else 1
                R, T = (RA, TA) if b == 0 else (RB, TB)
                eng.wait_ge(s_tab, 1 if b == 0 else 2)
                eng.wait_ge(s_tb, 1)
                if l == 0:
                    eng.wait_ge(s_free, k)
                if l:
                    eng.wait_ge(s_le, l)
                eng.wait_ge(s_bk, NKEYS)
                n = eng.value_load(NI[b][0:1, 0:1], min_val=NT0 + 1, max_val=NG // 4 - 1)

                def load(i, u):
                    eng.wait_ge(e.M, i * 4 + (u + 1))
                    eng.wait_ge(e.N, i * 4 + (u + 1))
                    r = eng.value_load(TI[b][32:33, bass.ds(i * 4 + (u + 1), 1)], min_val=0, max_val=EPAD)
                    eng.dma_start(TT[u][:, 0:G * R], T[bass.ds(r, GE), :].rearrange("(p t) f -> p (t f)", t=G))\
                       .then_inc(e.L[u], 16)

                if l < 2:
                    def slot(i, u):
                        if not isinstance(i, int) or l:
                            eng.wait_ge(s_bs[u], i * (16 * SBU[u]) + 16 * SBU[u] * NT0 * l)
                            eng.sem_inc(s_sp, 1)
                        rows_b(SL[u], i * sum(SBU) + (BL0[l] + sum(SBU[:u])), SBU[u], s_bl[u])

                    for u in range(4):
                        load(0, u)
                    eng.wait_ge(s_xn, NB * (l + 1))
                    for i in range(2):
                        eng.wait_ge(s_hd[l][i], 16 * (NB - NB // 2 if i == 0 else NB // 2))
                    for u in (0, 2):
                        slot(0, u)
                    with eng.Fori(1, NT0) as i:
                        for u in range(4):
                            load(i, u)
                            if SBU[u]:
                                slot(i, u)
                with eng.Fori(NT0 if l < 2 else 0, n + 1) as i:
                    for u in range(4):
                        load(i, u)
                for u in range(4):
                    eng.wait_ge(e.L[u], n * 16 + 16)
                eng.sem_inc(s_sp, 1)
                if l < 2:
                    eng.wait_ge(s_le, l + 1)
                    for c, m in BCH[l + 1]:
                        eng.wait_ge(s_free, k - 1)
                        rows_b(stageM[k % 2], c, m, s_stg[k % 2])
                        k += 1
                if l == 2:
                    for j in range(NB):
                        eng.wait_ge(s_o if j >= 2 else s_le, j - 1 if j >= 2 else l + 1)
                        eng.dma_start(SK[j % 2], SC[htile(l, j), :]).then_inc(s_sk[0][j % 2], 16)
                if l == 3:
                    eng.sem_inc(s_tl, 1)
                    eng.wait_ge(s_le, 4)
                    for k in range(-(-NB // SB)):
                        if k >= 2:
                            for j in range((k - 2) * SB, (k - 1) * SB):
                                put(j)
                        m = min(SB, NB - k * SB)
                        eng.dma_start(SK3[k % 2][:, 0:m, :],
                                      SC[k * SB * BN:(k * SB + m) * BN, 0:160].rearrange("(j p) d -> p j d", p=BN))\
                           .then_inc(s_sk[1][k % 2], 16)
            for j in range((-(-NB // SB) - 2) * SB, NB):
                put(j)
            eng.wait_ge(s_out, 16 * NB)

        @block.gpsimd
        def _(eng):
            for l in range(4):
                eng.memset(KV[l][:, :, :] if l == 1 else KV[l][:, :], 0.0).then_inc(s_g, 1)
            eng.memset(RSC[0:64, 0:1], 1.0).then_inc(s_g, 1)
            eng.memset(RSC[0:96, 1:2], 1.0).then_inc(s_g, 1)
            eng.wait_ge(s_g, 6)
            eng.memset(RSC[64:128, 0:1], 1.0 / R3).then_inc(s_g, 1)
            eng.wait_ge(s_g, 7)
            eng.memset(RSC[96:128, 1:2], float(1 / np.sqrt(2.0))).then_inc(s_g, 1)
            eng.wait_ge(s_g, 8)
            eng.memset(ident[:, :], 0.0).then_inc(s_g, 1)
            eng.memset(LT, 1.0).then_inc(s_g, 1)
            eng.wait_ge(s_g, 10)
            eng.affine_select(out=ident[:, :], in_=ident[:, :], compare_op=ALU.not_equal, fill=1.0, base=0,
                              pattern=[[-1, 128]], channel_multiplier=1).then_inc(s_gm, 1)
            eng.affine_select(out=LT, in_=LT, compare_op=ALU.is_gt, fill=0.0, base=0,
                              pattern=[[1, 128]], channel_multiplier=-1).then_inc(s_gm, 1)
            eng.memset(zero, 0.0).then_inc(s_gm, 1)
            eng.memset(ONE, 1.0).then_inc(s_g, 1)
            for t in WO:
                eng.memset(t[:, :, :], 0.0).then_inc(s_wz, 1)
            eng.memset(ZERO[:, :], 0.0).then_inc(s_wz, 1)
            eng.iota(iota1[:, :], [[1, BN]], base=1, channel_multiplier=0,
                     allow_small_or_imprecise_dtypes=True).then_inc(s_g, 1)
            eng.iota(GI[:, :], [[1, 256]], base=-1, channel_multiplier=0,
                     allow_small_or_imprecise_dtypes=True).then_inc(s_gm, 1)

            k = 0

            def fill(st, sl):
                eng.tensor_copy(st[:, :, SRCC:SRCC + 1].bitcast(I32), keyB[:, sl].unsqueeze(2)).then_inc(s_prep, 1)
                eng.tensor_scalar(st[:, :, LOCC:LOCC + 1], keyA[:, sl].unsqueeze(2), 1.0, None, ALU.add).then_inc(s_prep, 1)

            def place(T, ps, st, sm):
                for q in range(st.shape[1]):
                    eng.indirect_dma_start(out=T[:, :], out_offset=bass.IndirectOffsetOnAxis(ap=ps(q), axis=0),
                                           in_=st[:, q, :], in_offset=None).then_inc(sm, 16)

            eng.wait_ge(s_key, 32)
            eng.wait_ge(s_fl, 1)
            flag = eng.value_load(FLG[0:1, 0:1], min_val=0, max_val=EPAD)
            TAv = TA[0:EPAD, :].rearrange("(p c) f -> p (c f)", p=128)
            for case in range(2):
                with eng.If_eq(flag.val, 0) if case == 0 else eng.If_ne(flag.val, 0):
                    if case == 1:
                        eng.wait_ge(s_pos, 1)
                    for k in range(NCHA):
                        eng.wait_ge(s_stg[k % 2], 16 * (k // 2 + 1))
                        st = stage[k % 2][:, 0:CHA * RA].rearrange("p (c f) -> p c f", f=RA)
                        fill(st, slice(k * CHA, (k + 1) * CHA))
                        eng.wait_ge(s_prep, 2 * (k + 1))
                        if case == 0:
                            eng.dma_start(TAv[:, k * CHA * RA:(k + 1) * CHA * RA], stage[k % 2][:, 0:CHA * RA])\
                               .then_inc(s_ra[k % 2], 16)
                        else:
                            place(TA, lambda q: posA[:, k * CHA + q:k * CHA + q + 1], st, s_ra[k % 2])
                        if k >= 1:
                            eng.wait_ge(s_ra[(k - 1) % 2], 16 * ((k - 1) // 2 + 1) * (1 if case == 0 else CHA))
                            eng.sem_inc(s_free, 1)
                    k = NCHA - 1
                    eng.wait_ge(s_ra[k % 2], 16 * (k // 2 + 1) * (1 if case == 0 else CHA))
                    eng.sem_inc(s_free, 1)
            eng.wait_ge(s_zf, 32)
            eng.sem_inc(s_tab, 1)
            k = NCHA
            cnt = [0, 0]
            stg_ = [16 * ((NCHA + 1) // 2), 16 * (NCHA // 2)]

            def move(cs, stg):
                nonlocal k
                for n, (c, m) in enumerate(cs):
                    stg_[k % 2] += 32
                    eng.wait_ge(s_stg[k % 2], stg_[k % 2])
                    st = stg[k % 2][:, 0:m * RB].rearrange("p (c f) -> p c f", f=RB)
                    place(TB, lambda q: st[:, q, POSC:POSC + 1].bitcast(I32), st, s_rb[k % 2])
                    cnt[k % 2] += 16 * m
                    if n >= 1:
                        eng.wait_ge(s_rb[(k - 1) % 2], cnt[(k - 1) % 2])
                        eng.sem_inc(s_free, 1)
                    k += 1
                eng.wait_ge(s_rb[(k - 1) % 2], cnt[(k - 1) % 2])
                eng.sem_inc(s_free, 1)

            move(BCH[0], stage)

            for l, p in enumerate(LAYERS):
                e, b = EG[l], 0 if p["t"] == "A" else 1
                R, vc = (RA, SRCC) if b == 0 else (RB, DSTC)
                if l == 0:
                    eng.wait_ge(s_bk, NKEYS)
                    eng.wait_ge(s_px, 16)
                    eng.memset(ACC[:, 0:NB * p["nch"] * BN], 0.0).then_inc(s_az, 1)
                elif l <= 2:
                    move(BCH[l], stageM)
                if l == 2:
                    for u in (0, 2):
                        eng.wait_ge(s_bs[u], 16 * SBU[u] * NT0 * 2)
                    eng.sem_inc(s_tab, 1)

                eng.wait_ge(s_bk, NKEYS)
                n = eng.value_load(NI[b][0:1, 0:1], min_val=NT0 + 1, max_val=NG // 4 - 1)
                m = 32 if l >= 2 else 16
                eng.wait_ge(s_hd[l][0], m * (NB - NB // 2))
                eng.wait_ge(s_hd[l][1], m * (NB // 2))

                def gather(i, u):
                    idx = TT[u][:, 0:G * R].rearrange("p (t f) -> p t f", t=G)
                    eng.wait_ge(e.L[u], i * 16 + 16)
                    eng.wait_ge(e.M, i * 4 + (u + 3))
                    eng.sem_inc(s_go, 1)
                    for t in range(G):
                        eng.indirect_dma_start(
                            out=GB[u % 2][:, t, :], out_offset=None, in_=HT[:, :],
                            in_offset=bass.IndirectOffsetOnAxis(ap=idx[:, t, vc:vc + 1].bitcast(I32), axis=0))\
                           .then_inc(e.G[u % 2], 16)

                def scatter(i, u):
                    r = SBU[u]
                    st = SL[u][:, 0:r * RB].rearrange("p (c f) -> p c f", f=RB)
                    eng.wait_ge(s_bl[u], i * 32 + (32 * NT0 * l + 32))
                    eng.sem_inc(s_go, 1)
                    place(TB, lambda q: st[:, q, POSC:POSC + 1].bitcast(I32), st, s_bs[u])

                if l < 2:
                    with eng.Fori(0, NT0) as i:
                        for u in range(4):
                            gather(i, u)
                            if SBU[u]:
                                scatter(i, u)
                with eng.Fori(NT0 if l < 2 else 0, n) as i:
                    for u in range(4):
                        gather(i, u)

        @block.tensor
        def _(eng):
            eng.wait_ge(s_gm, 2)
            eng.wait_ge(s_g, 11)
            eng.wait_ge(s_gm, 4)
            for b in range(NKEYS):
                eng.wait_ge(s_cn, b + 1)
                eng.matmul(psO[0][:, 0:NB], LT, CNT, start=True, stop=True)
                eng.matmul(psO[1][:, 0:NB], ONE, CNT, start=True, stop=True)
                if b == 0:
                    eng.matmul(psO[1][:, 72:73], ONE, CF, start=True, stop=True)
                eng.matmul(psO[1][0:NB, 64:65], CNT, ONE[:, 0:1], start=True, stop=True).then_inc(s_cp, 1)
                eng.wait_ge(s_gc, b + 1)
                eng.matmul(psC[1][0:NB, 0:1], LT[0:NB, 0:NB], GRP, start=True, stop=True)
                eng.matmul(psC[1][:, 1:2], ONE[0:NB, :], GRP, start=True, stop=True).then_inc(s_gi, 1)
                eng.wait_ge(s_gd, b + 1)
                eng.matmul(psC[0][:, 0:256], ONE[0:NB, :], CMP, start=True, stop=True)
                eng.matmul(psC[0][:, 256:512], DDB, CMP, start=True, stop=True).then_inc(s_gq, 1)
            eng.wait_ge(s_w, 16 * len(loads))
            for i in range(4):
                m = eng.transpose(psN[0][0:96, i * 96:(i + 1) * 96], RW[i], ident[0:96, 0:96])
            m.then_inc(s_rt, 1)
            eng.wait_ge(s_rc, 1)
            for a in range(2):
                eng.matmul(psN[1][0:96, a * 96:a * 96 + 64], RWT[a], RW3s, start=True, stop=True)
                m = eng.matmul(psN[1][0:96, a * 96 + 64:a * 96 + 96], RWT[2 + a], RW3v, start=True, stop=True)
            m.then_inc(s_rp, 1)

            def phase(lo, ln):
                def tnode(j):
                    base = ln * NB
                    if ln == 1:
                        eng.wait_ge(s_hz, j + 1)
                    else:
                        eng.wait_ge(s_h, base + j + 1)
                    if base + j >= 2:
                        eng.wait_ge(s_ht, base + j - 1)
                    o, i_ = nT[j % 2], ident[0:BN, 0:BN]
                    if ln == 1:
                        eng.transpose(o[:, 0:BN], hz[j % 2][:, 0:128], i_)
                        eng.transpose(o[0:96, 128:128 + BN], hz[j % 2][:, 128:224], i_)
                        m = eng.transpose(o[0:96, 256:256 + BN], hz[j % 2][:, 224:320], i_)
                    else:
                        eng.transpose(o[0:64, 0:BN], h[j % 4][:, 0:64], i_)
                        m = eng.transpose(o[0:96, 128:128 + BN], h[j % 4][:, 64:160], i_)
                    m.then_inc(s_tp, 1)

                def mnode(j):
                    base = ln * NB
                    eng.wait_ge(s_ht, base + j + 1)
                    if base + j >= 2:
                        eng.wait_ge(s_ev, base + j - 1)
                    o = nR[j % 2][0:BN, :]
                    t = hT[j % 2]
                    if ln == 2:
                        eng.matmul(o[:, 0:64], t[0:64, 0, 0:BN], WS[2][:, 0:64], start=True, stop=True)
                        eng.matmul(o[:, 160:256], t[0:64, 0, 0:BN], WS[2][:, 64:160], start=True, stop=True)
                        eng.matmul(o[:, 64:160], t[0:96, 1, 0:BN], KV[2][:, 0:96], start=True, stop=True)
                        m = eng.matmul(o[:, 256:352], t[0:96, 1, 0:BN], KV[2][:, 96:192], start=True, stop=True)
                    else:
                        v = o[:, 0:320].rearrange("p (a f) -> p a f", a=2)
                        r = 128 if ln == 1 else 64
                        eng.matmul(v[:, :, 0:64], t[0:r, 0, 0:BN], WS[ln][:, :], start=True, stop=True)
                        if ln == 1:
                            for a in range(2):
                                m = eng.matmul(v[:, :, 64:160], t[0:96, 1 + a, 0:BN], KV[1][:, a, :], start=(a == 0), stop=(a == 1))
                        else:
                            m = eng.matmul(v[:, :, 64:160], t[0:96, 1, 0:BN], KV[ln][:, :], start=True, stop=True)
                    m.then_inc(s_po, 1)

                ch, nch = (LAYERS[lo or 0][x] for x in ("ch", "nch"))
                acc = ACC[0:ch, 0:NB * nch * BN].rearrange("p (j k n) -> p j k n", j=NB, k=nch)

                def mout(j):
                    base = lo * NB
                    if j >= 4:
                        if lo == 2:
                            eng.wait_ge(s_o, j - 3)
                        elif lo == 3:
                            eng.wait_ge(s_ox, j - 3)
                        else:
                            eng.wait_ge(s_xo, base + j - 3)
                    nc_ = WO[lo].shape[2]
                    for k in range(nch):
                        m = eng.matmul(psO[j % 4][0:BN, 0:nc_], acc[:, j, k, :], WO[lo][:, k, :],
                                       start=(k == 0), stop=(k == nch - 1))
                    m.then_inc(s_oo, 1)

                if lo is not None:
                    eng.wait_ge(s_wo, 16 * len(places))
                if lo == 3:
                    for j in range(NB):
                        m = eng.matmul(nT[0][0:BN, j:j + 1], acc[0:96, j, 0, :], L3W[:, :], start=True, stop=True)
                    m.then_inc(s_pa, 1)
                for t in range(NB + (LAG if ln is not None else 0)):
                    n = t - LAG
                    if lo is not None:
                        if t < NB:
                            mout(t)
                    if ln is not None:
                        if 0 <= n + 1 < NB:
                            tnode(n + 1)
                        if n >= 0:
                            mnode(n)

            eng.wait_ge(s_ws, 1)
            eng.wait_ge(s_bk, NKEYS)
            phase(None, 0)
            for l, p in enumerate(LAYERS):
                kf_, hid, wn, ch, nch = (p[x] for x in ("kf", "hid", "wn", "ch", "nch"))
                nm = ch * nch
                base = l * NB
                e, b = EG[l], 0 if p["t"] == "A" else 1
                R = RA if b == 0 else RB
                eng.wait_ge(s_xn, base + NB)
                eng.wait_ge(s_ev, base + NB)
                eng.wait_ge(s_bk, NKEYS)
                n = eng.value_load(NI[b][0:1, 0:1], min_val=NT0 + 1, max_val=NG // 4 - 1)

                def edge_t(i, u, d):
                    u2, c = (u + d) % 4, (u + d) // 4
                    ef = TT[u2][:, 0:G * R].rearrange("p (t f) -> p t f", t=G)
                    eng.wait_ge(e.L[u2], i * 16 + (16 * c + 16))
                    if not (isinstance(i, int) and i * 4 + u + d == 0):
                        eng.wait_ge(e.E, i * 4 + (u + d))
                    if l != 2:
                        if d == 3:
                            eng.wait_ge(e.D, i * (4 * ND) + (u + 1) * ND)
                        else:
                            eng.wait_ge(e.X, 1)
                    eng.sem_inc(s_pe, 1)
                    for t in range(G):
                        if l != 2:
                            m = eng.transpose(psTb[0:6 * kf_, t * 128:(t + 1) * 128], XS[u2][:, t, 0:6 * kf_], identb[:, :])
                            continue
                        m = eng.transpose(psT[0:kf_, t * 128:(t + 1) * 128], ef[:, t, p["c0"]:p["c0"] + kf_], ident[:, :])
                    m.then_inc(e.T, 1)

                def edge_f1(i, u, d):
                    q = (u + d) % 2
                    eng.wait_ge(e.E, i * 4 + (u + d + 1))
                    if not (isinstance(i, int) and i * 4 + u + d == 0):
                        eng.wait_ge(e.S, i * 4 + (u + d))
                    eng.sem_inc(s_pe, 1)
                    if l != 2:
                        m = eng.matmul(psH[0:hid, :], FB[l][:, :], ET[q].bitcast(BF16)[0:6 * kf_, 0:GE], start=True, stop=True)
                    else:
                        m = eng.matmul(psH[0:hid, :], F1[l][:, :], ET[q][0:kf_, :], start=True, stop=True)
                    m.then_inc(e.F1, 1)

                def edge_f2(i, u, d):
                    q = (u + d) % 2
                    eng.wait_ge(e.S, i * 4 + (u + d + 1))
                    eng.wait_ge(e.M, i * 4 + (u + d + 3))
                    for t in range(G):
                        m = eng.matmul(psW[q][:, t, 0:wn], HH[q][0:hid, t * 128:(t + 1) * 128], F2[l][:, :],
                                       start=True, stop=True)
                    m.then_inc(e.F2, 1)

                def edge_a(i, u):
                    q = u % 2
                    ms = MS[q][:, 0:G * nm].rearrange("p (t f) -> p t f", t=G)
                    eng.wait_ge(e.M, i * 4 + (u + 5))
                    eng.wait_ge(e.N, i * 4 + (u + 5))
                    eng.wait_ge(e.V, i * 4 + (u + 1))
                    for k in range(nch):
                        for t in range(G):
                            m = eng.matmul(psA[q][0:ch, k * BN:(k + 1) * BN], ms[:, t, k * ch:(k + 1) * ch], OH[q][:, t, :],
                                           start=(t == 0), stop=(t == G - 1))
                    m.then_inc(e.A, 1)

                eng.wait_ge(s_wo, 16 * len(places))
                edge_t(0, 0, 0)
                edge_t(0, 0, 1)
                edge_t(0, 0, 2)
                edge_f1(0, 0, 0)
                edge_f1(0, 0, 1)
                edge_f2(0, 0, 0)
                eng.wait_ge(s_az, l + 1)
                eng.matmul(psA[1][0:ch, 0:nch * BN], ACC[0:1, 0:ch], ACC[0:1, 0:nch * BN], start=True, stop=True).then_inc(e.A, 1)
                with eng.Fori(0, n) as i:
                    for u in range(4):
                        edge_f2(i, u, 1)
                        edge_f1(i, u, 2)
                        edge_a(i, u)
                        edge_t(i, u, 3)
                eng.wait_ge(e.T, n * 4 + 3)
                eng.wait_ge(e.F1, n * 4 + 2)
                eng.wait_ge(e.F2, n * 4 + 1)
                eng.wait_ge(e.E, n * 4 + 2)
                eng.wait_ge(e.S, n * 4 + 2)
                eng.wait_ge(s_le, l + 1)

                phase(l, l + 1 if l < 3 else None)

        @block.scalar
        def _(eng):
            own = 0
            eng.wait_ge(s_sq, 1)
            eng.activation(bq, bq, ACT.Sqrt, scale=1.0 / 3.0).then_inc(s_sqd, 1)
            def phase(lo, ln):
                if ln is not None:
                    eng.sem_inc(EG[ln].N, 4)

                def root(k):
                    eng.wait_ge(s_ve, ln * NBK + k + 1)
                    sl = slice(k * BLK, min(NB, (k + 1) * BLK))
                    eng.activation(VE[:, sl], VE[:, sl], ACT.Sqrt).then_inc(s_sd, 1)

                def hid_(j):
                    base = ln * NB
                    eng.wait_ge(s_st, ln * NBK + j // BLK + 1)
                    if ln == 1 and j >= 4:
                        eng.wait_ge(s_hz, j - 3)
                    elif j >= 4:
                        eng.wait_ge(s_tp, base + j - 3)
                    elif ln:
                        eng.wait_ge(s_tp, base)
                        if ln == 2:
                            eng.wait_ge(s_hz, NB)
                    eng.activation(h[j % 4], X[:, j, :], ACT.Relu, bias=NM[:, j:j + 1], scale=RS[:, j:j + 1])\
                       .then_inc(s_h, 1)

                def evac(j):
                    base = ln * NB
                    eng.wait_ge(s_po, base + j + 1)
                    if j >= 2:
                        eng.wait_ge(s_hd[ln][j % 2], (32 if ln >= 2 else 16) * (j // 2))
                    if base + j >= 2:
                        eng.wait_ge(s_xn, base + j - 1)
                    w = 352 if ln == 2 else 320
                    eng.activation(EV[j % 2][:, 0:w], nR[j % 2][0:BN, 0:w], ACT.Copy,
                                   scale=Z1[:, j:j + 1] if ln in (0, 3) else 1.0).then_inc(s_ev, 1)

                def store(j):
                    eng.wait_ge(s_ev, ln * NB + j + 1)
                    eng.dma_start(HT[htile(ln, j), :], EV[j % 2][:, 0:160]).then_inc(s_hd[ln][j % 2], 16)
                    if ln >= 2:
                        k = 192 if ln == 2 else 160
                        eng.dma_start(SC[htile(ln, j), 0:k], EV[j % 2][:, 160:160 + k]).then_inc(s_hd[ln][j % 2], 16)

                def gate(j):
                    eng.wait_ge(s_o, j + 1)
                    if j >= 2:
                        eng.wait_ge(s_xo, 2 * NB + j - 1)
                    eng.activation(SG[j % 2], OO[j % 2][:, 0:96], ACT.Sigmoid).then_inc(s_sg, 1)

                def clear(j):
                    if j == 0:
                        eng.wait_ge(s_wz, 5)
                        if lo == 1:
                            a = NB * LAYERS[1]["nch"] * BN
                            eng.activation(ACC[:, a:], ZERO[:, :].to_broadcast([128, NB * BN]), ACT.Copy)
                    eng.wait_ge(s_oo, lo * NB + j + 1)
                    m = LAYERS[lo]["nch"] * BN
                    x = eng.activation(ACC[:, j * m:(j + 1) * m], ZERO[:, :].to_broadcast([128, m]), ACT.Copy)
                    if j == NB - 1:
                        x.then_inc(s_az, 1)

                def spare(j):
                    eng.wait_ge(s_oo, lo * NB + j + 1)
                    eng.activation(OUTB[:, j, :], psO[j % 4][0:BN, 0:160], ACT.Copy).then_inc(s_ox, 1)

                if lo == 3:
                    eng.wait_ge(s_tl, 1)
                for t in range(NB + (LAG + 1 if ln is not None else 0)):
                    n = t - LAG
                    if lo == 3:
                        spare(t)
                        if t == 11:
                            eng.wait_ge(s_an, 1)
                            eng.activation(SN[:, :], SN[:, :], ACT.Sin).then_inc(s_sn, 1)
                            eng.activation(CS[:, :], CS[:, :], ACT.Sin).then_inc(s_sn, 1)
                    if lo == 2 and 1 <= t <= NB:
                        gate(t - 1)
                    if lo is not None and lo < 3 and 2 <= t < NB + 2:
                        clear(t - 2)
                    if ln is not None:
                        k = ended(lo, t - 1)
                        if k is not None:
                            root(k)
                        if 0 <= n + 3 < NB:
                            hid_(n + 3)
                        if n >= 1:
                            evac(n - 1)
                        if n >= 2:
                            store(n - 2)
                if ln is not None:
                    store(NB - 1)

            phase(None, 0)
            for l, p in enumerate(LAYERS):
                kf_, hid, vb = p["kf"], p["hid"], p["vb"]
                base = l * NB
                e, b = EG[l], 0 if p["t"] == "A" else 1
                eng.wait_ge(s_bk, NKEYS)
                n = eng.value_load(NI[b][0:1, 0:1], min_val=NT0 + 1, max_val=NG // 4 - 1)

                def edge_e(i, u, d):
                    eng.wait_ge(e.T, i * 4 + (u + d + 1))
                    if not (isinstance(i, int) and i * 4 + u + d < 2):
                        eng.wait_ge(e.F1, i * 4 + (u + d - 1))
                    if l != 2:
                        m = eng.activation(ET[(u + d) % 2].bitcast(BF16)[0:6 * kf_, 0:GE], psTb[0:6 * kf_, 0:GE], ACT.Copy)
                    else:
                        m = eng.activation(ET[(u + d) % 2][0:kf_, :], psT[0:kf_, :], ACT.Copy)
                    m.then_inc(e.E, 1)

                def edge_s(i, u, d):
                    eng.wait_ge(e.F1, i * 4 + (u + d + 1))
                    if not (isinstance(i, int) and i * 4 + u + d < 2):
                        eng.wait_ge(e.F2, i * 4 + (u + d - 1))
                    eng.activation(HH[(u + d) % 2][0:hid, :], psH[0:hid, :], p["fn"], scale=p["scale"]).then_inc(e.S, 1)

                edge_e(0, 0, 0)
                edge_e(0, 0, 1)
                edge_s(0, 0, 0)
                edge_s(0, 0, 1)
                def edge_n(i, u):
                    q = u % 2
                    R, y1 = (RB, SHC) if l == 2 else (RA, YC + 1)
                    tb = TT[u][:, 0:G * R].rearrange("p (t f) -> p t f", t=G)
                    m4 = MS[q][:, 0:G * (96 + 3 * vb)].rearrange("p (t f) -> p t f", t=G)
                    eng.wait_ge(e.D, i * (4 * ND) + (u * ND + KT))
                    for t in range(G):
                        for c in range(3):
                            m = eng.activation(m4[:, t, 96 + vb * c:160 + vb * c], tt_[q][:, t, :], ACT.Copy,
                                               scale=tb[:, t, y1 + c:y1 + c + 1])
                    m.then_inc(e.N, 1)

                with eng.Fori(0, n) as i:
                    for u in range(4):
                        edge_n(i, u)
                        edge_e(i, u, 2)
                        edge_s(i, u, 2)
                eng.wait_ge(s_le, l + 1)

                phase(l, l + 1 if l < 3 else None)

        @block.vector
        def _(eng):
            own = 0

            def v(ins):
                nonlocal own
                own += 1
                ins.then_inc(s_d, 1)
                return own

            def w_(k=None):
                eng.wait_ge(s_d, own if k is None else k)

            eng.wait_ge(s_key, 32)
            eng.wait_ge(s_nx, 16)
            v(eng.memset(z16, 0.0))

            def rank(ps, b, sm):
                k = 0
                v_ = 0
                for q in range(NB):
                    t = (cum, kf)[q % 2]
                    eng.tensor_tensor_scan(t, masks[:, q, :], z16, OFF[:, q:q + 1], ALU.add, ALU.add).then_inc(sm, 1)
                    v_ += 1
                    eng.wait_ge(sm, v_)
                    eng.copy_predicated(pos, masks[:, q, :].bitcast(U16), t).then_inc(sm, 1)
                    v_ += 1
                eng.wait_ge(sm, v_)
                eng.tensor_copy(ps, pos).then_inc(s_pos, 1)

            for b, key in enumerate((keyA, keyB)):
                v(eng.tensor_scalar(kf, key, 1.0, None, ALU.add))
                w_()
                if b == 0:
                    v(eng.scalar_tensor_tensor(out=cum, in0=nxt, scalar=1.0, in1=kf, op0=ALU.add, op1=ALU.is_lt,
                                               accum_out=CF))
                v(eng.tensor_scalar(bq, kf, float(-(BN + 1) // 2), 1.0 / BN, ALU.add, ALU.mult))
                w_()
                v(eng.tensor_scalar(bq, bq, MAGIC, -MAGIC, ALU.add, ALU.add))
                w_()
                v(eng.tensor_copy(bb, bq))
                w_()
                for q in range(NB):
                    m = eng.tensor_scalar(masks[:, q, :], bb, float(q), None, ALU.is_equal, ALU.add,
                                          accum_out=CNT[:, q:q + 1])
                m.then_inc(s_cn, 1)
                v(eng.memset(pos, 0.0))
                eng.wait_ge(s_cn, b + 1)
                w_()
                eng.wait_ge(s_cp, b + 1)
                if b == 0:
                    eng.tensor_copy(FLG[:, :], psO[1][0:1, 72:73]).then_inc(s_fl, 1)
                v(eng.tensor_scalar(GRP, psO[1][0:NB, 64:65], GE / 2 - 0.5, 1.0 / GE, ALU.add, ALU.mult))
                w_()
                eng.tensor_scalar(GRP, GRP, MAGIC, -MAGIC, ALU.add, ALU.add).then_inc(s_gc, 1)
                v(eng.tensor_tensor_scan(INC, psO[1][:, 0:NB], pos[:, 0:NB], 0.0, ALU.add, ALU.add))
                w_()
                v(eng.tensor_tensor(OFF, INC, psO[1][:, 0:NB], ALU.subtract))
                w_()
                v(eng.scalar_tensor_tensor(out=OFF, in0=OFF, scalar=-1.0, in1=psO[0][:, 0:NB], op0=ALU.add, op1=ALU.add))
                eng.wait_ge(s_gm, 4)
                eng.wait_ge(s_gi, b + 1)
                v(eng.tensor_tensor(ICC, psC[1][0:NB, 0:1], GRP, ALU.add))
                v(eng.scalar_tensor_tensor(out=DD, in0=GRP, scalar=-float(GE), in1=psO[1][0:NB, 64:65], op0=ALU.mult,
                                           op1=ALU.add))
                v(eng.tensor_scalar(NGF, psC[1][0:1, 1:2], 1.5, 0.25, ALU.add, ALU.mult))
                w_()
                v(eng.tensor_scalar(CMP, GI[0:NB, :], ICC, None, ALU.is_ge))
                v(eng.tensor_copy(DDB, DD.to_broadcast([NB, 128])))
                v(eng.tensor_scalar(NIF[:, :], NGF, MAGIC, -MAGIC, ALU.add, ALU.add))
                w_()
                eng.tensor_scalar(NI[b][:, :], NIF[:, :], float(NT0 + 1), None, ALU.max).then_inc(s_gd, 1)
                eng.wait_ge(s_gd, b + 1)
                eng.wait_ge(s_gq, b + 1)
                v(eng.scalar_tensor_tensor(out=BASF, in0=GI, scalar=float(GE), in1=psC[0][:, 256:512], op0=ALU.mult,
                                           op1=ALU.add))
                v(eng.tensor_scalar(BKO[b][:, :], psC[0][:, 0:256], float(NB - 1), float(BN), ALU.min, ALU.mult))
                v(eng.tensor_scalar(TI[b][0:1, :], psC[0][0:1, 0:256], float(NB - 1), None, ALU.min))
                w_()
                eng.tensor_scalar(TI[b][32:33, :], BASF[32:33, :], 0.0, float(EPAD), ALU.max, ALU.min).then_inc(s_bk, 1)
                eng.wait_ge(s_bk, b + 1)
                if b == 0:
                    flag = eng.value_load(FLG[0:1, 0:1], min_val=0, max_val=EPAD)
                    with eng.If_ne(flag.val, 0):
                        rank(posA, 0, s_rk)
                        eng.wait_ge(s_pos, 1)
                    pass
                else:
                    for q in range(NB):
                        t = (cum, kf)[q % 2]
                        v(eng.tensor_tensor_scan(t, masks[:, q, :], z16, OFF[:, q:q + 1], ALU.add, ALU.add))
                        w_()
                        v(eng.copy_predicated(pos, masks[:, q, :].bitcast(U16), t))
                    w_()
                    v(eng.tensor_copy(PX[:, :, POSC - 64].bitcast(I32), pos))
                    w_()

            eng.wait_ge(s_sh, 16)
            v(eng.tensor_tensor(kf, sh[:, :, 0], sh[:, :, 0], ALU.mult))
            v(eng.tensor_tensor(cum, sh[:, :, 1], sh[:, :, 1], ALU.mult))
            v(eng.tensor_tensor(rec, sh[:, :, 2], sh[:, :, 2], ALU.mult))
            w_()
            v(eng.tensor_tensor(kf, kf, cum, ALU.add))
            w_()
            eng.tensor_tensor(bq, kf, rec, ALU.add).then_inc(s_sq, 1)
            eng.wait_ge(s_sqd, 1)
            v(eng.reciprocal(rec, bq))
            w_()
            v(eng.tensor_copy(PX[:, :, DSTC - 64].bitcast(I32), keyA))
            v(eng.tensor_scalar(PX[:, :, LOCB - 64], keyB, 1.0, None, ALU.add))
            v(eng.tensor_tensor(PX[:, :, 0:3], sh, rec.unsqueeze(2).to_broadcast([128, EC, 3]), ALU.mult))
            v(eng.tensor_tensor(PX[:, :, 3:5], sh[:, :, 0:2], rec.unsqueeze(2).to_broadcast([128, EC, 2]), ALU.mult))
            w_()
            eng.sem_inc(s_tb, 1)

            eng.wait_ge(s_w, 16 * len(loads))
            eng.wait_ge(s_g, 12)
            r32 = float(1 / np.sqrt(32.0))
            r96 = float(1 / np.sqrt(96.0))

            def mul(t, c):
                v(eng.tensor_scalar(t, t, float(c), None, ALU.mult))

            mul(WS[0][:, 0:64], 1 / 8)
            mul(WS[0][:, 64:128], C_S / 8)
            mul(KV[0][:, 0:96], r32)
            mul(KV[0][:, 96:192], C_S * r32)
            mul(WS[1][:, 64:128], C_S)
            mul(KV[1][:, :, 96:192], C_S)
            mul(WS[3][:, :], 1 / 8)
            mul(KV[3][:, :], r32)
            c = C_X * r96 / np.sqrt(8.0) / 10
            v(eng.tensor_scalar(OS[0], OS[0], RSC[0:96, 0:1], float(c), ALU.mult, ALU.mult))
            mul(OV[0], c)
            v(eng.tensor_scalar(OS[2], OS[2], RSC[0:96, 0:1], 1 / 32, ALU.mult, ALU.mult))
            v(eng.tensor_scalar(OV[2], OV[2], RSC[:, 1:2], 1 / 32, ALU.mult, ALU.mult))
            c = r96 / 4 / 8
            v(eng.tensor_scalar(OS[3], OS[3], RSC[0:96, 0:1], float(c), ALU.mult, ALU.mult))
            mul(OV[3], c)
            v(eng.tensor_scalar(L3W[:, :], L3W[:, :], RSC[0:96, 0:1], float(0.1 * c), ALU.mult, ALU.mult))
            eng.wait_ge(s_rt, 1)
            eng.tensor_copy(NP[0:96, 2368:2752], psN[0][0:96, 0:384]).then_inc(s_rc, 1)
            eng.wait_ge(s_rp, 1)
            for a in range(2):
                v(eng.tensor_scalar(OS[1][:, a, :], psN[1][0:96, a * 96:a * 96 + 64], RSC[0:96, 0:1], C_X / 4, ALU.mult, ALU.mult))
                v(eng.tensor_scalar(OV[1][:, a, :], psN[1][0:96, a * 96 + 64:a * 96 + 96], C_X / 4, None, ALU.mult))
            eng.wait_ge(s_x, 64)
            v(eng.tensor_tensor(SA[:, :], Z1, Z3[:, :], ALU.mult))
            v(eng.tensor_tensor(SCC[:, :], Z2, Z3[:, :], ALU.mult))
            v(eng.tensor_copy(identb[:, :], ident[:, :]))
            for l in (0, 1, 3):
                v(eng.tensor_copy(FP3[l][0], F1[l][:, :]))
            w_()
            for l in (0, 1, 3):
                v(eng.tensor_tensor(FR[l], F1[l][:, :], FP3[l][0], ALU.subtract))
            w_()
            for l in (0, 1, 3):
                v(eng.tensor_copy(FP3[l][1], FR[l]))
            w_()
            for l in (0, 1, 3):
                v(eng.tensor_tensor(FP3[l][2], FR[l], FP3[l][1], ALU.subtract))
            w_()
            eng.sem_inc(s_ws, 1)

            def phase(lo, ln):
                if ln is not None:
                    eng.sem_inc(EG[ln].M, 4)
                    eng.sem_inc(EG[ln].V, 1)
                    eng.sem_inc(EG[ln].A, 1)

                def stats(k):
                    js = range(k * BLK, min(NB, (k + 1) * BLK))
                    sl = slice(js[0], js[-1] + 1)
                    if lo is not None:
                        eng.wait_ge(s_xo, lo * NB + js[-1] + 1)
                    for j in js:
                        v(eng.bn_stats(STT[:, j, :], X[:, j, :]))
                    w_()
                    for j in js:
                        v(eng.bn_aggr(MV[:, j, :], STT[:, j, :]))
                    w_()
                    eng.tensor_scalar(VE[:, sl], MV[:, sl, 1], 1e-5, None, ALU.add).then_inc(s_ve, 1)

                def norm(k):
                    sl = slice(k * BLK, min(NB, (k + 1) * BLK))
                    eng.wait_ge(s_sd, ln * NBK + k + 1)
                    v(eng.reciprocal(RS[:, sl], VE[:, sl]))
                    w_()
                    eng.scalar_tensor_tensor(out=NM[:, sl], in0=MV[:, sl, 0], scalar=-1.0, in1=RS[:, sl],
                                             op0=ALU.mult, op1=ALU.mult).then_inc(s_st, 1)

                def hscale(j):
                    eng.wait_ge(s_h, NB + j + 1)
                    if j >= 2:
                        eng.wait_ge(s_tp, NB + j - 1)
                    for c0, m in ((0, 64), (64, 96)):
                        o = hz[j % 2][:, 2 * c0:2 * c0 + 2 * m].rearrange("p (a f) -> p a f", a=2)
                        x = eng.tensor_tensor(o, h[j % 4][:, c0:c0 + m].unsqueeze(1).to_broadcast([BN, 2, m]),
                                              ZZ[:, :, j:j + 1].to_broadcast([BN, 2, m]), ALU.mult)
                    x.then_inc(s_hz, 1)

                def hcopy(j):
                    base = ln * NB
                    eng.wait_ge(s_tp, base + j + 1)
                    if base + j >= 2:
                        eng.wait_ge(s_po, base + j - 1)
                    t, o = hT[j % 2], nT[j % 2].rearrange("p (a n) -> p a n", a=4)
                    r, a = (128, 3) if ln == 1 else (64, 2)
                    eng.tensor_copy(t[0:r, 0, 0:BN], o[0:r, 0, 0:BN])
                    eng.tensor_copy(t[0:96, 1:a, 0:BN], o[0:96, 1:a, 0:BN]).then_inc(s_ht, 1)

                def xnode(j):
                    eng.wait_ge(s_ev, ln * NB + j + 1)
                    if ln < 2:
                        eng.tensor_tensor(X[:, j, :], X[:, j, :], EV[j % 2][:, 160:320], ALU.add).then_inc(s_xn, 1)
                    else:
                        eng.sem_inc(s_xn, 1)

                if lo == 3:
                    eng.wait_ge(s_pa, 1)
                    v(eng.tensor_tensor(ANG[:, :], nT[0][0:BN, 0:NB], Z1, ALU.mult))
                    w_()
                    for T, ph in ((SN, 0.0), (CS, 0.25)):
                        v(eng.tensor_scalar(KK[:, :], ANG[:, :], float(1 / (2 * np.pi)), ph, ALU.mult, ALU.add))
                        w_()
                        v(eng.tensor_scalar(KK[:, :], KK[:, :], MAGIC, -MAGIC, ALU.add, ALU.add))
                        w_()
                        v(eng.scalar_tensor_tensor(out=T[:, :], in0=KK[:, :], scalar=-6.28125, in1=ANG[:, :],
                                                   op0=ALU.mult, op1=ALU.add))
                        w_()
                        v(eng.scalar_tensor_tensor(out=T[:, :], in0=KK[:, :], scalar=-float(2 * np.pi - 6.28125),
                                                   in1=T[:, :], op0=ALU.mult, op1=ALU.add))
                        w_()
                        if ph:
                            v(eng.tensor_scalar(T[:, :], T[:, :], float(np.pi / 2), None, ALU.add))
                            w_()
                        v(eng.tensor_scalar(T[:, :], T[:, :], float(np.float32(np.pi)) * (1 - 1e-7),
                                            -float(np.float32(np.pi)) * (1 - 1e-7), ALU.min, ALU.max))
                        w_()
                    eng.sem_inc(s_an, 1)
                    eng.wait_ge(s_sn, 2)
                    v(eng.tensor_tensor(SN[:, :], SN[:, :], Z1, ALU.mult))
                    w_()

                def fin2(j):
                    eng.wait_ge(s_sg, j + 1)
                    o, s, f = OO[j % 2], SG[j % 2], FP[j % 2]
                    v(eng.tensor_tensor(f[:, 0:64], o[:, 0:64], s[:, 0:64], ALU.mult))
                    v(eng.tensor_tensor(f[:, 64:160].rearrange("p (c w) -> p c w", c=3),
                                        o[:, 96:192].rearrange("p (c w) -> p c w", c=3),
                                        s[:, 64:96].unsqueeze(1).to_broadcast([BN, 3, 32]), ALU.mult))
                    w_()
                    eng.tensor_tensor(X[:, j, :], X[:, j, :], f, ALU.add).then_inc(s_xo, 1)

                def xout(j):
                    base = lo * NB
                    if lo < 3:
                        eng.wait_ge(s_oo, base + j + 1)
                    o = psO[j % 4][0:BN, :]
                    if lo == 0:
                        eng.scalar_tensor_tensor(out=X[:, j, :], in0=o[:, 0:160], scalar=Z1[:, j:j + 1], in1=X[:, j, :],
                                                 op0=ALU.mult, op1=ALU.add).then_inc(s_xo, 1)
                    elif lo == 1:
                        v(eng.scalar_tensor_tensor(out=X[:, j, :], in0=o[:, 0:160], scalar=SA[:, j:j + 1], in1=X[:, j, :],
                                                   op0=ALU.mult, op1=ALU.add))
                        w_()
                        eng.scalar_tensor_tensor(out=X[:, j, :], in0=o[:, 160:320], scalar=SCC[:, j:j + 1], in1=X[:, j, :],
                                                 op0=ALU.mult, op1=ALU.add).then_inc(s_xo, 1)
                    elif lo == 2:
                        eng.wait_ge(s_sk[0][j % 2], 16 * (j // 2 + 1))
                        if j >= 2:
                            eng.wait_ge(s_xo, base + j - 1)
                        eng.tensor_tensor(OO[j % 2], o[:, 0:192], SK[j % 2], ALU.add).then_inc(s_o, 1)
                    else:
                        k = j // SB
                        eng.wait_ge(s_sk[1][k % 2], 16 * (k // 2 + 1))
                        eng.wait_ge(s_ox, j + 1)
                        v(eng.scalar_tensor_tensor(out=X[:, j, :], in0=SK3[k % 2][:, j % SB, :], scalar=CS[:, j:j + 1],
                                                   in1=X[:, j, :], op0=ALU.mult, op1=ALU.add))
                        w_()
                        eng.scalar_tensor_tensor(out=X[:, j, :], in0=OUTB[:, j, :], scalar=SN[:, j:j + 1], in1=X[:, j, :],
                                                 op0=ALU.mult, op1=ALU.add).then_inc(s_xo, 1)

                for t in range(NB + (LAG + 1 if ln is not None else 0)):
                    n = t - LAG
                    if lo is not None and t < NB:
                        xout(t)
                    if lo == 2 and 1 <= t <= NB:
                        fin2(t - 1)
                    if ln is not None:
                        if ln == 1 and 0 <= n + 2 < NB:
                            hscale(n + 2)
                        if 0 <= n + 1 < NB:
                            hcopy(n + 1)
                        if n >= 1:
                            xnode(n - 1)
                        k = ended(lo, t)
                        if k is not None:
                            stats(k)
                        k = ended(lo, t - 2)
                        if k is not None:
                            norm(k)
                if lo == 2 and ln is None:
                    fin2(NB - 1)
                if lo is not None:
                    eng.wait_ge(s_xo, (lo + 1) * NB)

            phase(None, 0)
            for l, p in enumerate(LAYERS):
                vb = p["vb"]
                nm = 96 + 3 * vb
                base = l * NB
                e, b = EG[l], 0 if p["t"] == "A" else 1
                R = RA if b == 0 else RB
                yc, lc = (YC, LOCC) if b == 0 else (SHC, LOCB)
                eng.wait_ge(s_az, l + 1)
                eng.wait_ge(s_bk, NKEYS)
                n = eng.value_load(NI[b][0:1, 0:1], min_val=NT0 + 1, max_val=NG // 4 - 1)
                ch, na = p["ch"], p["nch"] * BN
                acc = ACC[0:ch, 0:NB * na].rearrange("p (j f) -> p j f", j=NB)

                def parts(u):
                    c0, kf = p["c0"], p["kf"]
                    ef = TT[u][:, 0:G * RA].rearrange("p (t f) -> p t f", t=G)[:, :, c0:c0 + kf]
                    x, xr = XS[u], XR[:, :, 0:kf]
                    hh = x[:, :, 0:3 * kf].rearrange("p t (a f) -> p t a f", a=3)
                    mm = x[:, :, 3 * kf:5 * kf].rearrange("p t (a f) -> p t a f", a=2)
                    return (lambda: eng.tensor_copy(hh, ef.unsqueeze(2).to_broadcast([128, G, 3, kf])),
                            lambda: eng.tensor_tensor(xr, ef, x[:, :, 0:kf], ALU.subtract),
                            (lambda: eng.tensor_copy(mm, xr.unsqueeze(2).to_broadcast([128, G, 2, kf])),
                             lambda: eng.tensor_tensor(x[:, :, 5 * kf:6 * kf], xr, x[:, :, 3 * kf:4 * kf], ALU.subtract)))

                if l != 2:
                    eng.wait_ge(s_xn, NB * (l + 1))
                    m = 32 if l >= 2 else 16
                    eng.wait_ge(s_hd[l][0], m * (NB - NB // 2))
                    eng.wait_ge(s_hd[l][1], m * (NB // 2))
                    for u in range(3):
                        eng.wait_ge(e.L[u], 16)
                        x0, x1, x2 = parts(u)
                        for x in (x0, x1) + x2:
                            v(x())
                            w_()
                    eng.sem_inc(e.X, 1)

                def bucket(i, u):
                    return eng.value_load(TI[b][0:1, bass.ds(i * 4 + u, 1)], min_val=0, max_val=NB - 1)

                def add(i, u, q, j):
                    eng.wait_ge(e.A, i * 4 + (u + 2))
                    eng.tensor_tensor(acc[:, bass.ds(j, 1), :], acc[:, bass.ds(j, 1), :],
                                      psA[q][0:ch, 0:na].unsqueeze(1), ALU.add).then_inc(e.V, 1)

                with eng.Fori(0, n) as i:
                    for u in range(4):
                        q = u % 2
                        tb = TT[u][:, 0:G * R].rearrange("p (t f) -> p t f", t=G)
                        m4 = MS[q][:, 0:G * nm].rearrange("p (t f) -> p t f", t=G)
                        mv = m4[:, :, 96:nm].rearrange("p t (c f) -> p t c f", c=3)
                        e0 = GB[q][:, :, 0:64]
                        e1 = GB[q][:, :, 64:160].rearrange("p t (c f) -> p t c f", c=3)
                        W = psW[q]
                        done = 0

                        def op(ins):
                            nonlocal done
                            ins.then_inc(e.D, 1)
                            done += 1
                            return done

                        def need(k):
                            eng.wait_ge(e.D, i * (4 * ND) + (u * ND + k))

                        y1 = tb[:, :, yc + 1:yc + 4] if l != 2 else tb[:, :, yc:yc + 3]
                        y1b = y1.unsqueeze(3)
                        eng.wait_ge(e.L[u], i * 16 + 16)
                        eng.wait_ge(e.A, i * 4 + (u + 1))
                        op(eng.scalar_tensor_tensor(out=OH[q], in0=iota1[:, :].unsqueeze(1).to_broadcast([128, G, BN]),
                                                    scalar=BKO[b][:, bass.ds(i * 4 + (u + 1), 1)],
                                                    in1=tb[:, :, lc:lc + 1].to_broadcast([128, G, BN]),
                                                    op0=ALU.add, op1=ALU.is_equal))
                        eng.wait_ge(e.G[q], i * 128 + (u // 2 * 64 + 64))
                        if l != 2:
                            y0 = tb[:, :, yc:yc + 1]
                            u3 = (u + 3) % 4
                            x0, x1, x2 = parts(u3)
                            need(1)
                            kp = op(eng.tensor_tensor(tp[q], e1, y1b.to_broadcast([128, G, 3, 32]), ALU.mult))
                            eng.wait_ge(e.F2, i * 4 + (u + 1))
                            eng.wait_ge(e.N, i * 4 + (u + 4))
                            kt = op(eng.tensor_tensor(tt_[q], W[:, :, 64:128], e0, ALU.mult))
                            assert kt == KT
                            ky = op(eng.tensor_tensor(ty[q], e0, y0.to_broadcast([128, G, 64]), ALU.mult))
                            ku = op(eng.tensor_tensor(tu[q], W[:, :, 128:160], y0.to_broadcast([128, G, 32]), ALU.mult))
                            j = bucket(i, u)
                            need(kp)
                            kq = op(eng.tensor_tensor(tq[q], tp[q][:, :, 0, :], tp[q][:, :, 1, :], ALU.add))
                            need(ky)
                            op(eng.tensor_tensor(m4[:, :, 0:64], W[:, :, 0:64], ty[q], ALU.mult))
                            need(kq)
                            kr = op(eng.tensor_tensor(tq[q], tq[q], tp[q][:, :, 2, :], ALU.add))
                            eng.wait_ge(e.L[u3], i * 16 + (16 * ((u + 3) // 4) + 16))
                            eng.wait_ge(e.T, i * 4 + (u + 1))
                            k0 = op(x0())
                            need(kr)
                            op(eng.tensor_tensor(m4[:, :, 64:96], W[:, :, 160:192], tq[q], ALU.mult))
                            need(k0)
                            k1 = op(x1())
                            eng.tensor_tensor(mv[:, :, :, 64:96], tu[q].unsqueeze(2).to_broadcast([128, G, 3, 32]),
                                              e1, ALU.mult).then_inc(e.M, 1)
                            need(k1)
                            k2 = op(x2[0]())
                            need(k2)
                            op(x2[1]())
                        else:
                            need(1)
                            kp = op(eng.tensor_tensor(tp[q], e1, y1b.to_broadcast([128, G, 3, 32]), ALU.mult))
                            eng.wait_ge(e.F2, i * 4 + (u + 1))
                            eng.wait_ge(e.N, i * 4 + (u + 4))
                            kt = op(eng.tensor_tensor(tt_[q], W[:, :, 64:128], e0, ALU.mult))
                            assert kt == KT
                            kw = op(eng.tensor_tensor(tw[:, :, 0:3, :], e1,
                                                      W[:, :, 192:224].unsqueeze(2).to_broadcast([128, G, 3, 32]), ALU.mult))
                            op(eng.tensor_tensor(m4[:, :, 0:64], W[:, :, 0:64], e0, ALU.mult))
                            j = bucket(i, u)
                            need(kp)
                            kq = op(eng.tensor_tensor(tq[q], tp[q][:, :, 0, :], tp[q][:, :, 1, :], ALU.add))
                            need(kw)
                            kx = op(eng.tensor_copy(tw[:, :, 3:5, :], tw[:, :, 0:2, :]))
                            need(kq)
                            kr = op(eng.tensor_tensor(tq[q], tq[q], tp[q][:, :, 2, :], ALU.add))
                            need(kx)
                            k1 = op(eng.tensor_tensor(mv[:, :, :, 96:128], tw[:, :, 1:4, :],
                                                      tb[:, :, yc + 2:yc + 5].unsqueeze(3).to_broadcast([128, G, 3, 32]),
                                                      ALU.mult))
                            k2 = op(eng.tensor_tensor(tx, tw[:, :, 2:5, :],
                                                      tb[:, :, yc + 1:yc + 4].unsqueeze(3).to_broadcast([128, G, 3, 32]),
                                                      ALU.mult))
                            need(kr)
                            op(eng.tensor_tensor(m4[:, :, 64:96], W[:, :, 160:192], tq[q], ALU.mult))
                            op(eng.tensor_tensor(mv[:, :, :, 64:96], e1,
                                                 W[:, :, 128:160].unsqueeze(2).to_broadcast([128, G, 3, 32]), ALU.mult))
                            need(k2)
                            op(eng.tensor_tensor(mv[:, :, :, 96:128], mv[:, :, :, 96:128], tx, ALU.subtract))
                            need(done)
                            eng.sem_inc(e.M, 1)
                        assert done == ND, done
                        add(i, u, 1 - q, j)
                j = eng.value_load(TI[b][0:1, bass.ds(n * 4, 1)], min_val=0, max_val=NB - 1)
                eng.wait_ge(e.A, n * 4 + 2)
                eng.wait_ge(e.V, n * 4 + 1)
                eng.wait_ge(e.F1, n * 4 + 2)
                eng.wait_ge(e.F2, n * 4 + 1)
                eng.wait_ge(e.T, n * 4 + 3)
                if l < 2:
                    for u in (0, 2):
                        eng.wait_ge(s_bs[u], 16 * SBU[u] * NT0 * (l + 1))
                eng.tensor_tensor(acc[:, bass.ds(j, 1), :], acc[:, bass.ds(j, 1), :],
                                  psA[1][0:ch, 0:na].unsqueeze(1), ALU.add).then_inc(s_le, 1)
                eng.wait_ge(s_le, l + 1)

                phase(l, l + 1 if l < 3 else None)


def kernel(**inputs):
    import numpy as _np
    import concourse.bacc as _bacc
    from concourse import mybir as _mybir
    from concourse.bass_utils import run_bass_kernel_spmd as _run

    a = {k: _np.ascontiguousarray(v) for k, v in inputs.items()}

    def rows(t, n):
        return _np.concatenate([t, _np.zeros((n - t.shape[0],) + t.shape[1:], t.dtype)])

    def key(t):
        return _np.concatenate([t, _np.full((EPAD - E,), NOKEY, t.dtype)])

    host = dict(a)
    order = _np.concatenate([_np.arange(64), 64 + _np.arange(96).reshape(32, 3).T.ravel()])
    host["x"] = rows(a["x"][:, order], NPAD)
    host["keya"], host["keyb"] = key(a["dst"]), key(a["src"])
    host["keyn"] = _np.concatenate([host["keya"][1:], host["keya"][-1:]])
    ea = _np.concatenate([a["edge_attr_12"], a["edge_attr_10"], a["edge_attr_8"], a["edge_attr_4"],
                          _np.zeros((E, 2), a["x"].dtype)], axis=1)
    host["ea"] = rows(ea, EPAD)
    host["eb"] = rows(a["edge_attr_64"], EPAD)
    host["e3"] = _np.concatenate([a["edge_attr_3"], _np.ones((EPAD - E, 3), a["x"].dtype)])
    for n, s in (("z1", "node_vec1"), ("z2", "node_vec1_n2"), ("z3", "node_vec1_n3")):
        host[n] = _np.ascontiguousarray(rows(a[s], NPAD).reshape(NB, BN).T)
    nc = _bacc.Bacc("TRN2", target_bir_lowering=False, num_devices=1)
    arrays, args = {}, {}
    for name in _INS:
        t = host[name]
        arrays[f"in_{name}"] = t
        args[name] = nc.dram_tensor(f"in_{name}", t.shape, _mybir.dt.from_np(t.dtype), kind="ExternalInput").ap()
    o = nc.dram_tensor("out_0", (N, D), _mybir.dt.float32, kind="ExternalOutput").ap()
    program(nc, args, o)
    r = _run(nc, [arrays], core_ids=[0])
    res = _np.empty_like(r.results[0]["out_0"])
    res[:, order] = r.results[0]["out_0"]
    return res
```
